# Optimizing a Trainium2 kernel written in Bass

```python
import numpy as np
import jax
import jax.numpy as jnp

def _softmax(x, axis=-1):
    return jax.nn.softmax(x, axis=axis)

def _gelu(x):
    return jax.nn.gelu(x, approximate=True)

def _silu(x):
    return jax.nn.silu(x)

def _sigmoid(x):
    return jax.nn.sigmoid(x)

def _layernorm(x, axis=-1, eps=1e-05):
    m = jnp.mean(x, axis=axis, keepdims=True)
    v = jnp.var(x, axis=axis, keepdims=True)
    return (x - m) / jnp.sqrt(v + eps)

def _scatter_add(tgt, idx, src, axis=0):
    return tgt.at[idx].add(src)

def _segment_sum(src, seg, n):
    return jax.ops.segment_sum(src, seg, n)
kernel_name = 'mk_macaron_d2_jaxref_r4_1cadca'

def setup_inputs(seed: int=0):
    np.random.seed(seed)
    _w = jnp.asarray

    def _L0_attn_setup():
        import jax, jax.numpy as jnp
        import numpy as np
        B, T, C = (2, 512, 256)
        NH = 16
        HS = C // NH
        BD = max(HS // 4, 16)
        HORIZON = 32

        def _windows(t, delta):
            padded = jnp.pad(t, ((0, 0), (0, 0), (delta - 1, 0), (0, 0)))
            idx = jnp.arange(t.shape[2])[:, None] + jnp.arange(delta)[None, :]
            return padded[:, :, idx]
        key = jax.random.key(seed)
        ks = jax.random.split(key, 16)
        s = 0.02
        inp = {'x': jax.random.normal(ks[0], (B, T, C), dtype=jnp.float32), 'w_disp': jax.random.normal(ks[1], (C, NH * BD), dtype=jnp.float32) * s, 'b_disp': jnp.zeros((NH * BD,), dtype=jnp.float32), 'w_val': jax.random.normal(ks[2], (C, C), dtype=jnp.float32) * s, 'b_val': jnp.zeros((C,), dtype=jnp.float32), 'rel_pos_emb': jax.random.normal(ks[3], (HORIZON, BD), dtype=jnp.float32) * s, 'w_state': jax.random.normal(ks[4], (BD, BD), dtype=jnp.float32) * s, 'b_state': jnp.zeros((BD,), dtype=jnp.float32), 'w_strain': jax.random.normal(ks[5], (BD, BD), dtype=jnp.float32) * s, 'b_strain': jnp.zeros((BD,), dtype=jnp.float32), 'w_state_i': jax.random.normal(ks[6], (BD, BD), dtype=jnp.float32) * s, 'w_state_j': jax.random.normal(ks[7], (BD, BD), dtype=jnp.float32) * s, 'w_pos': jax.random.normal(ks[8], (BD, BD), dtype=jnp.float32) * s, 'w_bond_out': jax.random.normal(ks[9], (BD, 1), dtype=jnp.float32) * s, 'b_bond_out': jnp.zeros((1,), dtype=jnp.float32), 'w_damage': jax.random.normal(ks[10], (BD, BD), dtype=jnp.float32) * s, 'b_damage': jnp.zeros((BD,), dtype=jnp.float32), 'w_damage_out': jax.random.normal(ks[11], (BD, 1), dtype=jnp.float32) * s, 'b_damage_out': jnp.full((1,), -3.0, dtype=jnp.float32), 'w_cproj': jax.random.normal(ks[12], (C, C), dtype=jnp.float32) * s, 'b_cproj': jnp.zeros((C,), dtype=jnp.float32)}
        return inp
    _L0_attn_in = _L0_attn_setup()

    def _L0_ffn_setup():
        import jax, jax.numpy as jnp
        import numpy as np
        D = 256
        H = 1024
        E = 64
        K = 3
        B, S = (2, 512)
        C = 128
        key = jax.random.key(seed)
        ks = jax.random.split(key, 6)
        s = 0.02
        return {'x': jax.random.normal(ks[0], (B, S, D), jnp.float32), 'gate_w': jax.random.normal(ks[1], (D, E), jnp.float32) * s, 'gate_b': jnp.zeros((E,), jnp.float32), 'w1': jax.random.normal(ks[2], (E, D, H), jnp.float32) * s, 'b1': jnp.zeros((E, H), jnp.float32), 'w2': jax.random.normal(ks[3], (E, H, D), jnp.float32) * s, 'b2': jnp.zeros((E, D), jnp.float32)}
    _L0_ffn_in = _L0_ffn_setup()

    def _L1_attn_setup():
        import jax, jax.numpy as jnp
        import numpy as np
        NUM_HEADS = 16
        CLIP = 16
        key = jax.random.key(seed)
        ks = jax.random.split(key, 7)
        d = 256
        return {'x': jax.random.normal(ks[0], (2, 512, d), dtype=jnp.float32), 'Wq': jax.random.normal(ks[1], (d, d), dtype=jnp.float32) / np.sqrt(d), 'Wk': jax.random.normal(ks[2], (d, d), dtype=jnp.float32) / np.sqrt(d), 'Wv': jax.random.normal(ks[3], (d, d), dtype=jnp.float32) / np.sqrt(d), 'Wo': jax.random.normal(ks[4], (d, d), dtype=jnp.float32) / np.sqrt(d), 'bo': jax.random.normal(ks[5], (d,), dtype=jnp.float32) * 0.01, 'rel_emb': jax.random.normal(ks[6], (CLIP + 1,), dtype=jnp.float32)}
    _L1_attn_in = _L1_attn_setup()

    def _L1_ffn_setup():
        import jax, jax.numpy as jnp
        import numpy as np
        B, S, D, E, H, K = (4, 512, 256, 8, 128, 2)
        key = jax.random.key(seed)
        ks = jax.random.split(key, 11)
        sc = 0.02
        return {'x': jax.random.normal(ks[0], (B, S, D), dtype=jnp.float32), 'gate_W': jax.random.normal(ks[1], (D, E), dtype=jnp.float32) * sc, 'W1': jax.random.normal(ks[2], (E, D, H), dtype=jnp.float32) * sc, 'b1': jnp.zeros((E, H), dtype=jnp.float32), 'W2': jax.random.normal(ks[3], (E, H, D), dtype=jnp.float32) * sc, 'b2': jnp.zeros((E, D), dtype=jnp.float32), 'Ws1': jax.random.normal(ks[4], (D, H), dtype=jnp.float32) * sc, 'bs1': jnp.zeros((H,), dtype=jnp.float32), 'Ws2': jax.random.normal(ks[5], (H, D), dtype=jnp.float32) * sc, 'bs2': jnp.zeros((D,), dtype=jnp.float32), 'route_scale': jnp.ones((), dtype=jnp.float32)}
    _L1_ffn_in = _L1_ffn_setup()
    _d = {'L0_attn_x': _L0_attn_in['x'], 'L0_attn_w_disp': _L0_attn_in['w_disp'], 'L0_attn_b_disp': _L0_attn_in['b_disp'], 'L0_attn_w_val': _L0_attn_in['w_val'], 'L0_attn_b_val': _L0_attn_in['b_val'], 'L0_attn_rel_pos_emb': _L0_attn_in['rel_pos_emb'], 'L0_attn_w_state': _L0_attn_in['w_state'], 'L0_attn_b_state': _L0_attn_in['b_state'], 'L0_attn_w_strain': _L0_attn_in['w_strain'], 'L0_attn_b_strain': _L0_attn_in['b_strain'], 'L0_attn_w_state_i': _L0_attn_in['w_state_i'], 'L0_attn_w_state_j': _L0_attn_in['w_state_j'], 'L0_attn_w_pos': _L0_attn_in['w_pos'], 'L0_attn_w_bond_out': _L0_attn_in['w_bond_out'], 'L0_attn_b_bond_out': _L0_attn_in['b_bond_out'], 'L0_attn_w_damage': _L0_attn_in['w_damage'], 'L0_attn_b_damage': _L0_attn_in['b_damage'], 'L0_attn_w_damage_out': _L0_attn_in['w_damage_out'], 'L0_attn_b_damage_out': _L0_attn_in['b_damage_out'], 'L0_attn_w_cproj': _L0_attn_in['w_cproj'], 'L0_attn_b_cproj': _L0_attn_in['b_cproj'], 'L0_ffn_gate_w': _L0_ffn_in['gate_w'], 'L0_ffn_gate_b': _L0_ffn_in['gate_b'], 'L0_ffn_w1': _L0_ffn_in['w1'], 'L0_ffn_b1': _L0_ffn_in['b1'], 'L0_ffn_w2': _L0_ffn_in['w2'], 'L0_ffn_b2': _L0_ffn_in['b2'], 'L1_attn_Wq': _L1_attn_in['Wq'], 'L1_attn_Wk': _L1_attn_in['Wk'], 'L1_attn_Wv': _L1_attn_in['Wv'], 'L1_attn_Wo': _L1_attn_in['Wo'], 'L1_attn_bo': _L1_attn_in['bo'], 'L1_attn_rel_emb': _L1_attn_in['rel_emb'], 'L1_ffn_gate_W': _L1_ffn_in['gate_W'], 'L1_ffn_W1': _L1_ffn_in['W1'], 'L1_ffn_b1': _L1_ffn_in['b1'], 'L1_ffn_W2': _L1_ffn_in['W2'], 'L1_ffn_b2': _L1_ffn_in['b2'], 'L1_ffn_Ws1': _L1_ffn_in['Ws1'], 'L1_ffn_bs1': _L1_ffn_in['bs1'], 'L1_ffn_Ws2': _L1_ffn_in['Ws2'], 'L1_ffn_bs2': _L1_ffn_in['bs2'], 'L1_ffn_route_scale': _L1_ffn_in['route_scale']}
    _x0 = _d['L0_attn_x']
    _d['L0_attn_x'] = jax.random.normal(jax.random.fold_in(jax.random.key(seed), 1), (8, 512, 256), dtype=_x0.dtype)
    del _x0
    return _d

def reference(L0_attn_x, L0_attn_w_disp, L0_attn_b_disp, L0_attn_w_val, L0_attn_b_val, L0_attn_rel_pos_emb, L0_attn_w_state, L0_attn_b_state, L0_attn_w_strain, L0_attn_b_strain, L0_attn_w_state_i, L0_attn_w_state_j, L0_attn_w_pos, L0_attn_w_bond_out, L0_attn_b_bond_out, L0_attn_w_damage, L0_attn_b_damage, L0_attn_w_damage_out, L0_attn_b_damage_out, L0_attn_w_cproj, L0_attn_b_cproj, L0_ffn_gate_w, L0_ffn_gate_b, L0_ffn_w1, L0_ffn_b1, L0_ffn_w2, L0_ffn_b2, L1_attn_Wq, L1_attn_Wk, L1_attn_Wv, L1_attn_Wo, L1_attn_bo, L1_attn_rel_emb, L1_ffn_gate_W, L1_ffn_W1, L1_ffn_b1, L1_ffn_W2, L1_ffn_b2, L1_ffn_Ws1, L1_ffn_bs1, L1_ffn_Ws2, L1_ffn_bs2, L1_ffn_route_scale):

    def _L0_attn_ref(x, w_disp, b_disp, w_val, b_val, rel_pos_emb, w_state, b_state, w_strain, b_strain, w_state_i, w_state_j, w_pos, w_bond_out, b_bond_out, w_damage, b_damage, w_damage_out, b_damage_out, w_cproj, b_cproj):
        import jax, jax.numpy as jnp
        import numpy as np
        B, T, C = (2, 512, 256)
        NH = 16
        HS = C // NH
        BD = max(HS // 4, 16)
        HORIZON = 32

        def _windows(t, delta):
            padded = jnp.pad(t, ((0, 0), (0, 0), (delta - 1, 0), (0, 0)))
            idx = jnp.arange(t.shape[2])[:, None] + jnp.arange(delta)[None, :]
            return padded[:, :, idx]
        Bx, Tx, Cx = x.shape
        delta = min(HORIZON, Tx)
        gelu = lambda v: jax.nn.gelu(v, approximate=False)
        disp = (x @ w_disp + b_disp).reshape(Bx, Tx, NH, BD).transpose(0, 2, 1, 3)
        val = (x @ w_val + b_val).reshape(Bx, Tx, NH, HS).transpose(0, 2, 1, 3)
        disp_win = _windows(disp, delta)
        val_win = _windows(val, delta)
        cmask = jnp.arange(Tx)[:, None] - delta + 1 + jnp.arange(delta)[None, :] >= 0
        cmask_f = cmask.astype(x.dtype)
        strain = disp_win - disp[:, :, :, None, :]
        strain_for_state = strain @ w_state + b_state
        valid_counts = jnp.clip(cmask_f.sum(axis=-1), 1.0)
        state = (strain_for_state * cmask_f[None, None, :, :, None]).sum(axis=3) / valid_counts[None, None, :, None]
        state_win = _windows(state, delta)
        rel_emb = rel_pos_emb[:delta]
        bond_act = gelu(strain @ w_strain + b_strain + state[:, :, :, None, :] @ w_state_i + state_win @ w_state_j + rel_emb @ w_pos)
        bond_logits = (bond_act @ w_bond_out)[..., 0] + b_bond_out[0]
        damage_act = gelu(strain @ w_damage + b_damage)
        damage = jax.nn.sigmoid((damage_act @ w_damage_out)[..., 0] + b_damage_out[0])
        logits = bond_logits - damage * 10.0
        logits = jnp.where(cmask[None, None], logits, -jnp.inf)
        weights = jax.nn.softmax(logits, axis=-1)
        out = jnp.einsum('bntd,bntde->bnte', weights, val_win)
        out = out.transpose(0, 2, 1, 3).reshape(Bx, Tx, Cx)
        return out @ w_cproj + b_cproj

    def _L0_ffn_ref(x, gate_w, gate_b, w1, b1, w2, b2):
        import jax, jax.numpy as jnp
        import numpy as np
        D = 256
        H = 1024
        E = 64
        K = 3
        B, S = (2, 512)
        C = 128
        xf = x.reshape(-1, D)
        T = xf.shape[0]
        logits = xf @ gate_w + gate_b
        top_l, top_i = jax.lax.top_k(logits, K)
        gates = jax.nn.softmax(top_l, axis=-1)
        fe = top_i.reshape(-1)
        fg = gates.reshape(-1)
        tok = jnp.repeat(jnp.arange(T), K)
        oh = jax.nn.one_hot(fe, E, dtype=jnp.int32)
        pos = (jnp.cumsum(oh, axis=0) * oh).sum(-1) - 1
        valid = pos < C
        buf = jnp.zeros((E, C, D), x.dtype).at[fe, pos].set(xf[tok], mode='drop')
        h = jax.nn.gelu(jnp.einsum('ecd,edh->ech', buf, w1) + b1[:, None, :], approximate=False)
        y = jnp.einsum('ech,ehd->ecd', h, w2) + b2[:, None, :]
        rows = y[fe, jnp.minimum(pos, C - 1)] * (fg * valid.astype(x.dtype))[:, None]
        out = jnp.zeros_like(xf).at[tok].add(rows)
        return out.reshape(x.shape)

    def _L1_attn_ref(x, Wq, Wk, Wv, Wo, bo, rel_emb):
        import jax, jax.numpy as jnp
        import numpy as np
        NUM_HEADS = 16
        CLIP = 16
        b, s, d_in = x.shape
        h, hd = (NUM_HEADS, x.shape[-1] // NUM_HEADS)
        q = (x @ Wq).reshape(b, s, h, hd).transpose(0, 2, 1, 3)
        k = (x @ Wk).reshape(b, s, h, hd).transpose(0, 2, 1, 3)
        v = (x @ Wv).reshape(b, s, h, hd).transpose(0, 2, 1, 3)
        r = jnp.arange(s)
        dist = jnp.clip(jnp.abs(r[None, :] - r[:, None]), 0, CLIP)
        a_k = rel_emb[dist]
        scores = jnp.einsum('bhqd,bhkd->bhqk', q, k) * a_k
        causal = jnp.triu(jnp.ones((s, s), dtype=bool), k=1)
        scores = jnp.where(causal, -jnp.inf, scores)
        attn = jax.nn.softmax(scores / np.sqrt(hd), axis=-1)
        ctx = jnp.einsum('bhqk,bhkd->bhqd', attn, v)
        ctx = ctx.transpose(0, 2, 1, 3).reshape(b, s, h * hd)
        return ctx @ Wo + bo

    def _L1_ffn_ref(x, gate_W, W1, b1, W2, b2, Ws1, bs1, Ws2, bs2, route_scale):
        import jax, jax.numpy as jnp
        import numpy as np
        B, S, D, E, H, K = (4, 512, 256, 8, 128, 2)
        scores = jax.nn.sigmoid(x @ gate_W) * route_scale
        topk_scores, topk_idx = jax.lax.top_k(scores, K)
        topk_w = topk_scores / topk_scores.sum(-1, keepdims=True)
        onehot = jax.nn.one_hot(topk_idx, E, dtype=x.dtype)
        gate_full = jnp.einsum('bsk,bske->bse', topk_w, onehot)
        h = jax.nn.gelu(jnp.einsum('bsd,edh->bseh', x, W1) + b1, approximate=False)
        y = jnp.einsum('bseh,ehd->bsed', h, W2) + b2
        expert_out = jnp.einsum('bse,bsed->bsd', gate_full, y)
        shared = jax.nn.gelu(x @ Ws1 + bs1, approximate=False) @ Ws2 + bs2
        return expert_out + shared
    x = L0_attn_x
    x = x + 0.5 * _L0_ffn_ref(_layernorm(x, axis=-1), L0_ffn_gate_w, L0_ffn_gate_b, L0_ffn_w1, L0_ffn_b1, L0_ffn_w2, L0_ffn_b2)
    x = x + _L0_attn_ref(_layernorm(x, axis=-1), L0_attn_w_disp, L0_attn_b_disp, L0_attn_w_val, L0_attn_b_val, L0_attn_rel_pos_emb, L0_attn_w_state, L0_attn_b_state, L0_attn_w_strain, L0_attn_b_strain, L0_attn_w_state_i, L0_attn_w_state_j, L0_attn_w_pos, L0_attn_w_bond_out, L0_attn_b_bond_out, L0_attn_w_damage, L0_attn_b_damage, L0_attn_w_damage_out, L0_attn_b_damage_out, L0_attn_w_cproj, L0_attn_b_cproj)
    x = x + 0.5 * _L0_ffn_ref(_layernorm(x, axis=-1), L0_ffn_gate_w, L0_ffn_gate_b, L0_ffn_w1, L0_ffn_b1, L0_ffn_w2, L0_ffn_b2)
    x = x + 0.5 * _L1_ffn_ref(_layernorm(x, axis=-1), L1_ffn_gate_W, L1_ffn_W1, L1_ffn_b1, L1_ffn_W2, L1_ffn_b2, L1_ffn_Ws1, L1_ffn_bs1, L1_ffn_Ws2, L1_ffn_bs2, L1_ffn_route_scale)
    x = x + _L1_attn_ref(_layernorm(x, axis=-1), L1_attn_Wq, L1_attn_Wk, L1_attn_Wv, L1_attn_Wo, L1_attn_bo, L1_attn_rel_emb)
    x = x + 0.5 * _L1_ffn_ref(_layernorm(x, axis=-1), L1_ffn_gate_W, L1_ffn_W1, L1_ffn_b1, L1_ffn_W2, L1_ffn_b2, L1_ffn_Ws1, L1_ffn_bs1, L1_ffn_Ws2, L1_ffn_bs2, L1_ffn_route_scale)
    return x

_drawn_inputs = setup_inputs


def setup_inputs(seed=0):
    import zlib

    import numpy as np

    out = dict(_drawn_inputs(seed))
    spreads = {'L0_attn_b_disp': (0.0, 2.0),
     'L0_attn_b_val': (0.0, 0.1),
     'L0_attn_b_state': (0.0, 2.0),
     'L0_attn_b_strain': (0.0, 2.0),
     'L0_attn_b_damage': (0.0, 2.0),
     'L0_attn_b_cproj': (0.0, 0.1),
     'L0_ffn_gate_b': (0.0, 0.1),
     'L0_ffn_b1': (0.0, 0.43),
     'L0_ffn_b2': (0.0, 0.1),
     'L1_ffn_b1': (0.0, 0.8),
     'L1_ffn_b2': (0.0, 0.1),
     'L1_ffn_bs1': (0.0, 0.603),
     'L1_ffn_bs2': (0.0, 0.1)}
    factors = {'L0_attn_w_disp': 8.0,
     'L0_attn_rel_pos_emb': 64.0,
     'L0_attn_w_state': 26.686,
     'L0_attn_w_strain': 8.0,
     'L0_attn_w_state_i': 43.34,
     'L0_attn_w_state_j': 21.82,
     'L0_attn_w_pos': 64.0,
     'L0_attn_w_bond_out': 8.0,
     'L0_attn_w_damage': 37.521,
     'L0_attn_w_damage_out': 24.823,
     'L1_attn_bo': 5.343}
    for name, (base, spread) in spreads.items():
        noise = np.random.default_rng([zlib.crc32(name.encode()), seed]).standard_normal(out[name].shape)
        drawn = base * np.exp(spread * noise) if base else spread * noise
        out[name] = jnp.asarray(drawn.astype(out[name].dtype))
    for name, factor in factors.items():
        out[name] = (out[name] * factor).astype(out[name].dtype)
    return out
```

```python
from contextlib import ExitStack

import numpy as np

import concourse.bass as bass
from concourse import mybir

FP32 = mybir.dt.float32
BF16 = mybir.dt.bfloat16
U32 = mybir.dt.uint32
ALU = mybir.AluOpType
ACT = mybir.ActivationFunctionType
AX = mybir.AxisListType

P = 128
B, S, D = 8, 512, 256
TPB = S // P
DC = D // P
EPS = 1e-5


def due(count):
    return not isinstance(count, int) or count > 0


class Core:

    def __init__(self, nc, ctx):
        self.nc = nc
        self.sems = []
        self.x = ctx.enter_context(nc.sbuf_tensor("x_resid", [P, (B + 2) * TPB, D], FP32))
        self.ident = ctx.enter_context(nc.sbuf_tensor("ident", [P, P], FP32))

    def semaphore(self, name):
        self.sems.append(self.nc.alloc_semaphore(name))
        return self.sems[-1]

    def free_semaphores(self):
        self.nc.clear_and_free_semaphores(self.sems)
        self.nc.all_engine_barrier()
        self.sems = []

    def x_batch(self, i):
        return self.x[:, bass.ds((i + 1) * TPB, TPB), :]

    def tile(self, n, j):
        return self.x[:, n * TPB + j, :]


def load_phase(core, x_dram):
    nc = core.nc
    with ExitStack() as ctx:
        x_in = core.semaphore("x_in")
        zeroed = core.semaphore("zeroed")
        block = ctx.enter_context(nc.Block())

        @block.sync
        def _(sp):
            sp.dma_start(core.x[:, TPB:(B + 1) * TPB, :],
                         x_dram.rearrange("b (j p) d -> p (b j) d", p=P)).then_inc(x_in, 16)
            sp.wait_ge(x_in, 16)

        @block.gpsimd
        def _(pool):
            nc.gpsimd.memset(core.x[:, (B + 1) * TPB:, :], 0.0)
            nc.gpsimd.memset(core.x[:, 0:TPB, :], 0.0)
            nc.gpsimd.memset(core.ident[:, :], 0.0).then_inc(zeroed, 1)
            pool.wait_ge(zeroed, 1)
            nc.gpsimd.affine_select(out=core.ident[:, :], in_=core.ident[:, :], compare_op=ALU.not_equal,
                                    fill=1.0, base=0, pattern=[[-1, P]], channel_multiplier=1)


def store_phase(core, out_dram):
    nc = core.nc
    with ExitStack() as ctx:
        stored = core.semaphore("stored")
        block = ctx.enter_context(nc.Block())

        @block.sync
        def _(sp):
            sp.dma_start(out_dram.rearrange("b (j p) d -> p (b j) d", p=P),
                         core.x[:, TPB:(B + 1) * TPB, :]).then_inc(stored, 16)
            sp.wait_ge(stored, 16)


class Norm:

    def __init__(self, core, ctx, name, xn_buffers=1, pad=0):
        nc = core.nc
        self.core, self.nc = core, nc
        sb = lambda n, s: ctx.enter_context(nc.sbuf_tensor(f"{name}_{n}", s, FP32))
        sem = lambda n: core.semaphore(f"{name}_{n}")
        self.stats = sb("stats", [P, TPB, 6])
        self.mean_var = sb("mean_var", [P, TPB, 2])
        self.var_eps = sb("var_eps", [P, TPB])
        self.std = sb("std", [P, TPB])
        self.rstd = sb("rstd", [P, TPB])
        self.xns = [sb(f"xn{k}", [P, TPB, D]) for k in range(xn_buffers)]
        self.pad = pad
        self.xn_t = [sb(f"xn_t{k}", [P, DC, pad + S]) for k in range(2)]
        self.tp = ctx.enter_context(nc.psum_tensor(f"{name}_tp", [P, S], FP32))
        self.var_ready = sem("var_ready")
        self.std_ready = sem("std_ready")
        self.xn_ready = sem("xn_ready")
        self.t_ready = sem("t_ready")
        self.t_copied = sem("t_copied")
        self.free = sem("xn_t_free")

    def dve_stats(self, i):
        nc = self.nc
        for j in range(TPB):
            nc.vector.bn_stats(self.stats[:, j, :], self.core.tile(i + 1, j))
        nc.vector.drain()
        for j in range(TPB):
            nc.vector.bn_aggr(self.mean_var[:, j, :], self.stats[:, j, :])
        nc.vector.drain()
        nc.vector.tensor_scalar(self.var_eps[:, :], self.mean_var[:, :, 1], EPS, None,
                                ALU.add).then_inc(self.var_ready, 1)

    def act_std(self, i):
        self.nc.scalar.wait_ge(self.var_ready, i + 1)
        self.nc.scalar.activation(self.std[:, :], self.var_eps[:, :], ACT.Sqrt).then_inc(self.std_ready, 1)

    def dve_normalise(self, i, k=0):
        nc = self.nc
        nc.vector.wait_ge(self.std_ready, i + 1)
        nc.vector.reciprocal(self.rstd[:, :], self.std[:, :])
        nc.vector.drain()
        for j in range(TPB):
            last = nc.vector.tensor_scalar(self.xns[k][:, j, :], self.core.tile(i + 1, j),
                                           self.mean_var[:, j, 0:1], self.rstd[:, j:j + 1],
                                           ALU.subtract, ALU.mult)
        last.then_inc(self.xn_ready, 1)

    def pe_transpose(self, i, k=0):
        nc = self.nc
        nc.tensor.wait_ge(self.xn_ready, i + 1)
        for c in range(DC):
            if due(i * DC + c):
                nc.tensor.wait_ge(self.t_copied, i * DC + c)
            for j in range(TPB):
                last = nc.tensor.transpose(self.tp[:, j * P:(j + 1) * P], self.xns[k][:, j, c * P:(c + 1) * P],
                                           self.core.ident[:, :])
            last.then_inc(self.t_ready, 1)

    def dve_copy_t(self, i, k, guard=True):
        nc = self.nc
        if guard:
            if due(i - 1):
                nc.vector.wait_ge(self.free, i - 1)
        for c in range(DC):
            nc.vector.wait_ge(self.t_ready, i * DC + c + 1)
            nc.vector.tensor_copy(self.xn_t[k][:, c, self.pad:], self.tp[:, :]).then_inc(self.t_copied, 1)

    def wait_xn_t(self, eng, i):
        eng.wait_ge(self.t_copied, (i + 1) * DC)



def ffn1_phase(core, name, gate_w, w1, b1, w2, b2, ws1, bs1, ws2, bs2, route_scale):
    nc = core.nc
    E, H = w1.shape[0], w1.shape[2]
    NE = E + 1
    UNITS = 2 * (NE + 1)
    YB = 4
    ctx = ExitStack()
    with ctx:
        sb = lambda n, s, dt=FP32: ctx.enter_context(nc.sbuf_tensor(f"{name}_{n}", s, dt))
        ps = lambda n, s: ctx.enter_context(nc.psum_tensor(f"{name}_{n}", s, FP32))
        sem = lambda n: core.semaphore(f"{name}_{n}")
        norm = Norm(core, ctx, name)
        gate_w_sb = sb("gate_w", [P, DC, E])
        w1_sb = sb("w1", [P, NE, DC, H])
        w2_sb = sb("w2", [P, NE, D])
        b1_sb = sb("b1", [P, NE])
        b2_sb = sb("b2", [NE, D])
        route_sb = sb("route", [P, 1])
        iota_e = sb("iota_e", [P, TPB, E])
        sig = sb("sig", [P, TPB, E])
        score = sb("score", [P, TPB, E])
        top_v = sb("top_v", [P, TPB, 8])
        top_i = sb("top_i", [P, TPB, 8], U32)
        top_f = sb("top_f", [P, TPB, 2])
        inv = sb("inv", [P, TPB, 1])
        part = [sb(f"part{r}", [P, TPB, E]) for r in range(2)]
        weight = sb("weight", [P, TPB, 2])
        gate = [sb(f"gate{k}", [P, TPB, NE]) for k in range(2)]
        gate_t = [sb(f"gate_t{k}", [NE, S]) for k in range(2)]
        h_t = [sb(f"h_t{k}", [P, S]) for k in range(2)]
        acc = sb("acc", [P, TPB, D])
        gate_ps = ps("gate_ps", [P, 512])
        h_ps = [ps(f"h_ps{k}", [P, S]) for k in range(2)]
        y_ps = [ps(f"y_ps{k}", [P, 2, D]) for k in range(YB)]

        loaded = sem("loaded")
        const_ready = sem("const_ready")
        logits_ready = sem("logits_ready")
        sig_ready = sem("sig_ready")
        gate_ready = sem("gate_ready")
        gate_t_ready = sem("gate_t_ready")
        gate_t_copied = sem("gate_t_copied")
        h_ready = sem("h_ready")
        act_ready = sem("act_ready")
        y_ready = sem("y_ready")
        y_free = sem("y_free")
        block = ctx.enter_context(nc.Block())

        @block.sync
        def _(sp):
            def load(dst, src, **kind):
                sp.dma_start(dst, src, **kind).then_inc(loaded, 16)
            load(gate_w_sb[:, :, :], gate_w.rearrange("(c p) e -> p c e", p=P))
            load(route_sb[:, :], route_scale.partition_broadcast(P))
            for e in range(E):
                load(w1_sb[:, e, :, :], w1[e].rearrange("(c p) h -> p c h", p=P))
            load(w1_sb[:, E, :, :], ws1.rearrange("(c p) h -> p c h", p=P))
            load(w2_sb[:, 0:E, :], w2.rearrange("e h d -> h e d"))
            load(w2_sb[:, E, :], ws2)
            load(b1_sb[:, 0:E], b1.rearrange("e h -> h e"), allow_slow_non_contiguous=True)
            load(b1_sb[:, E:NE], bs1.rearrange("(h o) -> h o", o=1))
            load(b2_sb[0:E, :], b2)
            load(b2_sb[E:NE, :], bs2.rearrange("(o d) -> o d", o=1))
        LOADED = 16 * (E + 9)

        @block.gpsimd
        def _(pool):
            nc.gpsimd.iota(iota_e[:, :, :], pattern=[[0, TPB], [1, E]], base=0, channel_multiplier=0,
                           allow_small_or_imprecise_dtypes=True)
            for k in range(2):
                last = nc.gpsimd.memset(gate[k][:, :, E:NE], 1.0)
            last.then_inc(const_ready, 1)

        @block.tensor
        def _(pe):
            def logits(i, k):
                norm.wait_xn_t(pe, i)
                for j in range(TPB):
                    for c in range(DC):
                        last = nc.tensor.matmul(gate_ps[:, j * E:(j + 1) * E],
                                                norm.xn_t[k][:, c, j * P:(j + 1) * P],
                                                gate_w_sb[:, c, :], start=c == 0, stop=c == DC - 1)
                last.then_inc(logits_ready, 1)

            def turn_gates(i, k):
                pe.wait_ge(gate_ready, i + 1)
                for j in range(TPB):
                    last = nc.tensor.transpose(gate_ps[0:NE, j * P:(j + 1) * P], gate[k][:, j, :],
                                               core.ident[:, :])
                last.then_inc(gate_t_ready, 1)

            def up(i, k, e):
                n = i * NE + e
                pe.wait_ge(act_ready, n + 1)
                if e == 0:
                    norm.wait_xn_t(pe, i)
                for c in range(DC):
                    last = nc.tensor.matmul(h_ps[(k * NE + e) % 2][:, :], w1_sb[:, e, c, :],
                                            norm.xn_t[k][:, c, :], start=c == 0, stop=c == DC - 1)
                last.then_inc(h_ready, 1)

            def down(i, k, e):
                pe.wait_ge(act_ready, 2 + i * NE + e + 1)
                h = h_t[(k * NE + e) % 2]
                for half in range(2):
                    m = 2 * (e + 1) + half
                    pe.wait_ge(y_free, i * UNITS + m + 1)
                    for j in range(2):
                        t = 2 * half + j
                        last = nc.tensor.matmul(y_ps[m % YB][:, j, :], h[:, t * P:(t + 1) * P],
                                                w2_sb[:, e, :], start=True, stop=True)
                        if e == NE - 1 and t == 0:
                            last.then_inc(norm.free, 1)
                    last.then_inc(y_ready, 1)

            def biases(i, k):
                pe.wait_ge(gate_t_copied, i + 1)
                for half in range(2):
                    pe.wait_ge(y_free, i * UNITS + half + 1)
                    for j in range(2):
                        t = 2 * half + j
                        last = nc.tensor.matmul(y_ps[half][:, j, :], gate_t[k][:, t * P:(t + 1) * P],
                                                b2_sb[:, :], start=True, stop=True)
                    last.then_inc(y_ready, 1)

            pe.wait_ge(loaded, LOADED)
            norm.pe_transpose(0)
            logits(0, 0)
            turn_gates(0, 0)
            with pe.Fori(0, B // 2) as pair:
                for k in range(2):
                    i = pair * 2 + k
                    up(i, k, 0)
                    biases(i, k)
                    for e in range(NE):
                        if e + 1 < NE:
                            up(i, k, e + 1)
                        down(i, k, e)
                        if e == 2:
                            norm.pe_transpose(i + 1)
                        if e == 4:
                            logits(i + 1, 1 - k)
                        if e == 6:
                            turn_gates(i + 1, 1 - k)

        @block.scalar
        def _(act):
            def sigmoid(i):
                act.wait_ge(logits_ready, i + 1)
                nc.scalar.activation(sig[:, :, :], gate_ps[:, 0:TPB * E].rearrange("p (j e) -> p j e", e=E),
                                     ACT.Sigmoid).then_inc(sig_ready, 1)

            def gelu(i, k, e):
                n = i * NE + e
                act.wait_ge(h_ready, n + 1)
                act.wait_ge(y_ready, i * UNITS + 2 * e)
                nc.scalar.activation(h_t[(k * NE + e) % 2][:, :], h_ps[(k * NE + e) % 2][:, :], ACT.Gelu,
                                     bias=b1_sb[:, e:e + 1]).then_inc(act_ready, 1)

            act.sem_inc(act_ready, 2)
            act.wait_ge(loaded, LOADED)
            norm.act_std(0)
            sigmoid(0)
            with act.Fori(0, B // 2) as pair:
                for k in range(2):
                    i = pair * 2 + k
                    for e in range(NE):
                        gelu(i, k, e)
                        if e == 1:
                            norm.act_std(i + 1)
                        if e == 5:
                            sigmoid(i + 1)

        @block.vector
        def _(dve):
            def gates(i, k):
                dve.wait_ge(sig_ready, i + 1)
                nc.vector.tensor_scalar(score[:, :, :], sig[:, :, :], route_sb[:, 0:1], None, ALU.mult)
                nc.vector.drain()
                for j in range(TPB):
                    nc.vector.max(top_v[:, j, :], score[:, j, :])
                nc.vector.drain()
                for j in range(TPB):
                    nc.vector.max_index(top_i[:, j, :], top_v[:, j, :], score[:, j, :])
                nc.vector.tensor_tensor(inv[:, :, :], top_v[:, :, 0:1], top_v[:, :, 1:2], ALU.add)
                nc.vector.drain()
                nc.vector.reciprocal(inv[:, :, :], inv[:, :, :])
                nc.vector.tensor_copy(top_f[:, :, :], top_i[:, :, 0:2])
                nc.vector.drain()
                nc.vector.tensor_tensor(weight[:, :, :], top_v[:, :, 0:2],
                                        inv[:, :, :].broadcast_to([P, TPB, 2]), ALU.mult)
                for r in range(2):
                    nc.vector.tensor_tensor(part[r][:, :, :], iota_e[:, :, :],
                                            top_f[:, :, r:r + 1].broadcast_to([P, TPB, E]), ALU.is_equal)
                nc.vector.drain()
                for r in range(2):
                    nc.vector.tensor_tensor(part[r][:, :, :], part[r][:, :, :],
                                            weight[:, :, r:r + 1].broadcast_to([P, TPB, E]), ALU.mult)
                nc.vector.drain()
                nc.vector.tensor_tensor(gate[k][:, :, 0:E], part[0][:, :, :], part[1][:, :, :],
                                        ALU.add).then_inc(gate_ready, 1)

            def copy_gates(i, k):
                dve.wait_ge(gate_t_ready, i + 1)
                nc.vector.tensor_copy(gate_t[k][:, :], gate_ps[0:NE, :]).then_inc(gate_t_copied, 1)

            def add(i, k, n):
                nc.vector.drain()
                for half in range(2):
                    m = 2 * n + half
                    dve.wait_ge(y_ready, 2 + i * UNITS + m + 1)
                    y = y_ps[m % YB]
                    if n == 0:
                        last = nc.vector.tensor_copy(acc[:, 2 * half:2 * half + 2, :], y[:, :, :])
                    else:
                        for j in range(2):
                            t = 2 * half + j
                            last = nc.vector.scalar_tensor_tensor(
                                out=acc[:, t, :], in0=y[:, j, :], scalar=gate[k][:, t, n - 1:n],
                                in1=acc[:, t, :], op0=ALU.mult, op1=ALU.add)
                    last.then_inc(y_free, 1)

            dve.sem_inc(y_ready, 2)
            dve.sem_inc(y_free, YB)
            dve.wait_ge(loaded, LOADED)
            dve.wait_ge(const_ready, 1)
            norm.dve_stats(0)
            norm.dve_normalise(0)
            norm.dve_copy_t(0, 0)
            gates(0, 0)
            copy_gates(0, 0)
            with dve.Fori(0, B // 2) as pair:
                for k in range(2):
                    i = pair * 2 + k
                    for n in range(NE + 1):
                        add(i, k, n)
                        if n == 1:
                            norm.dve_stats(i + 1)
                        if n == 2:
                            norm.dve_normalise(i + 1)
                        if n == 3:
                            norm.dve_copy_t(i + 1, 1 - k)
                        if n == 5:
                            gates(i + 1, 1 - k)
                        if n == 7:
                            copy_gates(i + 1, 1 - k)
                    nc.vector.drain()
                    nc.vector.scalar_tensor_tensor(out=core.x_batch(i), in0=acc[:, :, :], scalar=0.5,
                                                   in1=core.x_batch(i), op0=ALU.mult, op1=ALU.add)



MASKED = -1e30


def attn1_phase(core, name, wq, wk, wv, wo, bo, rel_emb):
    nc = core.nc
    NH = 16
    HD = D // NH
    CLIP = rel_emb.shape[0] - 1
    HG = 4
    QT = NH // HG
    SCALE = HD ** -0.5
    UNITS = TPB * NH
    PR = 8
    TR = 4
    TB = 2
    BY_ACT = [m % 5 in (1, 3) for m in range(UNITS)]
    BEFORE = [(m + 1 - sum(BY_ACT[:m + 1]), sum(BY_ACT[:m + 1])) for m in range(UNITS)]
    N_DVE, N_ACT = BEFORE[-1]
    ctx = ExitStack()
    with ctx:
        sb = lambda n, s, dt=FP32: ctx.enter_context(nc.sbuf_tensor(f"{name}_{n}", s, dt))
        ps = lambda n, s: ctx.enter_context(nc.psum_tensor(f"{name}_{n}", s, FP32))
        sem = lambda n: core.semaphore(f"{name}_{n}")
        norm = Norm(core, ctx, name)
        wq_sb = sb("wq", [P, DC, QT, HG, 32])
        wk_sb = sb("wk", [P, DC, QT, HG, 32])
        wv_sb = sb("wv", [P, DC, D])
        wo_sb = sb("wo", [P, DC, D])
        bo_sb = sb("bo", [1, D])
        ones = sb("ones", [1, P])
        rel_sb = sb("rel", [P, CLIP + 1])
        factor = sb("factor", [P, S])
        dist = sb("dist", [P, S])
        hit = sb("hit", [P, S])
        mask_f = sb("mask_f", [P, P])
        mask_b = sb("mask_b", [P, P], BF16)
        ident_b = sb("ident_b", [P, P], BF16)
        q_t = sb("q_t", [P, QT, S])
        k_t = sb("k_t", [P, QT, S])
        v_sb = sb("v", [P, TPB, NH, HD + 1])
        prob = sb("prob", [P, PR, S])
        top = sb("top", [P, 2, HG])
        neg_top = sb("neg_top", [P, 2, HG])
        prob_t = sb("prob_t", [P, TR, S])
        inv = sb("inv", [P, NH, 1])
        ctx_sb = sb("ctx", [P, D])
        ctx_t = sb("ctx_t", [P, DC, P])
        s_ps = [ps(f"s_ps{k}", [P, S]) for k in range(HG)]
        t_ps = [ps(f"t_ps{k}", [P, S]) for k in range(TB)]
        o_ps = ps("o_ps", [P, NH, HD + 1])
        misc = norm.tp

        loaded = sem("loaded")
        zeroed = sem("zeroed")
        consts = sem("consts")
        factor_ready = sem("factor_ready")
        proj_ready = sem("proj_ready")
        proj_dve = sem("proj_dve")
        proj_act = sem("proj_act")
        qk_ready = sem("qk_ready")
        s_free = sem("s_free")
        groups_begun = sem("groups_begun")
        top_ready = sem("top_ready")
        exp_ready = sem("exp_ready")
        turned = sem("turned")
        t_dve = sem("t_dve")
        t_act = sem("t_act")
        pv_done = sem("pv_done")
        ctx_ready = sem("ctx_ready")
        ctx_turned = sem("ctx_turned")
        ctx_copied = sem("ctx_copied")
        out_ready = sem("out_ready")
        out_added = sem("out_added")
        block = ctx.enter_context(nc.Block())

        @block.sync
        def _(sp):
            def load(dst, src):
                sp.dma_start(dst, src).then_inc(loaded, 16)
            load(wv_sb[:, :, :], wv.rearrange("(c p) n -> p c n", p=P))
            load(wo_sb[:, :, :], wo.rearrange("(c p) n -> p c n", p=P))
            load(bo_sb[:, :], bo.rearrange("(o n) -> o n", o=1))
            load(rel_sb[:, :], rel_emb.partition_broadcast(P))
            sp.wait_ge(zeroed, 2)
            for dst, src in ((wq_sb, wq), (wk_sb, wk)):
                for c in range(DC):
                    load(dst[:, c, :, :, 0:HD].rearrange("p t g d -> p (t g) d"),
                         src[c * P:(c + 1) * P, :].rearrange("p (h d) -> p h d", d=HD))
        LOADED = 16 * (4 + 2 * DC)

        @block.gpsimd
        def _(pool):
            nc.gpsimd.memset(wq_sb[:, :, :, :, :], 0.0).then_inc(zeroed, 1)
            nc.gpsimd.memset(wk_sb[:, :, :, :, :], 0.0).then_inc(zeroed, 1)
            nc.gpsimd.memset(ones[:, :], 1.0)
            nc.gpsimd.memset(v_sb[:, :, :, HD:HD + 1], 1.0)
            nc.gpsimd.iota(dist[:, :], pattern=[[-1, S]], base=S - P, channel_multiplier=1,
                           allow_small_or_imprecise_dtypes=True)
            nc.gpsimd.memset(mask_f[:, :], 0.0).then_inc(consts, 1)
            pool.wait_ge(consts, 1)
            nc.gpsimd.affine_select(out=mask_f[:, :], in_=mask_f[:, :], compare_op=ALU.is_ge,
                                    fill=MASKED, base=0, pattern=[[-1, P]],
                                    channel_multiplier=1).then_inc(consts, 1)

        @block.tensor
        def _(pe):
            def project(i, k):
                norm.wait_xn_t(pe, i)
                for n in range(2 * QT):
                    w_sb = (wq_sb, wk_sb)[n // QT]
                    if n >= HG:
                        pe.wait_ge((proj_dve, proj_act)[n % 2], i * (QT + 1) + (n - HG) // 2 + 1)
                    for c in range(DC):
                        last = nc.tensor.matmul(s_ps[n % HG][:, :], w_sb[:, c, n % QT, :, :].rearrange("p g d -> p (g d)"),
                                                norm.xn_t[k][:, c, :], start=c == 0, stop=c == DC - 1)
                    last.then_inc(proj_ready, 1)
                for half in range(2):
                    for j in range(2):
                        t = 2 * half + j
                        for c in range(DC):
                            last = nc.tensor.matmul(t_ps[half][:, j * D:(j + 1) * D],
                                                    norm.xn_t[k][:, c, t * P:(t + 1) * P], wv_sb[:, c, :],
                                                    start=c == 0, stop=c == DC - 1)
                    last.then_inc(proj_ready, 1)

            def scores(i, m):
                t, h = divmod(m, NH)
                tile, g = divmod(h, HG)
                width = (t + 1) * P
                pe.wait_ge(s_free, i * UNITS + m + 1)
                rows = slice(32 * g, 32 * g + HD)
                first = nc.tensor.matmul(s_ps[m % HG][:, 0:width], q_t[rows, tile, t * P:(t + 1) * P],
                                         k_t[rows, tile, 0:width], start=True, stop=False)
                if m == 0:
                    first.then_inc(norm.free, 1)
                nc.tensor.matmul(s_ps[m % HG][:, t * P:width], ident_b[:, :], mask_b[:, :],
                                 start=False, stop=True).then_inc(qk_ready, 1)

            def turn(i, m):
                t = m // NH
                pe.wait_ge(exp_ready, i * UNITS + m + 1)
                if m >= TB:
                    wait_copied(i, m - TB)
                for kb in range(t + 1):
                    last = nc.tensor.transpose(t_ps[m % TB][:, kb * P:(kb + 1) * P],
                                               prob[:, m % PR, kb * P:(kb + 1) * P], core.ident[:, :])
                last.then_inc(turned, 1)

            def wait_copied(i, m):
                dve_n, act_n = BEFORE[m]
                if BY_ACT[m]:
                    pe.wait_ge(t_act, i * N_ACT + act_n)
                else:
                    pe.wait_ge(t_dve, i * N_DVE + dve_n)

            def values(i, m):
                t, h = divmod(m, NH)
                wait_copied(i, m)
                if h == 0 and t > 0:
                    pe.wait_ge(ctx_ready, i * TPB + t)
                for kb in range(t + 1):
                    last = nc.tensor.matmul(o_ps[:, h, :], prob_t[:, m % TR, kb * P:(kb + 1) * P],
                                            v_sb[:, kb, h, :], start=kb == 0, stop=kb == t)
                last.then_inc(pv_done, 1)

            def turn_ctx(i, t):
                pe.wait_ge(ctx_ready, i * TPB + t + 1)
                pe.wait_ge(out_added, i * TPB + t)
                for c in range(DC):
                    last = nc.tensor.transpose(misc[:, c * P:(c + 1) * P], ctx_sb[:, c * P:(c + 1) * P],
                                               core.ident[:, :])
                last.then_inc(ctx_turned, 1)

            def output(i, t):
                pe.wait_ge(ctx_copied, i * TPB + t + 1)
                for c in range(DC):
                    nc.tensor.matmul(misc[:, D:2 * D], ctx_t[:, c, :], wo_sb[:, c, :],
                                     start=c == 0, stop=False)
                nc.tensor.matmul(misc[:, D:2 * D], ones[:, :], bo_sb[:, :], start=False,
                                 stop=True).then_inc(out_ready, 1)

            pe.wait_ge(loaded, LOADED)
            pe.wait_ge(factor_ready, 1)
            norm.pe_transpose(0)
            with pe.Fori(0, B // 2) as pair:
                for k in range(2):
                    i = pair * 2 + k
                    project(i, k)
                    pe.wait_ge(proj_dve, (i + 1) * (QT + 1))
                    pe.wait_ge(proj_act, (i + 1) * (QT + 1))
                    for m in range(HG):
                        scores(i, m)
                    for m in range(UNITS):
                        if m % HG == 0 and m + HG < UNITS:
                            for g in range(HG):
                                scores(i, m + HG + g)
                        turn(i, m)
                        if m >= 2:
                            values(i, m - 2)
                        if m > NH and m % NH == 4:
                            turn_ctx(i, m // NH - 1)
                        if m > NH and m % NH == 7:
                            output(i, m // NH - 1)
                        if m == NH + 14:
                            pe.wait_ge(out_added, i * TPB + 1)
                            norm.pe_transpose(i + 1)
                    values(i, UNITS - 2)
                    values(i, UNITS - 1)
                    turn_ctx(i, TPB - 1)
                    output(i, TPB - 1)

        @block.scalar
        def _(act):
            def empty(i, m):
                t = m // NH
                act.wait_ge(turned, PR + i * UNITS + m + 1)
                act.wait_ge(pv_done, i * UNITS + m + 1)
                nc.scalar.copy(prob_t[:, m % TR, 0:(t + 1) * P],
                               t_ps[m % TB][:, 0:(t + 1) * P]).then_inc(t_act, 1)

            def exps(i, m):
                t, h = divmod(m, NH)
                if h % HG == 0:
                    act.wait_ge(top_ready, i * (UNITS // HG) + m // HG + 1)
                nc.scalar.activation(prob[:, m % PR, 0:(t + 1) * P], prob[:, m % PR, 0:(t + 1) * P],
                                     ACT.Exp, bias=neg_top[:, (m // HG) % 2, h % HG:h % HG + 1]).then_inc(exp_ready, 1)

            act.sem_inc(turned, PR)
            act.sem_inc(pv_done, TR)
            act.wait_ge(loaded, LOADED)
            norm.act_std(0)
            with act.Fori(0, B // 2) as pair:
                for k in range(2):
                    i = pair * 2 + k
                    for n in range(1, 2 * QT, 2):
                        act.wait_ge(proj_ready, i * (2 * QT + 2) + n + 1)
                        nc.scalar.copy((q_t, k_t)[n // QT][:, n % QT, :], s_ps[n % HG][:, :]).then_inc(proj_act, 1)
                    act.wait_ge(proj_ready, (i + 1) * (2 * QT + 2))
                    nc.scalar.copy(v_sb[:, 2:4, :, 0:HD],
                                   t_ps[1][:, :].rearrange("p (j h d) -> p j h d", j=2, d=HD)).then_inc(proj_act, 1)
                    for m in range(UNITS):
                        exps(i, m)
                        if m >= 3 and BY_ACT[m - 3]:
                            empty(i, m - 3)
                        if m == NH + 8:
                            norm.act_std(i + 1)
                    for m in range(UNITS - 3, UNITS):
                        if BY_ACT[m]:
                            empty(i, m)

        @block.vector
        def _(dve):
            def tables():
                nc.vector.tensor_copy(mask_b[:, :], mask_f[:, :])
                nc.vector.tensor_copy(ident_b[:, :], core.ident[:, :])
                nc.vector.tensor_scalar(dist[:, :], dist[:, :], float(CLIP), -1.0, ALU.min, ALU.max)
                nc.vector.memset(factor[:, :], 0.0)
                nc.vector.drain()
                for n in range(-1, CLIP + 1):
                    value = 1.0 if n < 0 else rel_sb[:, n:n + 1]
                    nc.vector.tensor_scalar(hit[:, :], dist[:, :], float(n), value, ALU.is_equal, ALU.mult)
                    nc.vector.drain()
                    nc.vector.tensor_tensor(factor[:, :], factor[:, :], hit[:, :], ALU.add)
                    nc.vector.drain()
                nc.vector.tensor_scalar(factor[:, :], factor[:, :], SCALE, None, ALU.mult).then_inc(factor_ready, 1)
                nc.vector.drain()

            def group(i, m):
                t = m // NH
                width = (t + 1) * P
                side = (m // HG) % 2
                dve.wait_ge(qk_ready, i * UNITS + m + HG)
                dve.wait_ge(turned, i * UNITS + m + HG)
                dve.sem_inc(groups_begun, 1)
                for g in range(HG):
                    nc.vector.tensor_tensor_reduce(
                        out=prob[:, (m + g) % PR, 0:width], in0=s_ps[g][:, 0:width],
                        in1=factor[:, S - width:S], scale=1.0, scalar=-3.0e38, op0=ALU.mult, op1=ALU.max,
                        accum_out=top[:, side, g:g + 1]).then_inc(s_free, 1)
                nc.vector.drain()
                nc.vector.tensor_scalar(neg_top[:, side, :], top[:, side, :], -1.0, None,
                                        ALU.mult).then_inc(top_ready, 1)

            def empty(i, m):
                t = m // NH
                dve.wait_ge(turned, PR + i * UNITS + m + 1)
                dve.wait_ge(pv_done, i * UNITS + m + 1)
                nc.vector.tensor_copy(prob_t[:, m % TR, 0:(t + 1) * P],
                                      t_ps[m % TB][:, 0:(t + 1) * P]).then_inc(t_dve, 1)

            def divide(i, t):
                nc.vector.drain()
                dve.wait_ge(pv_done, TR + i * UNITS + (t + 1) * NH)
                nc.vector.reciprocal(inv[:, :, :], o_ps[:, :, HD:HD + 1])
                nc.vector.drain()
                nc.vector.tensor_tensor(ctx_sb[:, :].rearrange("p (h d) -> p h d", d=HD), o_ps[:, :, 0:HD],
                                        inv[:, :, :].broadcast_to([P, NH, HD]), ALU.mult).then_inc(ctx_ready, 1)

            def copy_ctx(i, t):
                dve.wait_ge(ctx_turned, i * TPB + t + 1)
                nc.vector.tensor_copy(ctx_t[:, :, :], misc[:, 0:D].rearrange("p (c q) -> p c q", q=P)).then_inc(ctx_copied, 1)

            def add_out(i, t):
                dve.wait_ge(out_ready, i * TPB + t + 1)
                xt = core.tile(i + 1, t)
                nc.vector.tensor_tensor(xt, misc[:, D:2 * D], xt, ALU.add).then_inc(out_added, 1)

            dve.sem_inc(s_free, HG)
            dve.wait_ge(loaded, LOADED)
            dve.wait_ge(consts, 2)
            tables()
            norm.dve_stats(0)
            norm.dve_normalise(0)
            norm.dve_copy_t(0, 0)
            with dve.Fori(0, B // 2) as pair:
                for k in range(2):
                    i = pair * 2 + k
                    nc.vector.drain()
                    for n in range(0, 2 * QT, 2):
                        dve.wait_ge(proj_ready, i * (2 * QT + 2) + n + 1)
                        nc.vector.tensor_copy((q_t, k_t)[n // QT][:, n % QT, :], s_ps[n % HG][:, :]).then_inc(proj_dve, 1)
                    dve.wait_ge(proj_ready, i * (2 * QT + 2) + 2 * QT + 1)
                    nc.vector.tensor_copy(v_sb[:, 0:2, :, 0:HD],
                                          t_ps[0][:, :].rearrange("p (j h d) -> p j h d", j=2, d=HD)).then_inc(proj_dve, 1)
                    group(i, 0)
                    for m in range(UNITS):
                        if m % HG == 0 and m + HG < UNITS:
                            group(i, m + HG)
                        if not BY_ACT[m]:
                            empty(i, m)
                        if m > NH and m % NH == 1:
                            divide(i, m // NH - 1)
                        if m > NH and m % NH == 5:
                            copy_ctx(i, m // NH - 1)
                        if m > NH and m % NH == 9:
                            add_out(i, m // NH - 1)
                        if m == NH + 6:
                            norm.dve_stats(i + 1)
                        if m == NH + 12:
                            norm.dve_normalise(i + 1)
                        if m == NH + 14:
                            norm.dve_copy_t(i + 1, 1 - k)
                    divide(i, TPB - 1)
                    copy_ctx(i, TPB - 1)
                    add_out(i, TPB - 1)



TOP = 3
CAP = 128


class Sparse:

    def __init__(self, core, ctx, experts):
        nc = core.nc
        self.rows_in = nc.dram_tensor("rows_in", (experts * CAP, D), FP32, kind="Internal").ap()
        self.rows_out = nc.dram_tensor("rows_out", (experts * CAP, D), FP32, kind="Internal").ap()


def clear_rows(core, rows, name):
    nc = core.nc
    with ExitStack() as ctx:
        zeros = ctx.enter_context(nc.sbuf_tensor(f"{name}_zero_rows", [P, 8, D], FP32))
        ready = core.semaphore(f"{name}_zero_rows_ready")
        cleared = core.semaphore(f"{name}_rows_cleared")
        block = ctx.enter_context(nc.Block())
        per = 8
        n = rows.shape[0] // (P * per)

        @block.vector
        def _(dve):
            nc.vector.memset(zeros[:, :, :], 0.0).then_inc(ready, 1)

        @block.sync
        def _(sp):
            sp.wait_ge(ready, 1)
            view = rows.rearrange("(n p r) d -> n p r d", p=P, r=per)
            for m in range(n):
                sp.dma_start(view[m], zeros[:, :, :]).then_inc(cleared, 16)
            sp.wait_ge(cleared, 16 * n)


def ffn0_phase(core, sparse, name, gate_w, gate_b, w1, b1, w2, b2):
    nc = core.nc
    E, H = w1.shape[0], w1.shape[2]
    HC = H // P
    R = 4
    NT = B * TPB
    NK = TPB * TOP
    ctx = ExitStack()
    with ctx:
        sb = lambda n, s, dt=FP32: ctx.enter_context(nc.sbuf_tensor(f"{name}_{n}", s, dt))
        sem = lambda n: core.semaphore(f"{name}_{n}")
        w1_sb = [sb(f"w1_{s}", [P, DC, H]) for s in range(R)]
        w2_sb = [sb(f"w2_{s}", [P, HC, D]) for s in range(R)]
        b2_sb = [sb(f"b2_{s}", [1, D]) for s in range(R)]
        best = sb("best", [P, B, TOP, TPB])
        valid = sb("valid", [P, B, TOP, TPB])
        place = sb("place", [P, B, TOP, TPB], U32)
        w_loaded = [sem(f"w_loaded{s}") for s in range(R)]

        def load_weights(sp, s, e):
            sp.dma_start(w1_sb[s][:, :, :], w1[e, :, :].rearrange("(c p) h -> p c h", p=P)).then_inc(w_loaded[s], 16)
            sp.dma_start(w2_sb[s][:, :, :], w2[e, :, :].rearrange("(c p) d -> p c d", p=P)).then_inc(w_loaded[s], 16)
            sp.dma_start(b2_sb[s][:, :], b2[bass.ds(e, 1), :]).then_inc(w_loaded[s], 16)

        route(core, sparse, name, gate_w, gate_b, E, best, valid, place, load_weights, R)
        experts(core, sparse, name, b1, E, H, R, w1_sb, w2_sb, b2_sb, w_loaded, load_weights)
        combine(core, sparse, name, best, valid, place)


def route(core, sparse, name, gate_w, gate_b, E, best, valid, place, load_weights, R):
    nc = core.nc
    NK = TPB * TOP
    ctx = ExitStack()
    with ctx:
        sb = lambda n, s, dt=FP32: ctx.enter_context(nc.sbuf_tensor(f"{name}_{n}", s, dt))
        ps = lambda n, s: ctx.enter_context(nc.psum_tensor(f"{name}_{n}", s, FP32))
        sem = lambda n: core.semaphore(f"{name}_{n}")
        norm = Norm(core, ctx, name, xn_buffers=2)
        gate_w_sb = sb("gate_w", [P, DC, E])
        gate_b_sb = sb("gate_b", [P, E])
        iota_e = sb("iota_e", [P, E])
        before_f = sb("before_f", [P, P])
        before = sb("before", [P, P], BF16)
        ones = sb("ones", [P, P], BF16)
        logits = sb("logits", [P, TPB, E])
        top_v = sb("top_v", [P, TPB, 8])
        top_i = sb("top_i", [P, TPB, 8], U32)
        expert = sb("expert", [P, TOP, TPB])
        pick = sb("pick", [P, TOP, TPB, E])
        some = sb("some", [P, TPB, E])
        mask = sb("mask", [P, TPB, E], BF16)
        carry = sb("carry", [P, TPB + 1, E], BF16)
        product = sb("product", [P, TOP, TPB, E])
        pos = sb("pos", [P, TOP, TPB])
        over = sb("over", [P, TOP, TPB])
        near = sb("near", [P, TOP, TPB])
        target = [sb(f"target{k}", [P, TOP, TPB], U32) for k in range(2)]
        logit_ps = ps("logit_ps", [P, 512])
        pos_ps = ps("pos_ps", [P, 512])

        loaded = sem("r_loaded")
        consts = sem("r_consts")
        logits_ready = sem("r_logits")
        mask_ready = sem("r_mask")
        pos_ready = sem("r_pos")
        pos_read = sem("r_pos_read")
        target_ready = sem("r_target")
        carried = sem("r_carried")
        scattered = [sem(f"r_scattered{k}") for k in range(2)]
        block = ctx.enter_context(nc.Block())
        LOADED = 16 * 2

        @block.sync
        def _(sp):
            sp.dma_start(gate_w_sb[:, :, :], gate_w.rearrange("(c p) e -> p c e", p=P)).then_inc(loaded, 16)
            sp.dma_start(gate_b_sb[:, :], gate_b.partition_broadcast(P)).then_inc(loaded, 16)
            for s in range(R):
                load_weights(sp, s, s)

        @block.gpsimd
        def _(pool):
            nc.gpsimd.iota(iota_e[:, :], pattern=[[1, E]], base=0, channel_multiplier=0,
                           allow_small_or_imprecise_dtypes=True)
            nc.gpsimd.memset(carry[:, :, :], 0.0)
            nc.gpsimd.memset(ones[:, :], 1.0)
            nc.gpsimd.memset(before_f[:, :], 1.0).then_inc(consts, 1)
            pool.wait_ge(consts, 1)
            nc.gpsimd.affine_select(out=before_f[:, :], in_=before_f[:, :], compare_op=ALU.is_gt, fill=0.0,
                                    base=0, pattern=[[1, P]], channel_multiplier=-1).then_inc(consts, 1)
            with pool.Fori(0, B // 2) as pair:
                for k in range(2):
                    i = pair * 2 + k
                    pool.wait_ge(target_ready, i + 1)
                    pool.sem_inc(carried, 1)
                    for r in range(TOP):
                        for j in range(TPB):
                            nc.gpsimd.indirect_dma_start(
                                out=sparse.rows_in, out_offset=bass.IndirectOffsetOnAxis(ap=target[k][:, r, j:j + 1], axis=0),
                                in_=norm.xns[k][:, j, :], in_offset=None, bounds_check=E * CAP - 1,
                                oob_is_err=False).then_inc(scattered[k], 16)
            for k in range(2):
                pool.wait_ge(scattered[k], 16 * NK * (B // 2))

        @block.tensor
        def _(pe):
            pe.wait_ge(loaded, LOADED)
            norm.pe_transpose(0, 0)
            with pe.Fori(0, B // 2) as pair:
                for k in range(2):
                    i = pair * 2 + k
                    norm.wait_xn_t(pe, i)
                    pe.wait_ge(mask_ready, i)
                    for j in range(TPB):
                        for c in range(DC):
                            last = nc.tensor.matmul(logit_ps[:, j * E:(j + 1) * E],
                                                    norm.xn_t[k][:, c, j * P:(j + 1) * P],
                                                    gate_w_sb[:, c, :], start=c == 0, stop=c == DC - 1)
                    last.then_inc(logits_ready, 1)
                    norm.pe_transpose(i + 1, 1 - k)
                    pe.wait_ge(mask_ready, i + 1)
                    pe.wait_ge(pos_read, i)
                    nc.tensor.matmul(pos_ps[:, 0:TPB * E], before[:, :], mask[:, :, :].rearrange("p j e -> p (j e)"),
                                     start=True, stop=False).then_inc(norm.free, 1)
                    nc.tensor.matmul(pos_ps[:, 0:TPB * E], ones[:, :], carry[:, 0:TPB, :].rearrange("p j e -> p (j e)"),
                                     start=False, stop=True).then_inc(pos_ready, 1)

        @block.scalar
        def _(act):
            norm.act_std(0)
            with act.Fori(0, B) as i:
                norm.act_std(i + 1)

        @block.vector
        def _(dve):
            dve.wait_ge(loaded, LOADED)
            dve.wait_ge(consts, 2)
            nc.vector.tensor_copy(before[:, :], before_f[:, :])
            norm.dve_stats(0)
            norm.dve_normalise(0, 0)
            norm.dve_copy_t(0, 0)
            with dve.Fori(0, B // 2) as pair:
                for k in range(2):
                    i = pair * 2 + k
                    nc.vector.drain()
                    norm.dve_stats(i + 1)
                    dve.wait_ge(logits_ready, i + 1)
                    nc.vector.tensor_tensor(logits[:, :, :], logit_ps[:, 0:TPB * E].rearrange("p (j e) -> p j e", e=E),
                                            gate_b_sb[:, :].unsqueeze(1).broadcast_to([P, TPB, E]), ALU.add)
                    nc.vector.drain()
                    for j in range(TPB):
                        nc.vector.max(top_v[:, j, :], logits[:, j, :])
                    nc.vector.drain()
                    for j in range(TPB):
                        nc.vector.max_index(top_i[:, j, :], top_v[:, j, :], logits[:, j, :])
                    nc.vector.tensor_copy(best[:, i, :, :], top_v[:, :, 0:TOP].rearrange("p j r -> p r j"))
                    nc.vector.drain()
                    nc.vector.tensor_copy(expert[:, :, :], top_i[:, :, 0:TOP].rearrange("p j r -> p r j"))
                    dve.wait_ge(scattered[1 - k], pair * (16 * NK) + (0 if k == 0 else 16 * NK))
                    norm.dve_normalise(i + 1, 1 - k)
                    nc.vector.drain()
                    nc.vector.tensor_tensor(pick[:, :, :, :],
                                            iota_e[:, :].unsqueeze(1).unsqueeze(1).broadcast_to([P, TOP, TPB, E]),
                                            expert[:, :, :].unsqueeze(3).broadcast_to([P, TOP, TPB, E]), ALU.is_equal)
                    nc.vector.tensor_copy(carry[:, 0, :], carry[:, TPB, :])
                    nc.vector.drain()
                    nc.vector.tensor_tensor(some[:, :, :], pick[:, 0, :, :], pick[:, 1, :, :], ALU.add)
                    nc.vector.drain()
                    nc.vector.tensor_tensor(mask[:, :, :], some[:, :, :], pick[:, 2, :, :], ALU.add)
                    for j in range(TPB):
                        nc.vector.drain()
                        last = nc.vector.tensor_tensor(carry[:, j + 1, :], carry[:, j, :], mask[:, j, :], ALU.add)
                    last.then_inc(mask_ready, 1)
                    norm.dve_copy_t(i + 1, 1 - k)
                    dve.wait_ge(pos_ready, i + 1)
                    nc.vector.tensor_tensor(
                        product[:, :, :, :], pick[:, :, :, :],
                        pos_ps[:, 0:TPB * E].rearrange("p (j e) -> p j e", e=E).unsqueeze(1).broadcast_to([P, TOP, TPB, E]),
                        ALU.mult).then_inc(pos_read, 1)
                    nc.vector.drain()
                    nc.vector.tensor_reduce(pos[:, :, :], product[:, :, :, :], AX.X, ALU.add)
                    nc.vector.drain()
                    nc.vector.tensor_scalar(valid[:, i, :, :], pos[:, :, :], float(CAP), None, ALU.is_lt)
                    nc.vector.tensor_scalar(over[:, :, :], pos[:, :, :], float(CAP), float(2 * E * CAP), ALU.is_ge, ALU.mult)
                    nc.vector.tensor_scalar(near[:, :, :], pos[:, :, :], float(CAP - 1), None, ALU.min)
                    nc.vector.tensor_scalar(expert[:, :, :], expert[:, :, :], float(CAP), None, ALU.mult)
                    nc.vector.drain()
                    nc.vector.tensor_tensor(place[:, i, :, :], expert[:, :, :], near[:, :, :], ALU.add)
                    nc.vector.tensor_tensor(over[:, :, :], over[:, :, :], pos[:, :, :], ALU.add)
                    nc.vector.drain()
                    nc.vector.tensor_tensor(target[k][:, :, :], over[:, :, :], expert[:, :, :], ALU.add).then_inc(target_ready, 1)


def experts(core, sparse, name, b1, E, H, R, w1_sb, w2_sb, b2_sb, w_loaded, load_weights):
    nc = core.nc
    HC = H // P
    HB = 2
    ctx = ExitStack()
    with ctx:
        sb = lambda n, s, dt=FP32: ctx.enter_context(nc.sbuf_tensor(f"{name}_{n}", s, dt))
        ps = lambda n, s: ctx.enter_context(nc.psum_tensor(f"{name}_{n}", s, FP32))
        sem = lambda n: core.semaphore(f"{name}_{n}")
        ones = sb("e_ones", [1, P])
        b1_rows = sb("b1_rows", [E, H])
        b1_t = sb("b1_t", [P, HC, E])
        b1_e = [sb(f"b1_e{k}", [P, HC]) for k in range(2)]
        rows = [sb(f"rows{s}", [P, D]) for s in range(R)]
        rows_t = [sb(f"rows_t{k}", [P, DC, P]) for k in range(2)]
        h_t = [sb(f"h_t{k}", [P, HC, P]) for k in range(2)]
        y_sb = [sb(f"y{k}", [P, D]) for k in range(2)]
        t_ps = ps("t_ps", [P, 512])
        h_ps = [ps(f"h_ps{n}", [P, 512]) for n in range(HC // HB)]
        y_ps = [ps(f"y_ps{k}", [P, 512]) for k in range(2)]

        b1_loaded = sem("b1_loaded")
        consts = sem("e_consts")
        b1_turned = sem("b1_turned")
        b1_copied = sem("b1_copied")
        b1_ready = sem("b1_ready")
        x_loaded = [sem(f"x_loaded{s}") for s in range(R)]
        x_turned = sem("x_turned")
        x_copied = sem("x_copied")
        h_ready = sem("h_ready")
        gelu_done = sem("gelu_done")
        y_ready = sem("e_y_ready")
        y_copied = sem("y_copied")
        carried = sem("e_carried")
        y_stored = [sem(f"y_stored{k}") for k in range(2)]
        block = ctx.enter_context(nc.Block())

        @block.sync
        def _(sp):
            def load_rows(s, e):
                sp.dma_start(rows[s][:, :], sparse.rows_in[bass.ds(e * CAP, CAP), :]).then_inc(x_loaded[s], 16)
            sp.sem_inc(y_ready, R)
            sp.dma_start(b1_rows[:, :], b1).then_inc(b1_loaded, 16)
            for s in range(R):
                load_rows(s, s)
            with sp.Fori(1, E // R) as turn:
                for s in range(R):
                    e = turn * R + s
                    sp.wait_ge(y_ready, e + 1)
                    load_weights(sp, s, e)
                    load_rows(s, e)

        @block.gpsimd
        def _(pool):
            nc.gpsimd.memset(ones[:, :], 1.0).then_inc(consts, 1)
            with pool.Fori(0, E // 2) as pair:
                for k in range(2):
                    e = pair * 2 + k
                    pool.wait_ge(y_copied, e + 1)
                    pool.sem_inc(carried, 1)
                    pool.dma_start(sparse.rows_out[bass.ds(e * CAP, CAP), :], y_sb[k][:, :]).then_inc(y_stored[k], 16)
            for k in range(2):
                pool.wait_ge(y_stored[k], 16 * (E // 2))

        @block.tensor
        def _(pe):
            def turn_rows(turn, s):
                e = turn * R + s
                pe.wait_ge(x_loaded[s], (turn + 1) * 16)
                if due(e):
                    pe.wait_ge(x_copied, e)
                for c in range(DC):
                    last = nc.tensor.transpose(t_ps[:, c * P:(c + 1) * P], rows[s][:, c * P:(c + 1) * P],
                                               core.ident[:, :])
                last.then_inc(x_turned, 1)

            def up(turn, s):
                e, k = turn * R + s, s % 2
                pe.wait_ge(w_loaded[s], (turn + 1) * 48)
                pe.wait_ge(x_copied, e + 1)
                for n in range(HC):
                    if n % HB == 0:
                        pe.wait_ge(gelu_done, e * HC + n + HB)
                    for c in range(DC):
                        last = nc.tensor.matmul(h_ps[n // HB][:, (n % HB) * P:(n % HB + 1) * P], w1_sb[s][:, c, n * P:(n + 1) * P],
                                                rows_t[k][:, c, :], start=c == 0, stop=c == DC - 1)
                    if n % HB == HB - 1:
                        last.then_inc(h_ready, 1)

            def down(turn, s):
                e, k = turn * R + s, s % 2
                if due(e - 1):
                    pe.wait_ge(y_copied, e - 1)
                nc.tensor.matmul(y_ps[k][:, 0:D], ones[:, :], b2_sb[s][:, :], start=True, stop=False)
                for n in range(HC):
                    pe.wait_ge(gelu_done, HC + e * HC + n + 1)
                    last = nc.tensor.matmul(y_ps[k][:, 0:D], h_t[k][:, n, :], w2_sb[s][:, n, :],
                                            start=False, stop=n == HC - 1)
                last.then_inc(y_ready, 1)

            pe.wait_ge(consts, 1)
            pe.wait_ge(b1_loaded, 16)
            for n in range(HC):
                last = nc.tensor.transpose(h_ps[0][:, n * E:(n + 1) * E],
                                           b1_rows[:, n * P:(n + 1) * P], core.ident[0:E, 0:E])
            last.then_inc(b1_turned, 1)
            pe.wait_ge(b1_copied, 1)
            turn_rows(0, 0)
            for s in range(R):
                up(0, s)
                turn_rows((s + 1) // R, (s + 1) % R)
                down(0, s)
            with pe.Fori(1, E // R - 1) as turn:
                for s in range(R):
                    up(turn, s)
                    turn_rows(turn + (s + 1) // R, (s + 1) % R)
                    down(turn, s)
            for s in range(R):
                up(E // R - 1, s)
                if s + 1 < R:
                    turn_rows(E // R - 1, s + 1)
                down(E // R - 1, s)

        @block.scalar
        def _(act):
            act.sem_inc(gelu_done, HC)
            with act.Fori(0, E // 2) as pair:
                for k in range(2):
                    e = pair * 2 + k
                    act.wait_ge(b1_ready, e + 1)
                    act.wait_ge(y_ready, e + R - 1)
                    for n in range(HC):
                        if n % HB == 0:
                            act.wait_ge(h_ready, e * (HC // HB) + n // HB + 1)
                        nc.scalar.activation(h_t[k][:, n, :], h_ps[n // HB][:, (n % HB) * P:(n % HB + 1) * P], ACT.Gelu,
                                             bias=b1_e[k][:, n:n + 1]).then_inc(gelu_done, 1)

        @block.vector
        def _(dve):
            dve.wait_ge(b1_turned, 1)
            nc.vector.tensor_copy(b1_t[:, :, :], h_ps[0][:, :].rearrange("p (n e) -> p n e", e=E)).then_inc(b1_copied, 1)
            nc.vector.drain()
            def prepare(e, k):
                dve.wait_ge(gelu_done, HC + e * HC)
                nc.vector.tensor_copy(b1_e[k][:, :], b1_t[:, :, e]).then_inc(b1_ready, 1)
                dve.wait_ge(x_turned, e + 1)
                nc.vector.tensor_copy(rows_t[k][:, :, :],
                                      t_ps[:, 0:D].rearrange("p (c q) -> p c q", q=P)).then_inc(x_copied, 1)

            def finish(e, k, stored):
                dve.wait_ge(y_ready, R + e + 1)
                dve.wait_ge(y_stored[k], stored)
                nc.vector.tensor_copy(y_sb[k][:, :], y_ps[k][:, 0:D]).then_inc(y_copied, 1)

            prepare(0, 0)
            with dve.Fori(0, E // 2 - 1) as pair:
                for k in range(2):
                    prepare(pair * 2 + k + 1, 1 - k)
                    finish(pair * 2 + k, k, pair * 16)
            prepare(E - 1, 1)
            for k in range(2):
                finish(E - 2 + k, k, (E // 2 - 1) * 16)


def combine(core, sparse, name, best, valid, place):
    nc = core.nc
    NK = TPB * TOP
    ctx = ExitStack()
    with ctx:
        sb = lambda n, s, dt=FP32: ctx.enter_context(nc.sbuf_tensor(f"{name}_{n}", s, dt))
        sem = lambda n: core.semaphore(f"{name}_{n}")
        shifted = sb("shifted", [P, B, TOP, TPB])
        total = sb("total", [P, B, 1, TPB])
        index = [sb(f"index{k}", [P, NK], U32) for k in range(2)]
        gate = [sb(f"gate{k}", [P, NK]) for k in range(2)]
        back = [sb(f"back{k}", [P, NK, D]) for k in range(2)]
        shift_ready = sem("c_shift")
        exp_ready = sem("c_exp")
        index_ready = sem("c_index")
        carried = sem("c_carried")
        gathered = [sem(f"c_gathered{k}") for k in range(2)]
        used = sem("c_used")
        block = ctx.enter_context(nc.Block())

        @block.scalar
        def _(act):
            act.wait_ge(shift_ready, 1)
            nc.scalar.activation(shifted[:, :, :, :], shifted[:, :, :, :], ACT.Exp).then_inc(exp_ready, 1)

        @block.gpsimd
        def _(pool):
            with pool.Fori(0, B // 2) as pair:
                for k in range(2):
                    i = pair * 2 + k
                    pool.wait_ge(index_ready, i + 1)
                    pool.sem_inc(carried, 1)
                    for n in range(NK):
                        nc.gpsimd.indirect_dma_start(
                            out=back[k][:, n, :], out_offset=None, in_=sparse.rows_out,
                            in_offset=bass.IndirectOffsetOnAxis(ap=index[k][:, n:n + 1], axis=0),
                            bounds_check=sparse.rows_out.shape[0] - 1, oob_is_err=False).then_inc(gathered[k], 16)

        @block.vector
        def _(dve):
            def fetch(i, k):
                nc.vector.drain()
                nc.vector.tensor_copy(gate[k][:, :], shifted[:, i, :, :].rearrange("p r j -> p (r j)"))
                nc.vector.tensor_copy(index[k][:, :], place[:, i, :, :].rearrange("p r j -> p (r j)")).then_inc(index_ready, 1)

            def use(i, k, count):
                nc.vector.drain()
                dve.wait_ge(gathered[k], count)
                for r in range(TOP):
                    if r:
                        nc.vector.drain()
                    for j in range(TPB):
                        xt = core.tile(i + 1, j)
                        nc.vector.scalar_tensor_tensor(out=xt, in0=back[k][:, r * TPB + j, :],
                                                       scalar=gate[k][:, r * TPB + j:r * TPB + j + 1], in1=xt,
                                                       op0=ALU.mult, op1=ALU.add)

            nc.vector.tensor_tensor(shifted[:, :, :, :], best[:, :, :, :],
                                    best[:, :, 0:1, :].broadcast_to([P, B, TOP, TPB]), ALU.subtract).then_inc(shift_ready, 1)
            dve.wait_ge(exp_ready, 1)
            nc.vector.tensor_tensor(total[:, :, :, :], shifted[:, :, 0:1, :], shifted[:, :, 1:2, :], ALU.add)
            nc.vector.drain()
            nc.vector.tensor_tensor(total[:, :, :, :], total[:, :, :, :], shifted[:, :, 2:3, :], ALU.add)
            nc.vector.drain()
            nc.vector.reciprocal(total[:, :, :, :], total[:, :, :, :])
            nc.vector.drain()
            nc.vector.tensor_tensor(shifted[:, :, :, :], shifted[:, :, :, :],
                                    total[:, :, :, :].broadcast_to([P, B, TOP, TPB]), ALU.mult)
            nc.vector.drain()
            nc.vector.scalar_tensor_tensor(
                out=shifted[:, :, :, :].rearrange("p b r j -> p (b r j)"),
                in0=shifted[:, :, :, :].rearrange("p b r j -> p (b r j)"), scalar=0.5,
                in1=valid[:, :, :, :].rearrange("p b r j -> p (b r j)"), op0=ALU.mult, op1=ALU.mult)
            for k in range(2):
                fetch(k, k)
            with dve.Fori(0, B // 2 - 1) as pair:
                for k in range(2):
                    i = pair * 2 + k
                    use(i, k, (pair + 1) * (16 * NK))
                    fetch(i + 2, k)
            for k in range(2):
                use(B - 2 + k, k, (B // 2) * (16 * NK))



WIN = 32


def attn0_phase(core, name, skew_dram, w_disp, b_disp, w_val, b_val, rel_pos, w_state, b_state, w_strain,
                b_strain, w_state_i, w_state_j, w_pos, w_bond, b_bond, w_damage, b_damage,
                w_damage_out, b_damage_out, w_cproj, b_cproj):
    nc = core.nc
    BD = w_state.shape[0]
    NH = D // BD
    HH = P // BD
    HALF = NH // HH
    PAD = WIN
    DG = 4
    NQ = WIN // DG
    STEPS = HALF * NQ
    SPAN = 2 * WIN
    NBLK = S // WIN
    BPT = P // WIN
    HP = NH // 2
    ctx = ExitStack()
    with ctx:
        sb = lambda n, s, dt=FP32: ctx.enter_context(nc.sbuf_tensor(f"{name}_{n}", s, dt))
        ps = lambda n, s: ctx.enter_context(nc.psum_tensor(f"{name}_{n}", s, FP32))
        sem = lambda n: core.semaphore(f"{name}_{n}")
        norm = Norm(core, ctx, name, pad=PAD)
        w_disp_sb = sb("w_disp", [P, DC, D])
        w_val_sb = sb("w_val", [P, DC, HP, 2, BD])
        w_out_sb = sb("w_out", [P, DC, D])
        b_out_sb = sb("b_out", [1, D])
        ones = sb("ones", [1, P])
        b_disp_sb = sb("b_disp", [P, HALF])
        b_val_sb = sb("b_val", [P, HP, 2, BD])
        bond_b = sb("bond_b", [P, 1])
        damage_b = sb("damage_b", [P, 1])
        STATE, STRAIN, STATE_I, STATE_J, DAMAGE = range(5)
        COLS = 5 * BD
        SM = COLS + 5 + WIN
        small = sb("small", [BD, SM])
        rel_t = sb("rel_t", [BD, WIN])
        w_pos_sb = sb("w_pos", [BD, BD])
        select = sb("select", [BD, HH, BD])
        small_rep = sb("small_rep", [P, SM])
        diag = sb("diag", [P, HH, BD])
        mats = [sb(f"mat{n}", [P, HH, BD]) for n in range(5)]
        neg_strain = sb("neg_strain", [P, HH, BD])
        col_bond = sb("col_bond", [P, HH])
        col_damage = sb("col_damage", [P, HH])
        inv_count = sb("inv_count", [P, S])
        early = sb("early", [P, WIN])
        disp = [sb(f"disp{h}", [P, S]) for h in range(HALF)]
        sum_a = sb("sum_a", [P, PAD + S])
        sum_b = sb("sum_b", [P, PAD + S])
        u_less_b = sb("u_less_b", [P, S])
        state = [sb(f"state{h}", [P, S]) for h in range(HALF)]
        a_sb = [[sb(f"a{k}{h}", [P, PAD + S]) for h in range(HALF)] for k in range(2)]
        c_sb = [[sb(f"c{k}{h}", [P, PAD + S]) for h in range(HALF)] for k in range(2)]
        q_sb = [[sb(f"q{k}{h}", [P, S]) for h in range(HALF)] for k in range(2)]
        f_sb = [[sb(f"f{k}{h}", [P, S]) for h in range(HALF)] for k in range(2)]
        bond_buf = [sb(f"bond_buf{k}", [P, DG, S]) for k in range(2)]
        dmg_buf = [sb(f"dmg_buf{k}", [P, DG, S]) for k in range(2)]
        bond = sb("bond", [P, TPB, NH, WIN])
        dmg = sb("dmg", [P, TPB, NH, WIN])
        top = sb("top", [P, TPB * NH, 1])
        expd = dmg
        inv_sum = [sb(f"inv_sum{k}", [P, TPB, NH]) for k in range(2)]
        skewed = sb("skewed", [P, TPB, NH * SPAN])
        turned = sb("turned", [P, HP, P])
        vals = sb("vals", [P, NBLK, HP, 2, BD])
        ctx_sb = sb("ctx", [P, D])
        ctx_t = sb("ctx_t", [P, DC, P])
        bond_ps = [ps(f"bond_ps{n}", [P, 2, HH, WIN]) for n in range(2)]
        dmg_ps = [ps(f"dmg_ps{n}", [P, 2, HH, WIN]) for n in range(2)]
        t_ps = ps("t_ps", [P, 512])
        o_ps = ps("o_ps", [P, 512])
        misc = ps("misc", [P, 512])
        pj = norm.tp

        loaded = sem("loaded")
        rel_loaded = sem("rel_loaded")
        zeroed = sem("zeroed")
        consts = sem("consts")
        tables_a = sem("tables_a")
        tables_b = sem("tables_b")
        tables = sem("tables")
        bond_pre = sem("bond_pre")
        dmg_pre = sem("dmg_pre")
        gelu_done = sem("gelu_done")
        chunk_used = sem("chunk_used")
        half_read = sem("half_read")
        sig_done = sem("sig_done")
        soft_ready = sem("soft_ready")
        exp_done = sem("exp_done")
        skew_stored = sem("skew_stored")
        skew_loaded = sem("skew_loaded")
        w_turned = sem("w_turned")
        w_copied = sem("w_copied")
        out_ready = sem("out_ready")
        ctx_ready = sem("ctx_ready")
        ctx_turned = sem("ctx_turned")
        ctx_copied = sem("ctx_copied")
        proj_ready = sem("proj_ready")
        proj_added = sem("proj_added")
        pj_ready = sem("pj_ready")
        pj_copied = sem("pj_copied")
        state_ready = sem("state_ready")
        val_ready = sem("val_ready")
        val_copied = sem("val_copied")
        block = ctx.enter_context(nc.Block())

        PJ = [(what, h) for what in ("disp", "u", "a", "q", "c") for h in range(HALF)]
        PJ_STEP = 4
        NPJ = len(PJ)
        VAL_STEP = 12
        T_STEP = 8

        def window(x, d):
            first = x[:, d + 1:d + 1 + S]
            return bass.AP(tensor=first.tensor, offset=first.offset, ap=[first.ap[0], [1, DG], [1, S]])

        @block.sync
        def _(sp):
            def load(dst, src, **kind):
                sp.dma_start(dst, src, **kind).then_inc(loaded, 16)
            load(w_disp_sb[:, :, :], w_disp.rearrange("(c p) n -> p c n", p=P))
            load(w_val_sb[:, :, :, :, :].rearrange("p c h r d -> p c (h r d)"), w_val.rearrange("(c p) n -> p c n", p=P))
            load(w_out_sb[:, :, :], w_cproj.rearrange("(c p) n -> p c n", p=P))
            load(b_out_sb[:, :], b_cproj.rearrange("(o n) -> o n", o=1))
            load(b_disp_sb[:, :], b_disp.rearrange("(h p) -> p h", p=P), allow_slow_non_contiguous=True)
            load(b_val_sb[:, :, :, :].rearrange("p h r d -> p (h r d)"), b_val.partition_broadcast(P))
            load(bond_b[:, :], b_bond.partition_broadcast(P))
            load(damage_b[:, :], b_damage_out.partition_broadcast(P))
            for n, w in enumerate((w_state, w_strain, w_state_i, w_state_j, w_damage)):
                load(small[:, n * BD:(n + 1) * BD], w)
            load(small[:, COLS:COLS + 1], w_bond)
            load(small[:, COLS + 1:COLS + 2], w_damage_out)
            for n, b in enumerate((b_state, b_strain, b_damage)):
                load(small[:, COLS + 2 + n:COLS + 3 + n], b.rearrange("(d o) -> d o", o=1))
            sp.dma_start(rel_t[:, :], rel_pos.rearrange("w d -> d w"),
                         allow_slow_non_contiguous=True).then_inc(rel_loaded, 16)
            sp.dma_start(w_pos_sb[:, :], w_pos).then_inc(rel_loaded, 16)

            def skew_weights(j):
                sp.wait_ge(exp_done, j + 1)
                for a in range(BPT):
                    row = TPB * NH * SPAN
                    rows = bass.AP(tensor=skew_dram.tensor, offset=a * WIN * row + 1,
                                   ap=[[row + 1, WIN], [SPAN, TPB * NH], [1, WIN]])
                    sp.dma_start(rows, expd[a * WIN:(a + 1) * WIN, :, :, :].rearrange(
                        "p j h w -> p (j h) w")).then_inc(skew_stored, 16)
                sp.wait_ge(skew_stored, (j + 1) * 16 * BPT)
                sp.wait_ge(w_turned, j * 2 * TPB)
                sp.dma_start(skewed[:, :, :].rearrange("p j s -> p (j s)"), skew_dram).then_inc(skew_loaded, 16)

            with sp.Fori(0, B + 1) as j:
                skew_weights(j)

        LOADED = 16 * 18

        @block.gpsimd
        def _(pool):
            for k in range(2):
                nc.gpsimd.memset(norm.xn_t[k][:, :, 0:PAD], 0.0)
                nc.gpsimd.memset(inv_sum[k][:, :, :], 0.0)
                for h in range(HALF):
                    nc.gpsimd.memset(a_sb[k][h][:, 0:PAD], 0.0)
                    nc.gpsimd.memset(c_sb[k][h][:, 0:PAD], 0.0)
            nc.gpsimd.memset(vals[:, :, :, :, :], 0.0)
            nc.gpsimd.memset(sum_a[:, :], 0.0)
            nc.gpsimd.memset(sum_b[:, :], 0.0)
            nc.gpsimd.memset(bond[:, :, :, :], 0.0)
            nc.gpsimd.memset(dmg[:, :, :, :], 0.0)
            nc.gpsimd.memset(ones[:, :], 1.0)
            nc.gpsimd.memset(early[:, :], 0.0)
            nc.gpsimd.memset(diag[:, :, :], 1.0)
            nc.gpsimd.iota(inv_count[:, :], pattern=[[1, S]], base=1, channel_multiplier=0,
                           allow_small_or_imprecise_dtypes=True).then_inc(consts, 1)
            pool.wait_ge(consts, 1)
            nc.gpsimd.affine_select(out=early[:, :], in_=early[:, :], compare_op=ALU.is_ge, fill=MASKED,
                                    base=-(WIN - 1), pattern=[[1, WIN]], channel_multiplier=1)
            nc.gpsimd.affine_select(out=diag[:, :, :], in_=diag[:, :, :], compare_op=ALU.is_ge, fill=0.0,
                                    base=0, pattern=[[-BD, HH], [0, BD]], channel_multiplier=1).then_inc(consts, 1)
            pool.wait_ge(consts, 2)
            nc.gpsimd.affine_select(out=diag[:, :, :], in_=diag[:, :, :], compare_op=ALU.is_ge, fill=0.0,
                                    base=BD - 1, pattern=[[BD, HH], [0, BD]], channel_multiplier=-1).then_inc(consts, 1)
            with pool.Fori(0, B // 2) as pair:
                for k in range(2):
                    i = pair * 2 + k
                    pool.wait_ge(pj_copied, (i + 1) * NPJ)
                    for q in range(STEPS):
                        h, dg = divmod(q, NQ)
                        pool.wait_ge(chunk_used, i * 2 * STEPS + 2 * q + 2)
                        d = dg * DG
                        nc.gpsimd.tensor_tensor(dmg_buf[q % 2][:, :, :], window(c_sb[k][h], d),
                                                f_sb[k][h][:, :].unsqueeze(1).broadcast_to([P, DG, S]),
                                                ALU.add).then_inc(dmg_pre, 1)

        @block.tensor
        def _(pe):
            def chunk(i, k, q, kind):
                h, dg = divmod(q, NQ)
                buf, banks, col = ((bond_buf, bond_ps, col_bond), (dmg_buf, dmg_ps, col_damage))[kind]
                if dg == 0:
                    pe.wait_ge(half_read, i * HALF + h + 1)
                pe.wait_ge(gelu_done, i * 2 * STEPS + 2 * q + kind + 1)
                for dd in range(DG):
                    for j in range(TPB):
                        last = nc.tensor.matmul(banks[j // 2][:, j % 2, :, dg * DG + dd],
                                                buf[q % 2][:, dd, j * P:(j + 1) * P], col[:, :],
                                                start=True, stop=True)
                last.then_inc(chunk_used, 1)

            def product(i, k, n):
                what, h = PJ[n]
                if due(i * NPJ + n):
                    pe.wait_ge(pj_copied, i * NPJ + n)
                mm = lambda w, x, first, end: nc.tensor.matmul(pj[:, :], w, x, start=first, stop=end)
                flat = lambda m: m[:, :, :].rearrange("p h d -> p (h d)")
                if what == "disp":
                    norm.wait_xn_t(pe, i)
                    for c in range(DC):
                        last = mm(w_disp_sb[:, c, h * P:(h + 1) * P], norm.xn_t[k][:, c, PAD:], c == 0, c == DC - 1)
                elif what == "u":
                    last = mm(flat(mats[STATE]), disp[h][:, :], True, True)
                elif what == "a":
                    pe.wait_ge(state_ready, i * HALF + h + 1)
                    mm(flat(mats[STRAIN]), disp[h][:, :], True, False)
                    last = mm(flat(mats[STATE_J]), state[h][:, :], False, True)
                elif what == "q":
                    mm(flat(neg_strain), disp[h][:, :], True, False)
                    last = mm(flat(mats[STATE_I]), state[h][:, :], False, True)
                else:
                    last = mm(flat(mats[DAMAGE]), disp[h][:, :], True, True)
                last.then_inc(pj_ready, 1)

            def values(i, k, n):
                pe.wait_ge(val_copied, (i * 4 + n) * 2)
                for a in range(4):
                    at = (4 * n + a) * WIN
                    for r in range(2):
                        for c in range(DC):
                            last = nc.tensor.matmul(t_ps[r * SPAN:(r + 1) * SPAN, a * P:(a + 1) * P],
                                                    norm.xn_t[k][:, c, at:at + SPAN], w_val_sb[:, c, :, r, :],
                                                    start=c == 0, stop=c == DC - 1)
                last.then_inc(val_ready, 1)

            def turn(j, x):
                if x == 0:
                    pe.wait_ge(skew_loaded, (j + 1) * 16)
                    pe.wait_ge(val_copied, j * 8)
                for half in range(2):
                    pe.wait_ge(w_copied, (j * TPB + x) * 2 + half)
                    for n in range(4):
                        hp = half * 4 + n
                        last = nc.tensor.transpose(t_ps[:, n * P:(n + 1) * P],
                                                   skewed[:, x, hp * P:(hp + 1) * P], core.ident[:, :])
                    last.then_inc(w_turned, 1)

            def sums(j, x):
                pe.wait_ge(w_copied, (j * TPB + x + 1) * 2)
                pe.wait_ge(ctx_ready, j * TPB + x)
                for hp in range(HP):
                    for a in range(BPT):
                        last = nc.tensor.matmul(o_ps[a * WIN:(a + 1) * WIN, hp * 2 * BD:(hp + 1) * 2 * BD],
                                                turned[:, hp, a * WIN:(a + 1) * WIN],
                                                vals[:, x * BPT + a, hp, :, :].rearrange("p r d -> p (r d)"),
                                                start=True, stop=True)
                last.then_inc(out_ready, 1)

            def turn_ctx(j, x):
                pe.wait_ge(ctx_ready, j * TPB + x + 1)
                pe.wait_ge(proj_added, j * TPB + x)
                for c in range(DC):
                    last = nc.tensor.transpose(misc[:, c * P:(c + 1) * P], ctx_sb[:, c * P:(c + 1) * P], core.ident[:, :])
                last.then_inc(ctx_turned, 1)

            def project(j, x):
                pe.wait_ge(ctx_copied, j * TPB + x + 1)
                for c in range(DC):
                    nc.tensor.matmul(misc[:, D:2 * D], ctx_t[:, c, :], w_out_sb[:, c, :], start=c == 0, stop=False)
                nc.tensor.matmul(misc[:, D:2 * D], ones[:, :], b_out_sb[:, :], start=False, stop=True).then_inc(proj_ready, 1)

            def finish_step(j, q):
                x = q - T_STEP
                if 0 <= x - 1 < TPB:
                    sums(j, x - 1)
                if 0 <= x < TPB:
                    turn(j, x)
                if 0 <= x - 3 < TPB:
                    project(j, x - 3)
                if 0 <= x - 2 < TPB:
                    turn_ctx(j, x - 2)

            def prepare_step(i, k, q):
                if q == 3:
                    if due(i * NPJ):
                        pe.wait_ge(pj_copied, i * NPJ)
                    norm.pe_transpose(i)
                if 0 <= q - PJ_STEP < NPJ:
                    product(i, k, q - PJ_STEP)

            pe.wait_ge(tables_a, 1)
            nc.tensor.matmul(pj[0:BD, 0:WIN], w_pos_sb[:, :], rel_t[:, :], start=True, stop=True).then_inc(pj_ready, 1)
            pe.wait_ge(tables_b, 1)
            nc.tensor.matmul(misc[:, 0:SM], select[:, :, :].rearrange("k h d -> k (h d)"), small[:, :],
                             start=True, stop=True).then_inc(proj_ready, 1)
            pe.wait_ge(tables, 1)
            for q in range(STEPS):
                prepare_step(0, 0, q)
            with pe.Fori(0, B // 2) as pair:
                for k in range(2):
                    i = pair * 2 + k
                    for q in range(STEPS):
                        finish_step(i, q)
                        prepare_step(i + 1, 1 - k, q)
                        if q >= VAL_STEP:
                            values(i, k, q - VAL_STEP)
                        chunk(i, k, q, 0)
                        chunk(i, k, q, 1)
            for q in range(STEPS):
                finish_step(B, q)

        @block.scalar
        def _(act):
            def gelu(i, q, kind):
                act.wait_ge((bond_pre, dmg_pre)[kind], i * STEPS + q + 1)
                buf = (bond_buf, dmg_buf)[kind][q % 2]
                nc.scalar.activation(buf[:, :, :], buf[:, :, :], ACT.Gelu).then_inc(gelu_done, 1)

            def sigmoid(j):
                act.wait_ge(half_read, j * HALF + 1)
                nc.scalar.activation(dmg[:, :, :, :], dmg[:, :, :, :], ACT.Sigmoid).then_inc(sig_done, 1)

            def exps(j):
                act.wait_ge(soft_ready, j + 1)
                act.wait_ge(skew_stored, j * 16 * BPT)
                nc.scalar.activation(expd[:, :, :, :], bond[:, :, :, :], ACT.Exp).then_inc(exp_done, 1)

            norm.act_std(0)
            with act.Fori(0, B) as i:
                for q in range(STEPS):
                    gelu(i, q, 0)
                    gelu(i, q, 1)
                    if q == 0:
                        norm.act_std(i + 1)
                    if q == 1:
                        sigmoid(i)
                    if q == 5:
                        exps(i)
            sigmoid(B)
            exps(B)

        @block.vector
        def _(dve):
            def read_half(j, h):
                if h == 0:
                    dve.wait_ge(skew_stored, j * 16 * BPT)
                    dve.wait_ge(chunk_used, 4 + j * 2 * STEPS - STEPS)
                else:
                    dve.wait_ge(chunk_used, 4 + j * 2 * STEPS)
                for banks, dst, b in ((bond_ps, bond, bond_b), (dmg_ps, dmg, damage_b)):
                    for n in range(2):
                        last = nc.vector.tensor_scalar(dst[:, 2 * n:2 * n + 2, h * HH:(h + 1) * HH, :],
                                                       banks[n][:, :, :, :], b[:, 0:1], None, ALU.add)
                last.then_inc(half_read, 1)

            def combine_logits(j):
                dve.wait_ge(sig_done, j + 1)
                nc.vector.scalar_tensor_tensor(out=flat(bond), in0=flat(dmg), scalar=-10.0, in1=flat(bond),
                                               op0=ALU.mult, op1=ALU.add)
                nc.vector.drain()
                nc.vector.tensor_tensor(bond[:, 0, :, :], bond[:, 0, :, :],
                                        early[:, :].unsqueeze(1).broadcast_to([P, NH, WIN]), ALU.add)

            def less_top(j):
                rows = bond[:, :, :, :].rearrange("p j h w -> p (j h) w")
                nc.vector.drain()
                nc.vector.tensor_reduce(top[:, :, 0], rows, AX.X, ALU.max)
                nc.vector.drain()
                nc.vector.tensor_tensor(rows, rows, top[:, :, :].broadcast_to([P, TPB * NH, WIN]),
                                        ALU.subtract).then_inc(soft_ready, 1)

            def inverse_sums(j, k):
                nc.vector.drain()
                dve.wait_ge(exp_done, j + 1)
                nc.vector.tensor_reduce(inv_sum[k][:, :, :].rearrange("p j h -> p (j h)"),
                                        expd[:, :, :, :].rearrange("p j h w -> p (j h) w"), AX.X, ALU.add)
                nc.vector.drain()
                nc.vector.reciprocal(inv_sum[k][:, :, :], inv_sum[k][:, :, :])

            def flat(x):
                return x[:, :, :, :].rearrange("p j h w -> p (j h w)")

            def finish_step(j, k, q):
                if q == 1:
                    read_half(j, 1)
                if q == 3:
                    combine_logits(j)
                if q == 4:
                    less_top(j)
                if q == 7:
                    inverse_sums(j, k)
                x = q - T_STEP
                if 0 <= x < TPB:
                    for half in range(2):
                        dve.wait_ge(w_turned, (j * TPB + x) * 2 + half + 1)
                        if half == 0:
                            dve.wait_ge(out_ready, j * TPB + x)
                        nc.vector.tensor_copy(turned[:, half * 4:half * 4 + 4, :],
                                              t_ps[:, :].rearrange("p (n t) -> p n t", t=P)).then_inc(w_copied, 1)
                if 0 <= x - 3 < TPB:
                    dve.wait_ge(proj_ready, 1 + j * TPB + x - 2)
                    xt = core.tile(j, x - 3)
                    nc.vector.tensor_tensor(xt, misc[:, D:2 * D], xt, ALU.add).then_inc(proj_added, 1)
                if 0 <= x - 1 < TPB:
                    dve.wait_ge(out_ready, j * TPB + x)
                    dve.wait_ge(ctx_turned, j * TPB + x - 1)
                    nc.vector.tensor_tensor(ctx_sb[:, :].rearrange("p (h d) -> p h d", d=BD),
                                            o_ps[:, 0:D].rearrange("p (h d) -> p h d", d=BD),
                                            inv_sum[k][:, x - 1, :].unsqueeze(2).broadcast_to([P, NH, BD]),
                                            ALU.mult).then_inc(ctx_ready, 1)
                if 0 <= x - 2 < TPB:
                    dve.wait_ge(ctx_turned, j * TPB + x - 1)
                    nc.vector.tensor_copy(ctx_t[:, :, :], misc[:, 0:D].rearrange("p (c q) -> p c q", q=P)).then_inc(ctx_copied, 1)

            def copy_product(i, k, n):
                what, h = PJ[n]
                bias = lambda m: small_rep[:, COLS + 2 + m:COLS + 3 + m]
                dve.wait_ge(pj_ready, 1 + i * NPJ + n + 1)
                if what == "disp":
                    last = nc.vector.tensor_scalar(disp[h][:, :], pj[:, :], b_disp_sb[:, h:h + 1], None, ALU.add)
                elif what == "u":
                    nc.vector.tensor_copy(sum_a[:, PAD:], pj[:, :])
                    last = nc.vector.tensor_scalar(u_less_b[:, :], pj[:, :], bias(0), None, ALU.subtract)
                elif what == "a":
                    last = nc.vector.tensor_copy(a_sb[k][h][:, PAD:], pj[:, :])
                elif what == "q":
                    last = nc.vector.tensor_scalar(q_sb[k][h][:, :], pj[:, :], bias(1), None, ALU.add)
                else:
                    nc.vector.tensor_copy(c_sb[k][h][:, PAD:], pj[:, :])
                    last = nc.vector.tensor_scalar(f_sb[k][h][:, :], pj[:, :], -1.0, bias(2), ALU.mult, ALU.add)
                last.then_inc(pj_copied, 1)
                if what == "u":
                    src, dst, step = sum_a, sum_b, 1
                    while step < WIN:
                        nc.vector.drain()
                        nc.vector.tensor_tensor(dst[:, step:], src[:, step:], src[:, 0:PAD + S - step], ALU.add)
                        src, dst, step = dst, src, 2 * step
                    nc.vector.drain()
                    nc.vector.tensor_tensor(dst[:, PAD:], src[:, PAD:], inv_count[:, :], ALU.mult)
                    nc.vector.drain()
                    nc.vector.tensor_tensor(state[h][:, :], dst[:, PAD:], u_less_b[:, :], ALU.subtract).then_inc(state_ready, 1)
                    nc.vector.drain()

            def prepare_step(i, k, q):
                if q == 0:
                    norm.dve_stats(i)
                if q == 2:
                    norm.dve_normalise(i)
                if q == 3:
                    norm.dve_copy_t(i, k, guard=False)
                if 0 <= q - PJ_STEP < NPJ:
                    copy_product(i, k, q - PJ_STEP)

            def copy_values(i, n):
                dve.wait_ge(val_ready, i * 4 + n + 1)
                for r in range(2):
                    rows = slice(r * SPAN, (r + 1) * SPAN)
                    nc.vector.tensor_tensor(
                        vals[rows, 4 * n:4 * n + 4, :, r, :],
                        t_ps[rows, :].rearrange("p (a h d) -> p a h d", a=4, d=BD),
                        b_val_sb[rows, :, r, :].unsqueeze(1).broadcast_to([SPAN, 4, HP, BD]),
                        ALU.add).then_inc(val_copied, 1)

            def bond_chunk(i, k, q):
                h, dg = divmod(q, NQ)
                dve.wait_ge(chunk_used, i * 2 * STEPS + 2 * q + 1)
                for dd in range(DG):
                    d = dg * DG + dd
                    last = nc.vector.scalar_tensor_tensor(
                        out=bond_buf[q % 2][:, dd, :], in0=a_sb[k][h][:, d + 1:d + 1 + S],
                        scalar=small_rep[:, COLS + 5 + d:COLS + 6 + d], in1=q_sb[k][h][:, :],
                        op0=ALU.add, op1=ALU.add)
                last.then_inc(bond_pre, 1)

            dve.sem_inc(chunk_used, 4)
            for banks in (bond_ps, dmg_ps):
                for n in range(2):
                    nc.vector.memset(banks[n][:, :, :, :], 0.0)
            nc.vector.tensor_copy(select[:, :, :], core.ident[0:BD, 0:BD].unsqueeze(1).broadcast_to([BD, HH, BD]))
            dve.wait_ge(consts, 3)
            nc.vector.tensor_scalar(inv_count[:, :], inv_count[:, :], float(WIN), None, ALU.min)
            nc.vector.drain()
            nc.vector.reciprocal(inv_count[:, :], inv_count[:, :])
            dve.wait_ge(loaded, LOADED)
            dve.wait_ge(rel_loaded, 32)
            nc.vector.drain().then_inc(tables_a, 1)
            dve.wait_ge(pj_ready, 1)
            nc.vector.tensor_copy(small[:, COLS + 5:], pj[0:BD, 0:WIN]).then_inc(tables_b, 1)
            dve.wait_ge(proj_ready, 1)
            nc.vector.tensor_copy(small_rep[:, :], misc[:, 0:SM])
            nc.vector.drain()
            for n in range(5):
                nc.vector.tensor_tensor(mats[n][:, :, :], diag[:, :, :],
                                        small_rep[:, n * BD:(n + 1) * BD].unsqueeze(1).broadcast_to([P, HH, BD]), ALU.mult)
            nc.vector.tensor_scalar(col_bond[:, :], diag[:, :, 0], small_rep[:, COLS:COLS + 1], None, ALU.mult)
            nc.vector.tensor_scalar(col_damage[:, :], diag[:, :, 0], small_rep[:, COLS + 1:COLS + 2], None, ALU.mult)
            nc.vector.drain()
            nc.vector.tensor_scalar(neg_strain[:, :, :], mats[STRAIN][:, :, :], -1.0, None, ALU.mult).then_inc(tables, 1)
            for q in range(STEPS):
                prepare_step(0, 0, q)
            with dve.Fori(0, B // 2) as pair:
                for k in range(2):
                    i = pair * 2 + k
                    for q in range(STEPS):
                        if q == 0:
                            nc.vector.drain()
                        bond_chunk(i, k, q)
                        if q == NQ + 1:
                            read_half(i + 1, 0)
                        finish_step(i, 1 - k, q)
                        prepare_step(i + 1, 1 - k, q)
                        if q >= VAL_STEP:
                            copy_values(i, q - VAL_STEP)
            for q in range(STEPS):
                finish_step(B, 1, q)


def macaron(nc, t, out, phases="f0 a0 f0 f1 a1 f1"):
    with ExitStack() as ctx:
        core = Core(nc, ctx)
        load_phase(core, t["L0_attn_x"])
        sparse = Sparse(core, ctx, t["L0_ffn_w1"].shape[0])
        if "f0" in phases:
            clear_rows(core, sparse.rows_in, "sparse")
        skew = nc.dram_tensor("skew", (P, TPB * (D // 16) * 2 * WIN), FP32, kind="Internal").ap()
        if "a0" in phases:
            clear_rows(core, skew.rearrange("p (r d) -> (p r) d", d=D), "skew")
        for n, ph in enumerate(phases.split()):
            core.free_semaphores()
            if ph == "f0":
                ffn0_phase(core, sparse, f"f0_{n}", *[t["L0_ffn_" + s] for s in
                           ("gate_w", "gate_b", "w1", "b1", "w2", "b2")])
            if ph == "f1":
                ffn1_phase(core, f"f1_{n}", *[t["L1_ffn_" + s] for s in
                           ("gate_W", "W1", "b1", "W2", "b2", "Ws1", "bs1", "Ws2", "bs2", "route_scale")])
            if ph == "a0":
                attn0_phase(core, f"a0_{n}", skew, *[t["L0_attn_" + s] for s in
                            ("w_disp", "b_disp", "w_val", "b_val", "rel_pos_emb", "w_state", "b_state", "w_strain",
                             "b_strain", "w_state_i", "w_state_j", "w_pos", "w_bond_out", "b_bond_out", "w_damage",
                             "b_damage", "w_damage_out", "b_damage_out", "w_cproj", "b_cproj")])
            if ph == "a1":
                attn1_phase(core, f"a1_{n}", *[t["L1_attn_" + s] for s in
                            ("Wq", "Wk", "Wv", "Wo", "bo", "rel_emb")])
        core.free_semaphores()
        store_phase(core, out)
        core.free_semaphores()


_L0_ATTN = ("x", "w_disp", "b_disp", "w_val", "b_val", "rel_pos_emb", "w_state", "b_state", "w_strain", "b_strain",
            "w_state_i", "w_state_j", "w_pos", "w_bond_out", "b_bond_out", "w_damage", "b_damage", "w_damage_out",
            "b_damage_out", "w_cproj", "b_cproj")
_L0_FFN = ("gate_w", "gate_b", "w1", "b1", "w2", "b2")
_L1_ATTN = ("Wq", "Wk", "Wv", "Wo", "bo", "rel_emb")
_L1_FFN = ("gate_W", "W1", "b1", "W2", "b2", "Ws1", "bs1", "Ws2", "bs2", "route_scale")
_INS = [part + n for part, names in (("L0_attn_", _L0_ATTN), ("L0_ffn_", _L0_FFN), ("L1_attn_", _L1_ATTN),
                                     ("L1_ffn_", _L1_FFN)) for n in names]


def kernel(**inputs):
    import numpy as _np
    import concourse.bacc as _bacc
    from concourse import mybir as _mybir
    from concourse.bass_utils import run_bass_kernel_spmd as _run

    nc = _bacc.Bacc("TRN2", target_bir_lowering=False, num_devices=1)
    arrays, tensors = {}, {}
    for name in _INS:
        a = _np.ascontiguousarray(inputs[name])
        a = a.reshape(a.shape or (1,))
        arrays[f"in_{name}_dram"] = a
        tensors[name] = nc.dram_tensor(f"in_{name}_dram", a.shape, _mybir.dt.from_np(a.dtype),
                                       kind="ExternalInput").ap()
    x = inputs["L0_attn_x"]
    out = nc.dram_tensor("out_0_dram", tuple(x.shape), _mybir.dt.float32, kind="ExternalOutput").ap()
    macaron(nc, tensors, out)
    r = _run(nc, [arrays], core_ids=[0])
    return r.results[0]["out_0_dram"]
```

```python
from contextlib import ExitStack

import numpy as np

import concourse.bass as bass
from concourse import mybir

FP32 = mybir.dt.float32
BF16 = mybir.dt.bfloat16
U32 = mybir.dt.uint32
ALU = mybir.AluOpType
ACT = mybir.ActivationFunctionType
AX = mybir.AxisListType

P = 128
B, S, D = 8, 512, 256
TPB = S // P
DC = D // P
EPS = 1e-5


def due(count):
    return not isinstance(count, int) or count > 0


class Core:

    def __init__(self, nc, ctx):
        self.nc = nc
        self.sems = []
        self.x = ctx.enter_context(nc.sbuf_tensor("x_resid", [P, (B + 2) * TPB, D], FP32))
        self.ident = ctx.enter_context(nc.sbuf_tensor("ident", [P, P], FP32))

    def semaphore(self, name):
        self.sems.append(self.nc.alloc_semaphore(name))
        return self.sems[-1]

    def free_semaphores(self):
        self.nc.clear_and_free_semaphores(self.sems)
        self.nc.all_engine_barrier()
        self.sems = []

    def x_batch(self, i):
        return self.x[:, bass.ds((i + 1) * TPB, TPB), :]

    def tile(self, n, j):
        return self.x[:, n * TPB + j, :]


def load_phase(core, x_dram):
    nc = core.nc
    with ExitStack() as ctx:
        x_in = core.semaphore("x_in")
        zeroed = core.semaphore("zeroed")
        block = ctx.enter_context(nc.Block())

        @block.sync
        def _(sp):
            sp.dma_start(core.x[:, TPB:(B + 1) * TPB, :],
                         x_dram.rearrange("b (j p) d -> p (b j) d", p=P)).then_inc(x_in, 16)
            sp.wait_ge(x_in, 16)

        @block.gpsimd
        def _(pool):
            nc.gpsimd.memset(core.x[:, (B + 1) * TPB:, :], 0.0)
            nc.gpsimd.memset(core.x[:, 0:TPB, :], 0.0)
            nc.gpsimd.memset(core.ident[:, :], 0.0).then_inc(zeroed, 1)
            pool.wait_ge(zeroed, 1)
            nc.gpsimd.affine_select(out=core.ident[:, :], in_=core.ident[:, :], compare_op=ALU.not_equal,
                                    fill=1.0, base=0, pattern=[[-1, P]], channel_multiplier=1)


def store_phase(core, out_dram):
    nc = core.nc
    with ExitStack() as ctx:
        stored = core.semaphore("stored")
        block = ctx.enter_context(nc.Block())

        @block.sync
        def _(sp):
            sp.dma_start(out_dram.rearrange("b (j p) d -> p (b j) d", p=P),
                         core.x[:, TPB:(B + 1) * TPB, :]).then_inc(stored, 16)
            sp.wait_ge(stored, 16)


class Norm:

    def __init__(self, core, ctx, name, xn_buffers=1, pad=0):
        nc = core.nc
        self.core, self.nc = core, nc
        sb = lambda n, s: ctx.enter_context(nc.sbuf_tensor(f"{name}_{n}", s, FP32))
        sem = lambda n: core.semaphore(f"{name}_{n}")
        self.stats = sb("stats", [P, TPB, 6])
        self.mean_var = sb("mean_var", [P, TPB, 2])
        self.var_eps = sb("var_eps", [P, TPB])
        self.std = sb("std", [P, TPB])
        self.rstd = sb("rstd", [P, TPB])
        self.xns = [sb(f"xn{k}", [P, TPB, D]) for k in range(xn_buffers)]
        self.pad = pad
        self.xn_t = [sb(f"xn_t{k}", [P, DC, pad + S]) for k in range(2)]
        self.tp = ctx.enter_context(nc.psum_tensor(f"{name}_tp", [P, S], FP32))
        self.var_ready = sem("var_ready")
        self.std_ready = sem("std_ready")
        self.xn_ready = sem("xn_ready")
        self.t_ready = sem("t_ready")
        self.t_copied = sem("t_copied")
        self.free = sem("xn_t_free")

    def dve_stats(self, i):
        nc = self.nc
        for j in range(TPB):
            nc.vector.bn_stats(self.stats[:, j, :], self.core.tile(i + 1, j))
        nc.vector.drain()
        for j in range(TPB):
            nc.vector.bn_aggr(self.mean_var[:, j, :], self.stats[:, j, :])
        nc.vector.drain()
        nc.vector.tensor_scalar(self.var_eps[:, :], self.mean_var[:, :, 1], EPS, None,
                                ALU.add).then_inc(self.var_ready, 1)

    def act_std(self, i):
        self.nc.scalar.wait_ge(self.var_ready, i + 1)
        self.nc.scalar.activation(self.std[:, :], self.var_eps[:, :], ACT.Sqrt).then_inc(self.std_ready, 1)

    def dve_normalise(self, i, k=0):
        nc = self.nc
        nc.vector.wait_ge(self.std_ready, i + 1)
        nc.vector.reciprocal(self.rstd[:, :], self.std[:, :])
        nc.vector.drain()
        for j in range(TPB):
            last = nc.vector.tensor_scalar(self.xns[k][:, j, :], self.core.tile(i + 1, j),
                                           self.mean_var[:, j, 0:1], self.rstd[:, j:j + 1],
                                           ALU.subtract, ALU.mult)
        last.then_inc(self.xn_ready, 1)

    def pe_transpose(self, i, k=0, chunks=range(DC)):
        nc = self.nc
        nc.tensor.wait_ge(self.xn_ready, i + 1)
        for c in chunks:
            if due(i * DC + c):
                nc.tensor.wait_ge(self.t_copied, i * DC + c)
            for j in range(TPB):
                last = nc.tensor.transpose(self.tp[:, j * P:(j + 1) * P], self.xns[k][:, j, c * P:(c + 1) * P],
                                           self.core.ident[:, :])
            last.then_inc(self.t_ready, 1)

    def dve_copy_t(self, i, k, guard=True, chunks=range(DC)):
        nc = self.nc
        if guard:
            if due(i - 1):
                nc.vector.wait_ge(self.free, i - 1)
        for c in chunks:
            nc.vector.wait_ge(self.t_ready, i * DC + c + 1)
            nc.vector.tensor_copy(self.xn_t[k][:, c, self.pad:], self.tp[:, :]).then_inc(self.t_copied, 1)

    def wait_xn_t(self, eng, i):
        eng.wait_ge(self.t_copied, (i + 1) * DC)



def ffn1_phase(core, name, gate_w, w1, b1, w2, b2, ws1, bs1, ws2, bs2, route_scale):
    nc = core.nc
    E, H = w1.shape[0], w1.shape[2]
    NE = E + 1
    UNITS = 2 * (NE + 1)
    YB = 4
    ctx = ExitStack()
    with ctx:
        sb = lambda n, s, dt=FP32: ctx.enter_context(nc.sbuf_tensor(f"{name}_{n}", s, dt))
        ps = lambda n, s: ctx.enter_context(nc.psum_tensor(f"{name}_{n}", s, FP32))
        sem = lambda n: core.semaphore(f"{name}_{n}")
        norm = Norm(core, ctx, name)
        gate_w_sb = sb("gate_w", [P, DC, E])
        w1_sb = sb("w1", [P, NE, DC, H])
        w2_sb = sb("w2", [P, NE, D])
        b1_sb = sb("b1", [P, NE])
        b2_sb = sb("b2", [NE, D])
        route_sb = sb("route", [P, 1])
        iota_e = sb("iota_e", [P, TPB, E])
        sig = sb("sig", [P, TPB, E])
        score = sb("score", [P, TPB, E])
        top_v = sb("top_v", [P, TPB, 8])
        top_i = sb("top_i", [P, TPB, 8], U32)
        top_f = sb("top_f", [P, TPB, 2])
        inv = sb("inv", [P, TPB, 1])
        part = [sb(f"part{r}", [P, TPB, E]) for r in range(2)]
        weight = sb("weight", [P, TPB, 2])
        gate = [sb(f"gate{k}", [P, TPB, NE]) for k in range(2)]
        gate_t = [sb(f"gate_t{k}", [NE, S]) for k in range(2)]
        h_t = [sb(f"h_t{k}", [P, S]) for k in range(2)]
        acc = sb("acc", [P, TPB, D])
        gate_ps = ps("gate_ps", [P, 512])
        h_ps = [ps(f"h_ps{k}", [P, S]) for k in range(2)]
        y_ps = [ps(f"y_ps{k}", [P, 2, D]) for k in range(YB)]

        loaded = sem("loaded")
        const_ready = sem("const_ready")
        logits_ready = sem("logits_ready")
        sig_ready = sem("sig_ready")
        gate_ready = sem("gate_ready")
        gate_t_ready = sem("gate_t_ready")
        gate_t_copied = sem("gate_t_copied")
        h_ready = sem("h_ready")
        act_ready = sem("act_ready")
        y_ready = sem("y_ready")
        y_free = sem("y_free")
        block = ctx.enter_context(nc.Block())

        @block.sync
        def _(sp):
            def load(dst, src, **kind):
                sp.dma_start(dst, src, **kind).then_inc(loaded, 16)
            load(gate_w_sb[:, :, :], gate_w.rearrange("(c p) e -> p c e", p=P))
            load(route_sb[:, :], route_scale.partition_broadcast(P))
            for e in range(E):
                load(w1_sb[:, e, :, :], w1[e].rearrange("(c p) h -> p c h", p=P))
            load(w1_sb[:, E, :, :], ws1.rearrange("(c p) h -> p c h", p=P))
            load(w2_sb[:, 0:E, :], w2.rearrange("e h d -> h e d"))
            load(w2_sb[:, E, :], ws2)
            load(b1_sb[:, 0:E], b1.rearrange("e h -> h e"), allow_slow_non_contiguous=True)
            load(b1_sb[:, E:NE], bs1.rearrange("(h o) -> h o", o=1))
            load(b2_sb[0:E, :], b2)
            load(b2_sb[E:NE, :], bs2.rearrange("(o d) -> o d", o=1))
        LOADED = 16 * (E + 9)

        @block.gpsimd
        def _(pool):
            nc.gpsimd.iota(iota_e[:, :, :], pattern=[[0, TPB], [1, E]], base=0, channel_multiplier=0,
                           allow_small_or_imprecise_dtypes=True)
            for k in range(2):
                last = nc.gpsimd.memset(gate[k][:, :, E:NE], 1.0)
            last.then_inc(const_ready, 1)

        @block.tensor
        def _(pe):
            def logits(i, k):
                norm.wait_xn_t(pe, i)
                for j in range(TPB):
                    for c in range(DC):
                        last = nc.tensor.matmul(gate_ps[:, j * E:(j + 1) * E],
                                                norm.xn_t[k][:, c, j * P:(j + 1) * P],
                                                gate_w_sb[:, c, :], start=c == 0, stop=c == DC - 1)
                last.then_inc(logits_ready, 1)

            def turn_gates(i, k):
                pe.wait_ge(gate_ready, i + 1)
                for j in range(TPB):
                    last = nc.tensor.transpose(gate_ps[0:NE, j * P:(j + 1) * P], gate[k][:, j, :],
                                               core.ident[:, :])
                last.then_inc(gate_t_ready, 1)

            def up(i, k, e):
                n = i * NE + e
                pe.wait_ge(act_ready, n + 1)
                if e == 0:
                    norm.wait_xn_t(pe, i)
                for c in range(DC):
                    last = nc.tensor.matmul(h_ps[(k * NE + e) % 2][:, :], w1_sb[:, e, c, :],
                                            norm.xn_t[k][:, c, :], start=c == 0, stop=c == DC - 1)
                last.then_inc(h_ready, 1)

            def down(i, k, e):
                pe.wait_ge(act_ready, 2 + i * NE + e + 1)
                h = h_t[(k * NE + e) % 2]
                for half in range(2):
                    m = 2 * (e + 1) + half
                    pe.wait_ge(y_free, i * UNITS + m + 1)
                    for j in range(2):
                        t = 2 * half + j
                        last = nc.tensor.matmul(y_ps[m % YB][:, j, :], h[:, t * P:(t + 1) * P],
                                                w2_sb[:, e, :], start=True, stop=True)
                        if e == NE - 1 and t == 0:
                            last.then_inc(norm.free, 1)
                    last.then_inc(y_ready, 1)

            def biases(i, k):
                pe.wait_ge(gate_t_copied, i + 1)
                for half in range(2):
                    pe.wait_ge(y_free, i * UNITS + half + 1)
                    for j in range(2):
                        t = 2 * half + j
                        last = nc.tensor.matmul(y_ps[half][:, j, :], gate_t[k][:, t * P:(t + 1) * P],
                                                b2_sb[:, :], start=True, stop=True)
                    last.then_inc(y_ready, 1)

            pe.wait_ge(loaded, LOADED)
            norm.pe_transpose(0)
            logits(0, 0)
            turn_gates(0, 0)
            with pe.Fori(0, B // 2) as pair:
                for k in range(2):
                    i = pair * 2 + k
                    up(i, k, 0)
                    biases(i, k)
                    for e in range(NE):
                        if e + 1 < NE:
                            up(i, k, e + 1)
                        down(i, k, e)
                        if e == 2:
                            norm.pe_transpose(i + 1)
                        if e == 4:
                            logits(i + 1, 1 - k)
                        if e == 6:
                            turn_gates(i + 1, 1 - k)

        @block.scalar
        def _(act):
            def sigmoid(i):
                act.wait_ge(logits_ready, i + 1)
                nc.scalar.activation(sig[:, :, :], gate_ps[:, 0:TPB * E].rearrange("p (j e) -> p j e", e=E),
                                     ACT.Sigmoid).then_inc(sig_ready, 1)

            def gelu(i, k, e):
                n = i * NE + e
                act.wait_ge(h_ready, n + 1)
                act.wait_ge(y_ready, i * UNITS + 2 * e)
                nc.scalar.activation(h_t[(k * NE + e) % 2][:, :], h_ps[(k * NE + e) % 2][:, :], ACT.Gelu,
                                     bias=b1_sb[:, e:e + 1]).then_inc(act_ready, 1)

            act.sem_inc(act_ready, 2)
            act.wait_ge(loaded, LOADED)
            norm.act_std(0)
            sigmoid(0)
            with act.Fori(0, B // 2) as pair:
                for k in range(2):
                    i = pair * 2 + k
                    for e in range(NE):
                        gelu(i, k, e)
                        if e == 1:
                            norm.act_std(i + 1)
                        if e == 5:
                            sigmoid(i + 1)

        @block.vector
        def _(dve):
            def gates(i, k):
                dve.wait_ge(sig_ready, i + 1)
                nc.vector.tensor_scalar(score[:, :, :], sig[:, :, :], route_sb[:, 0:1], None, ALU.mult)
                nc.vector.drain()
                for j in range(TPB):
                    nc.vector.max(top_v[:, j, :], score[:, j, :])
                nc.vector.drain()
                for j in range(TPB):
                    nc.vector.max_index(top_i[:, j, :], top_v[:, j, :], score[:, j, :])
                nc.vector.tensor_tensor(inv[:, :, :], top_v[:, :, 0:1], top_v[:, :, 1:2], ALU.add)
                nc.vector.drain()
                nc.vector.reciprocal(inv[:, :, :], inv[:, :, :])
                nc.vector.tensor_copy(top_f[:, :, :], top_i[:, :, 0:2])
                nc.vector.drain()
                nc.vector.tensor_tensor(weight[:, :, :], top_v[:, :, 0:2],
                                        inv[:, :, :].broadcast_to([P, TPB, 2]), ALU.mult)
                for r in range(2):
                    nc.vector.tensor_tensor(part[r][:, :, :], iota_e[:, :, :],
                                            top_f[:, :, r:r + 1].broadcast_to([P, TPB, E]), ALU.is_equal)
                nc.vector.drain()
                for r in range(2):
                    nc.vector.tensor_tensor(part[r][:, :, :], part[r][:, :, :],
                                            weight[:, :, r:r + 1].broadcast_to([P, TPB, E]), ALU.mult)
                nc.vector.drain()
                nc.vector.tensor_tensor(gate[k][:, :, 0:E], part[0][:, :, :], part[1][:, :, :],
                                        ALU.add).then_inc(gate_ready, 1)

            def copy_gates(i, k):
                dve.wait_ge(gate_t_ready, i + 1)
                nc.vector.tensor_copy(gate_t[k][:, :], gate_ps[0:NE, :]).then_inc(gate_t_copied, 1)

            def add(i, k, n):
                nc.vector.drain()
                for half in range(2):
                    m = 2 * n + half
                    dve.wait_ge(y_ready, 2 + i * UNITS + m + 1)
                    y = y_ps[m % YB]
                    if n == 0:
                        last = nc.vector.tensor_copy(acc[:, 2 * half:2 * half + 2, :], y[:, :, :])
                    else:
                        for j in range(2):
                            t = 2 * half + j
                            last = nc.vector.scalar_tensor_tensor(
                                out=acc[:, t, :], in0=y[:, j, :], scalar=gate[k][:, t, n - 1:n],
                                in1=acc[:, t, :], op0=ALU.mult, op1=ALU.add)
                    last.then_inc(y_free, 1)

            dve.sem_inc(y_ready, 2)
            dve.sem_inc(y_free, YB)
            dve.wait_ge(loaded, LOADED)
            dve.wait_ge(const_ready, 1)
            norm.dve_stats(0)
            norm.dve_normalise(0)
            norm.dve_copy_t(0, 0)
            gates(0, 0)
            copy_gates(0, 0)
            with dve.Fori(0, B // 2) as pair:
                for k in range(2):
                    i = pair * 2 + k
                    for n in range(NE + 1):
                        add(i, k, n)
                        if n == 1:
                            norm.dve_stats(i + 1)
                        if n == 2:
                            norm.dve_normalise(i + 1)
                        if n == 3:
                            norm.dve_copy_t(i + 1, 1 - k)
                        if n == 5:
                            gates(i + 1, 1 - k)
                        if n == 7:
                            copy_gates(i + 1, 1 - k)
                    nc.vector.drain()
                    nc.vector.scalar_tensor_tensor(out=core.x_batch(i), in0=acc[:, :, :], scalar=0.5,
                                                   in1=core.x_batch(i), op0=ALU.mult, op1=ALU.add)



MASKED = -1e30


def attn1_phase(core, name, wq, wk, wv, wo, bo, rel_emb):
    nc = core.nc
    NH = 16
    HD = D // NH
    CLIP = rel_emb.shape[0] - 1
    HG = 4
    QT = NH // HG
    SCALE = HD ** -0.5
    UNITS = TPB * NH
    PR = 8
    LAG = 3
    TR = 6
    AHEAD = 3
    VC = 32
    TB = 2
    BY_ACT = [m % 5 in (1, 3) for m in range(UNITS)]
    BEFORE = [(m + 1 - sum(BY_ACT[:m + 1]), sum(BY_ACT[:m + 1])) for m in range(UNITS)]
    N_DVE, N_ACT = BEFORE[-1]
    ctx = ExitStack()
    with ctx:
        sb = lambda n, s, dt=FP32: ctx.enter_context(nc.sbuf_tensor(f"{name}_{n}", s, dt))
        ps = lambda n, s: ctx.enter_context(nc.psum_tensor(f"{name}_{n}", s, FP32))
        sem = lambda n: core.semaphore(f"{name}_{n}")
        norm = Norm(core, ctx, name)
        wq_sb = sb("wq", [P, DC, QT, HG, 32])
        wk_sb = sb("wk", [P, DC, QT, HG, 32])
        wv_sb = sb("wv", [P, DC, D])
        wo_sb = sb("wo", [P, DC, D])
        bo_sb = sb("bo", [1, D])
        ones = sb("ones", [1, P])
        rel_sb = sb("rel", [P, CLIP + 1])
        factor = sb("factor", [P, S])
        dist = sb("dist", [P, S])
        hit = sb("hit", [P, S])
        mask_f = sb("mask_f", [P, P])
        mask_b = sb("mask_b", [P, P], BF16)
        ident_b = sb("ident_b", [P, P], BF16)
        q_t = sb("q_t", [P, QT, S])
        k_t = sb("k_t", [P, QT, S])
        v_sb = [sb(f"v{k}", [P, TPB, NH, VC]) for k in range(2)]
        prob = sb("prob", [P, PR, S])
        top = sb("top", [P, 2, HG])
        neg_top = sb("neg_top", [P, 2, HG])
        prob_t = sb("prob_t", [P, TR, S])
        inv = sb("inv", [P, NH, 1])
        o_sb = sb("o", [P, S])
        ctx_sb = sb("ctx", [P, D])
        ctx_t = sb("ctx_t", [P, DC, P])
        s_ps = [ps(f"s_ps{k}", [P, S]) for k in range(HG)]
        t_ps = [ps(f"t_ps{k}", [P, S]) for k in range(TB)]
        o_ps = ps("o_ps", [P, S])
        misc = norm.tp

        loaded = sem("loaded")
        zeroed = sem("zeroed")
        consts = sem("consts")
        factor_ready = sem("factor_ready")
        proj_ready = sem("proj_ready")
        proj_dve = sem("proj_dve")
        proj_act = sem("proj_act")
        qk_ready = sem("qk_ready")
        s_free = sem("s_free")
        groups_begun = sem("groups_begun")
        top_ready = sem("top_ready")
        exp_ready = sem("exp_ready")
        turned = sem("turned")
        t_dve = sem("t_dve")
        t_act = sem("t_act")
        pv_done = sem("pv_done")
        o_copied = sem("o_copied")
        o_turned = sem("o_turned")
        ctx_ready = sem("ctx_ready")
        ctx_turned = sem("ctx_turned")
        ctx_copied = sem("ctx_copied")
        out_ready = sem("out_ready")
        out_added = sem("out_added")
        block = ctx.enter_context(nc.Block())

        PRODUCTS = (range(0, HG), range(HG, 2 * QT), range(2 * QT, 2 * QT + 2))
        PROJ_M = UNITS - HG

        @block.sync
        def _(sp):
            def load(dst, src):
                sp.dma_start(dst, src).then_inc(loaded, 16)
            load(wv_sb[:, :, :], wv.rearrange("(c p) n -> p c n", p=P))
            load(wo_sb[:, :, :], wo.rearrange("(c p) n -> p c n", p=P))
            load(bo_sb[:, :], bo.rearrange("(o n) -> o n", o=1))
            load(rel_sb[:, :], rel_emb.partition_broadcast(P))
            sp.wait_ge(zeroed, 2)
            for dst, src in ((wq_sb, wq), (wk_sb, wk)):
                for c in range(DC):
                    load(dst[:, c, :, :, 0:HD].rearrange("p t g d -> p (t g) d"),
                         src[c * P:(c + 1) * P, :].rearrange("p (h d) -> p h d", d=HD))
        LOADED = 16 * (4 + 2 * DC)

        @block.gpsimd
        def _(pool):
            nc.gpsimd.memset(wq_sb[:, :, :, :, :], 0.0).then_inc(zeroed, 1)
            nc.gpsimd.memset(wk_sb[:, :, :, :, :], 0.0).then_inc(zeroed, 1)
            nc.gpsimd.memset(ones[:, :], 1.0)
            for v in v_sb:
                nc.gpsimd.memset(v[:, :, :, HD:HD + 1], 1.0)
                nc.gpsimd.memset(v[:, :, :, HD + 1:VC], 0.0)
            nc.gpsimd.iota(dist[:, :], pattern=[[-1, S]], base=S - P, channel_multiplier=1,
                           allow_small_or_imprecise_dtypes=True)
            nc.gpsimd.memset(mask_f[:, :], 0.0).then_inc(consts, 1)
            pool.wait_ge(consts, 1)
            nc.gpsimd.affine_select(out=mask_f[:, :], in_=mask_f[:, :], compare_op=ALU.is_ge,
                                    fill=MASKED, base=0, pattern=[[-1, P]],
                                    channel_multiplier=1).then_inc(consts, 1)

        @block.tensor
        def _(pe):
            def project(i, k, products):
                if products[0] == 0:
                    norm.wait_xn_t(pe, i)
                    pe.wait_ge(s_free, i * UNITS + HG)
                for n in products:
                    bank = s_ps[n % HG]
                    if n >= HG:
                        pe.wait_ge((proj_dve, proj_act)[n % 2], i * (QT + 1) + (n - HG) // 2 + 1)
                    if n < 2 * QT:
                        w_sb = (wq_sb, wk_sb)[n // QT]
                        for c in range(DC):
                            last = nc.tensor.matmul(bank[:, :], w_sb[:, c, n % QT, :, :].rearrange("p g d -> p (g d)"),
                                                    norm.xn_t[k][:, c, :], start=c == 0, stop=c == DC - 1)
                    else:
                        for j in range(2):
                            t = 2 * (n - 2 * QT) + j
                            for c in range(DC):
                                last = nc.tensor.matmul(bank[:, j * D:(j + 1) * D],
                                                        norm.xn_t[k][:, c, t * P:(t + 1) * P], wv_sb[:, c, :],
                                                        start=c == 0, stop=c == DC - 1)
                    last.then_inc(proj_ready, 1)

            def first_scores(i):
                pe.wait_ge(proj_dve, (i + 1) * (QT + 1))
                pe.wait_ge(proj_act, (i + 1) * (QT + 1))
                for m in range(HG):
                    scores(i, m)

            def scores(i, m):
                t, h = divmod(m, NH)
                tile, g = divmod(h, HG)
                width = (t + 1) * P
                pe.wait_ge(s_free, i * UNITS + m + 1)
                rows = slice(32 * g, 32 * g + HD)
                nc.tensor.matmul(s_ps[m % HG][:, 0:width], q_t[rows, tile, t * P:(t + 1) * P],
                                 k_t[rows, tile, 0:width], start=True, stop=False)
                nc.tensor.matmul(s_ps[m % HG][:, t * P:width], ident_b[:, :], mask_b[:, :],
                                 start=False, stop=True).then_inc(qk_ready, 1)

            def turn(i, m):
                t = m // NH
                pe.wait_ge(exp_ready, i * UNITS + m + 1)
                if m >= TB:
                    wait_copied(i, m - TB)
                for kb in range(t + 1):
                    last = nc.tensor.transpose(t_ps[m % TB][:, kb * P:(kb + 1) * P],
                                               prob[:, m % PR, kb * P:(kb + 1) * P], core.ident[:, :])
                last.then_inc(turned, 1)

            def wait_copied(i, m):
                dve_n, act_n = BEFORE[m]
                if BY_ACT[m]:
                    pe.wait_ge(t_act, i * N_ACT + act_n)
                else:
                    pe.wait_ge(t_dve, i * N_DVE + dve_n)

            def values(i, k, m):
                t, h = divmod(m, NH)
                group, g = divmod(h, HG)
                wait_copied(i, m)
                if h == 0:
                    pe.wait_ge(o_copied, i * TPB + t + 1)
                for kb in range(t + 1):
                    last = nc.tensor.matmul(o_ps[g * VC:(g + 1) * VC, group * P:(group + 1) * P],
                                            v_sb[k][:, kb, h, :], prob_t[:, m % TR, kb * P:(kb + 1) * P],
                                            start=kb == 0, stop=kb == t)
                last.then_inc(pv_done, 1)

            def turn_o(n):
                pe.wait_ge(o_copied, n + 1)
                pe.wait_ge(out_added, n + 1)
                for group in range(QT):
                    last = nc.tensor.transpose(misc[:, group * P:(group + 1) * P], o_sb[:, group * P:(group + 1) * P],
                                               core.ident[:, :])
                last.then_inc(o_turned, 1)

            def turn_ctx(n):
                pe.wait_ge(ctx_ready, n + 1)
                for c in range(DC):
                    last = nc.tensor.transpose(misc[:, c * P:(c + 1) * P], ctx_sb[:, c * P:(c + 1) * P],
                                               core.ident[:, :])
                last.then_inc(ctx_turned, 1)

            def output(n):
                pe.wait_ge(ctx_copied, n + 1)
                for c in range(DC):
                    nc.tensor.matmul(misc[:, D:2 * D], ctx_t[:, c, :], wo_sb[:, c, :],
                                     start=c == 0, stop=False)
                nc.tensor.matmul(misc[:, D:2 * D], ones[:, :], bo_sb[:, :], start=False,
                                 stop=True).then_inc(out_ready, 1)

            pe.wait_ge(loaded, LOADED)
            pe.wait_ge(factor_ready, 1)
            norm.pe_transpose(0)
            for products in PRODUCTS:
                project(0, 0, products)
            first_scores(0)
            with pe.Fori(0, B // 2) as pair:
                for k in range(2):
                    i = pair * 2 + k
                    for m in range(UNITS):
                        t, h = divmod(m, NH)
                        if m % HG == 0 and m + HG < UNITS:
                            for g in range(HG):
                                scores(i, m + HG + g)
                        if m >= PROJ_M and m < UNITS - 1:
                            project(i + 1, 1 - k, PRODUCTS[m - PROJ_M])
                        if m == UNITS - 1:
                            first_scores(i + 1)
                        turn(i, m)
                        if m >= LAG:
                            values(i, k, m - LAG)
                        if h == 6:
                            if t == 1:
                                norm.wait_xn_t(pe, i + 1)
                            turn_o(i * TPB + t)
                        if h == 10:
                            turn_ctx(i * TPB + t)
                        if h == 12:
                            output(i * TPB + t)
                        if m == NH:
                            pe.wait_ge(out_added, i * TPB + 2)
                            norm.pe_transpose(i + 1, chunks=(0,))
                        if m == NH + 3:
                            norm.pe_transpose(i + 1, chunks=(1,))
                    for m in range(UNITS - LAG, UNITS):
                        values(i, k, m)
            turn_o(B * TPB)
            turn_ctx(B * TPB)
            output(B * TPB)

        @block.scalar
        def _(act):
            def empty(i, m):
                t = m // NH
                act.wait_ge(turned, PR + i * UNITS + m + 1)
                act.wait_ge(pv_done, i * UNITS + m + 1)
                nc.scalar.copy(prob_t[:, m % TR, 0:(t + 1) * P],
                               t_ps[m % TB][:, 0:(t + 1) * P]).then_inc(t_act, 1)

            def exps(i, m):
                t, h = divmod(m, NH)
                if h % HG == 0:
                    act.wait_ge(top_ready, i * (UNITS // HG) + m // HG + 1)
                nc.scalar.activation(prob[:, m % PR, 0:(t + 1) * P], prob[:, m % PR, 0:(t + 1) * P],
                                     ACT.Exp, bias=neg_top[:, (m // HG) % 2, h % HG:h % HG + 1]).then_inc(exp_ready, 1)

            act.sem_inc(turned, PR)
            act.sem_inc(pv_done, TR)
            act.wait_ge(loaded, LOADED)
            norm.act_std(0)

            def copy_products(i, k, products):
                for n in products:
                    if n % 2 == 0:
                        continue
                    act.wait_ge(proj_ready, i * (2 * QT + 2) + n + 1)
                    if n < 2 * QT:
                        last = nc.scalar.copy((q_t, k_t)[n // QT][:, n % QT, :], s_ps[n % HG][:, :])
                    else:
                        last = nc.scalar.copy(v_sb[k][:, 2:4, :, 0:HD],
                                              s_ps[n % HG][:, :].rearrange("p (j h d) -> p j h d", j=2, d=HD))
                    last.then_inc(proj_act, 1)

            for products in PRODUCTS:
                copy_products(0, 0, products)
            with act.Fori(0, B // 2) as pair:
                for k in range(2):
                    i = pair * 2 + k
                    for m in range(UNITS + AHEAD):
                        if m < UNITS:
                            exps(i, m)
                        if m == 8:
                            norm.act_std(i + 1)
                        if m - AHEAD in range(PROJ_M, UNITS - 1):
                            copy_products(i + 1, 1 - k, PRODUCTS[m - AHEAD - PROJ_M])
                        if m >= AHEAD and BY_ACT[m - AHEAD]:
                            empty(i, m - AHEAD)

        @block.vector
        def _(dve):
            def tables():
                nc.vector.tensor_copy(mask_b[:, :], mask_f[:, :])
                nc.vector.tensor_copy(ident_b[:, :], core.ident[:, :])
                nc.vector.tensor_scalar(dist[:, :], dist[:, :], float(CLIP), -1.0, ALU.min, ALU.max)
                nc.vector.memset(factor[:, :], 0.0)
                nc.vector.drain()
                for n in range(-1, CLIP + 1):
                    value = 1.0 if n < 0 else rel_sb[:, n:n + 1]
                    nc.vector.tensor_scalar(hit[:, :], dist[:, :], float(n), value, ALU.is_equal, ALU.mult)
                    nc.vector.drain()
                    nc.vector.tensor_tensor(factor[:, :], factor[:, :], hit[:, :], ALU.add)
                    nc.vector.drain()
                nc.vector.tensor_scalar(factor[:, :], factor[:, :], SCALE, None, ALU.mult).then_inc(factor_ready, 1)
                nc.vector.drain()

            def group(i, m):
                t = m // NH
                width = (t + 1) * P
                side = (m // HG) % 2
                dve.wait_ge(qk_ready, i * UNITS + m + HG)
                dve.wait_ge(turned, i * UNITS + m + HG)
                dve.sem_inc(groups_begun, 1)
                for g in range(HG):
                    nc.vector.tensor_tensor_reduce(
                        out=prob[:, (m + g) % PR, 0:width], in0=s_ps[g][:, 0:width],
                        in1=factor[:, S - width:S], scale=1.0, scalar=-3.0e38, op0=ALU.mult, op1=ALU.max,
                        accum_out=top[:, side, g:g + 1]).then_inc(s_free, 1)
                nc.vector.drain()
                nc.vector.tensor_scalar(neg_top[:, side, :], top[:, side, :], -1.0, None,
                                        ALU.mult).then_inc(top_ready, 1)

            def empty(i, m):
                t = m // NH
                dve.wait_ge(turned, PR + i * UNITS + m + 1)
                dve.wait_ge(pv_done, i * UNITS + m + 1)
                nc.vector.tensor_copy(prob_t[:, m % TR, 0:(t + 1) * P],
                                      t_ps[m % TB][:, 0:(t + 1) * P]).then_inc(t_dve, 1)

            def copy_o(n):
                dve.wait_ge(pv_done, TR + n * NH)
                nc.vector.tensor_copy(o_sb[:, :], o_ps[:, :]).then_inc(o_copied, 1)

            def divide(n):
                o = misc[:, :].rearrange("p (h d) -> p h d", d=VC)
                dve.wait_ge(o_turned, n + 1)
                nc.vector.reciprocal(inv[:, :, :], o[:, :, HD:HD + 1])
                nc.vector.drain()
                nc.vector.tensor_tensor(ctx_sb[:, :].rearrange("p (h d) -> p h d", d=HD), o[:, :, 0:HD],
                                        inv[:, :, :].broadcast_to([P, NH, HD]), ALU.mult).then_inc(ctx_ready, 1)

            def copy_ctx(n):
                dve.wait_ge(ctx_turned, n + 1)
                nc.vector.tensor_copy(ctx_t[:, :, :], misc[:, 0:D].rearrange("p (c q) -> p c q", q=P)).then_inc(ctx_copied, 1)

            def add_out(n, xt):
                dve.wait_ge(out_ready, n + 1)
                nc.vector.tensor_tensor(xt, misc[:, D:2 * D], xt, ALU.add).then_inc(out_added, 1)

            def copy_products(i, k, products):
                for n in products:
                    if n % 2 == 1:
                        continue
                    dve.wait_ge(proj_ready, i * (2 * QT + 2) + n + 1)
                    if n < 2 * QT:
                        last = nc.vector.tensor_copy((q_t, k_t)[n // QT][:, n % QT, :], s_ps[n % HG][:, :])
                    else:
                        last = nc.vector.tensor_copy(v_sb[k][:, 0:2, :, 0:HD],
                                                     s_ps[n % HG][:, :].rearrange("p (j h d) -> p j h d", j=2, d=HD))
                    last.then_inc(proj_dve, 1)

            dve.sem_inc(s_free, HG)
            dve.sem_inc(out_added, 1)
            nc.vector.memset(o_ps[:, :], 1.0)
            dve.wait_ge(loaded, LOADED)
            dve.wait_ge(consts, 2)
            tables()
            norm.dve_stats(0)
            norm.dve_normalise(0)
            norm.dve_copy_t(0, 0, guard=False)
            for products in PRODUCTS:
                copy_products(0, 0, products)
            group(0, 0)
            with dve.Fori(0, B // 2) as pair:
                for k in range(2):
                    i = pair * 2 + k
                    for m in range(UNITS):
                        t, h = divmod(m, NH)
                        if h == 3:
                            copy_o(i * TPB + t)
                        if m % HG == 0 and m + HG < UNITS:
                            group(i, m + HG)
                        if m >= PROJ_M and m < UNITS - 1:
                            copy_products(i + 1, 1 - k, PRODUCTS[m - PROJ_M])
                        if m == UNITS - 1:
                            group(i + 1, 0)
                        if not BY_ACT[m]:
                            empty(i, m)
                        if h == 8:
                            divide(i * TPB + t)
                        if h == 11:
                            copy_ctx(i * TPB + t)
                        if h == 14:
                            add_out(i * TPB + t, core.tile(i, TPB - 1) if t == 0 else core.tile(i + 1, t - 1))
                        if m == 5:
                            norm.dve_stats(i + 1)
                        if m == 13:
                            norm.dve_normalise(i + 1)
                        if m == NH + 1:
                            norm.dve_copy_t(i + 1, 1 - k, guard=False, chunks=(0,))
                        if m == NH + 4:
                            norm.dve_copy_t(i + 1, 1 - k, guard=False, chunks=(1,))
            copy_o(B * TPB)
            divide(B * TPB)
            copy_ctx(B * TPB)
            add_out(B * TPB, core.tile(B, TPB - 1))



TOP = 3
CAP = 128


class Sparse:

    def __init__(self, core, ctx, experts):
        nc = core.nc
        self.rows_in = nc.dram_tensor("rows_in", (experts * CAP, D), FP32, kind="Internal").ap()
        self.rows_out = nc.dram_tensor("rows_out", (experts * CAP, D), FP32, kind="Internal").ap()


def clear_rows(core, rows, name):
    nc = core.nc
    with ExitStack() as ctx:
        zeros = ctx.enter_context(nc.sbuf_tensor(f"{name}_zero_rows", [P, 8, D], FP32))
        ready = core.semaphore(f"{name}_zero_rows_ready")
        cleared = core.semaphore(f"{name}_rows_cleared")
        block = ctx.enter_context(nc.Block())
        per = 8
        n = rows.shape[0] // (P * per)

        @block.vector
        def _(dve):
            nc.vector.memset(zeros[:, :, :], 0.0).then_inc(ready, 1)

        @block.sync
        def _(sp):
            sp.wait_ge(ready, 1)
            view = rows.rearrange("(n p r) d -> n p r d", p=P, r=per)
            for m in range(n):
                sp.dma_start(view[m], zeros[:, :, :]).then_inc(cleared, 16)
            sp.wait_ge(cleared, 16 * n)


def ffn0_phase(core, sparse, name, gate_w, gate_b, w1, b1, w2, b2):
    nc = core.nc
    E, H = w1.shape[0], w1.shape[2]
    HC = H // P
    R = 4
    NT = B * TPB
    NK = TPB * TOP
    ctx = ExitStack()
    with ctx:
        sb = lambda n, s, dt=FP32: ctx.enter_context(nc.sbuf_tensor(f"{name}_{n}", s, dt))
        sem = lambda n: core.semaphore(f"{name}_{n}")
        w1_sb = [sb(f"w1_{s}", [P, DC, H]) for s in range(R)]
        w2_sb = [sb(f"w2_{s}", [P, HC, D]) for s in range(R)]
        b2_sb = [sb(f"b2_{s}", [1, D]) for s in range(R)]
        best = sb("best", [P, B, TOP, TPB])
        valid = sb("valid", [P, B, TOP, TPB])
        place = sb("place", [P, B, TOP, TPB], U32)
        w_loaded = [sem(f"w_loaded{s}") for s in range(R)]

        def load_weights(sp, s, e):
            sp.dma_start(w1_sb[s][:, :, :], w1[e, :, :].rearrange("(c p) h -> p c h", p=P)).then_inc(w_loaded[s], 16)
            sp.dma_start(w2_sb[s][:, :, :], w2[e, :, :].rearrange("(c p) d -> p c d", p=P)).then_inc(w_loaded[s], 16)
            sp.dma_start(b2_sb[s][:, :], b2[bass.ds(e, 1), :]).then_inc(w_loaded[s], 16)

        route(core, sparse, name, gate_w, gate_b, E, best, valid, place, load_weights, R)
        experts(core, sparse, name, b1, E, H, R, w1_sb, w2_sb, b2_sb, w_loaded, load_weights)
        combine(core, sparse, name, best, valid, place)


def route(core, sparse, name, gate_w, gate_b, E, best, valid, place, load_weights, R):
    nc = core.nc
    NK = TPB * TOP
    ctx = ExitStack()
    with ctx:
        sb = lambda n, s, dt=FP32: ctx.enter_context(nc.sbuf_tensor(f"{name}_{n}", s, dt))
        ps = lambda n, s: ctx.enter_context(nc.psum_tensor(f"{name}_{n}", s, FP32))
        sem = lambda n: core.semaphore(f"{name}_{n}")
        norm = Norm(core, ctx, name, xn_buffers=2)
        gate_w_sb = sb("gate_w", [P, DC, E])
        gate_b_sb = sb("gate_b", [P, E])
        iota_e = sb("iota_e", [P, E])
        before_f = sb("before_f", [P, P])
        before = sb("before", [P, P], BF16)
        ones = sb("ones", [P, P], BF16)
        logits = sb("logits", [P, TPB, E])
        top_v = sb("top_v", [P, TPB, 8])
        top_i = sb("top_i", [P, TPB, 8], U32)
        expert = sb("expert", [P, TOP, TPB])
        pick = sb("pick", [P, TOP, TPB, E])
        some = sb("some", [P, TPB, E])
        mask = sb("mask", [P, TPB, E], BF16)
        carry = sb("carry", [P, TPB + 1, E], BF16)
        product = sb("product", [P, TOP, TPB, E])
        pos = sb("pos", [P, TOP, TPB])
        over = sb("over", [P, TOP, TPB])
        near = sb("near", [P, TOP, TPB])
        target = [sb(f"target{k}", [P, TOP, TPB], U32) for k in range(2)]
        logit_ps = ps("logit_ps", [P, 512])
        pos_ps = ps("pos_ps", [P, 512])

        loaded = sem("r_loaded")
        consts = sem("r_consts")
        logits_ready = sem("r_logits")
        mask_ready = sem("r_mask")
        pos_ready = sem("r_pos")
        pos_read = sem("r_pos_read")
        target_ready = sem("r_target")
        carried = sem("r_carried")
        scattered = [sem(f"r_scattered{k}") for k in range(2)]
        block = ctx.enter_context(nc.Block())
        LOADED = 16 * 2

        @block.sync
        def _(sp):
            sp.dma_start(gate_w_sb[:, :, :], gate_w.rearrange("(c p) e -> p c e", p=P)).then_inc(loaded, 16)
            sp.dma_start(gate_b_sb[:, :], gate_b.partition_broadcast(P)).then_inc(loaded, 16)
            for s in range(R):
                load_weights(sp, s, s)

        @block.gpsimd
        def _(pool):
            nc.gpsimd.iota(iota_e[:, :], pattern=[[1, E]], base=0, channel_multiplier=0,
                           allow_small_or_imprecise_dtypes=True)
            nc.gpsimd.memset(carry[:, :, :], 0.0)
            nc.gpsimd.memset(ones[:, :], 1.0)
            nc.gpsimd.memset(before_f[:, :], 1.0).then_inc(consts, 1)
            pool.wait_ge(consts, 1)
            nc.gpsimd.affine_select(out=before_f[:, :], in_=before_f[:, :], compare_op=ALU.is_gt, fill=0.0,
                                    base=0, pattern=[[1, P]], channel_multiplier=-1).then_inc(consts, 1)
            with pool.Fori(0, B // 2) as pair:
                for k in range(2):
                    i = pair * 2 + k
                    pool.wait_ge(target_ready, i + 1)
                    pool.sem_inc(carried, 1)
                    for r in range(TOP):
                        for j in range(TPB):
                            nc.gpsimd.indirect_dma_start(
                                out=sparse.rows_in, out_offset=bass.IndirectOffsetOnAxis(ap=target[k][:, r, j:j + 1], axis=0),
                                in_=norm.xns[k][:, j, :], in_offset=None, bounds_check=E * CAP - 1,
                                oob_is_err=False).then_inc(scattered[k], 16)
            for k in range(2):
                pool.wait_ge(scattered[k], 16 * NK * (B // 2))

        @block.tensor
        def _(pe):
            pe.wait_ge(loaded, LOADED)
            norm.pe_transpose(0, 0)
            with pe.Fori(0, B // 2) as pair:
                for k in range(2):
                    i = pair * 2 + k
                    norm.wait_xn_t(pe, i)
                    pe.wait_ge(mask_ready, i)
                    for j in range(TPB):
                        for c in range(DC):
                            last = nc.tensor.matmul(logit_ps[:, j * E:(j + 1) * E],
                                                    norm.xn_t[k][:, c, j * P:(j + 1) * P],
                                                    gate_w_sb[:, c, :], start=c == 0, stop=c == DC - 1)
                    last.then_inc(logits_ready, 1)
                    norm.pe_transpose(i + 1, 1 - k)
                    pe.wait_ge(mask_ready, i + 1)
                    pe.wait_ge(pos_read, i)
                    nc.tensor.matmul(pos_ps[:, 0:TPB * E], before[:, :], mask[:, :, :].rearrange("p j e -> p (j e)"),
                                     start=True, stop=False).then_inc(norm.free, 1)
                    nc.tensor.matmul(pos_ps[:, 0:TPB * E], ones[:, :], carry[:, 0:TPB, :].rearrange("p j e -> p (j e)"),
                                     start=False, stop=True).then_inc(pos_ready, 1)

        @block.scalar
        def _(act):
            norm.act_std(0)
            with act.Fori(0, B) as i:
                norm.act_std(i + 1)

        @block.vector
        def _(dve):
            dve.wait_ge(loaded, LOADED)
            dve.wait_ge(consts, 2)
            nc.vector.tensor_copy(before[:, :], before_f[:, :])
            norm.dve_stats(0)
            norm.dve_normalise(0, 0)
            norm.dve_copy_t(0, 0)
            with dve.Fori(0, B // 2) as pair:
                for k in range(2):
                    i = pair * 2 + k
                    nc.vector.drain()
                    norm.dve_stats(i + 1)
                    dve.wait_ge(logits_ready, i + 1)
                    nc.vector.tensor_tensor(logits[:, :, :], logit_ps[:, 0:TPB * E].rearrange("p (j e) -> p j e", e=E),
                                            gate_b_sb[:, :].unsqueeze(1).broadcast_to([P, TPB, E]), ALU.add)
                    nc.vector.drain()
                    for j in range(TPB):
                        nc.vector.max(top_v[:, j, :], logits[:, j, :])
                    nc.vector.drain()
                    for j in range(TPB):
                        nc.vector.max_index(top_i[:, j, :], top_v[:, j, :], logits[:, j, :])
                    nc.vector.tensor_copy(best[:, i, :, :], top_v[:, :, 0:TOP].rearrange("p j r -> p r j"))
                    nc.vector.drain()
                    nc.vector.tensor_copy(expert[:, :, :], top_i[:, :, 0:TOP].rearrange("p j r -> p r j"))
                    dve.wait_ge(scattered[1 - k], pair * (16 * NK) + (0 if k == 0 else 16 * NK))
                    norm.dve_normalise(i + 1, 1 - k)
                    nc.vector.drain()
                    nc.vector.tensor_tensor(pick[:, :, :, :],
                                            iota_e[:, :].unsqueeze(1).unsqueeze(1).broadcast_to([P, TOP, TPB, E]),
                                            expert[:, :, :].unsqueeze(3).broadcast_to([P, TOP, TPB, E]), ALU.is_equal)
                    nc.vector.tensor_copy(carry[:, 0, :], carry[:, TPB, :])
                    nc.vector.drain()
                    nc.vector.tensor_tensor(some[:, :, :], pick[:, 0, :, :], pick[:, 1, :, :], ALU.add)
                    nc.vector.drain()
                    nc.vector.tensor_tensor(mask[:, :, :], some[:, :, :], pick[:, 2, :, :], ALU.add)
                    for j in range(TPB):
                        nc.vector.drain()
                        last = nc.vector.tensor_tensor(carry[:, j + 1, :], carry[:, j, :], mask[:, j, :], ALU.add)
                    last.then_inc(mask_ready, 1)
                    norm.dve_copy_t(i + 1, 1 - k)
                    dve.wait_ge(pos_ready, i + 1)
                    nc.vector.tensor_tensor(
                        product[:, :, :, :], pick[:, :, :, :],
                        pos_ps[:, 0:TPB * E].rearrange("p (j e) -> p j e", e=E).unsqueeze(1).broadcast_to([P, TOP, TPB, E]),
                        ALU.mult).then_inc(pos_read, 1)
                    nc.vector.drain()
                    nc.vector.tensor_reduce(pos[:, :, :], product[:, :, :, :], AX.X, ALU.add)
                    nc.vector.drain()
                    nc.vector.tensor_scalar(valid[:, i, :, :], pos[:, :, :], float(CAP), None, ALU.is_lt)
                    nc.vector.tensor_scalar(over[:, :, :], pos[:, :, :], float(CAP), float(2 * E * CAP), ALU.is_ge, ALU.mult)
                    nc.vector.tensor_scalar(near[:, :, :], pos[:, :, :], float(CAP - 1), None, ALU.min)
                    nc.vector.tensor_scalar(expert[:, :, :], expert[:, :, :], float(CAP), None, ALU.mult)
                    nc.vector.drain()
                    nc.vector.tensor_tensor(place[:, i, :, :], expert[:, :, :], near[:, :, :], ALU.add)
                    nc.vector.tensor_tensor(over[:, :, :], over[:, :, :], pos[:, :, :], ALU.add)
                    nc.vector.drain()
                    nc.vector.tensor_tensor(target[k][:, :, :], over[:, :, :], expert[:, :, :], ALU.add).then_inc(target_ready, 1)


def experts(core, sparse, name, b1, E, H, R, w1_sb, w2_sb, b2_sb, w_loaded, load_weights):
    nc = core.nc
    HC = H // P
    HB = 2
    ctx = ExitStack()
    with ctx:
        sb = lambda n, s, dt=FP32: ctx.enter_context(nc.sbuf_tensor(f"{name}_{n}", s, dt))
        ps = lambda n, s: ctx.enter_context(nc.psum_tensor(f"{name}_{n}", s, FP32))
        sem = lambda n: core.semaphore(f"{name}_{n}")
        ones = sb("e_ones", [1, P])
        b1_rows = sb("b1_rows", [E, H])
        b1_t = sb("b1_t", [P, HC, E])
        b1_e = [sb(f"b1_e{k}", [P, HC]) for k in range(2)]
        rows = [sb(f"rows{s}", [P, D]) for s in range(R)]
        rows_t = [sb(f"rows_t{k}", [P, DC, P]) for k in range(2)]
        h_t = [sb(f"h_t{k}", [P, HC, P]) for k in range(2)]
        y_sb = [sb(f"y{k}", [P, D]) for k in range(2)]
        t_ps = ps("t_ps", [P, 512])
        h_ps = [ps(f"h_ps{n}", [P, 512]) for n in range(HC // HB)]
        y_ps = [ps(f"y_ps{k}", [P, 512]) for k in range(2)]

        b1_loaded = sem("b1_loaded")
        consts = sem("e_consts")
        b1_turned = sem("b1_turned")
        b1_copied = sem("b1_copied")
        b1_ready = sem("b1_ready")
        x_loaded = [sem(f"x_loaded{s}") for s in range(R)]
        x_turned = sem("x_turned")
        x_copied = sem("x_copied")
        h_ready = sem("h_ready")
        gelu_done = sem("gelu_done")
        y_ready = sem("e_y_ready")
        y_copied = sem("y_copied")
        carried = sem("e_carried")
        y_stored = [sem(f"y_stored{k}") for k in range(2)]
        block = ctx.enter_context(nc.Block())

        @block.sync
        def _(sp):
            def load_rows(s, e):
                sp.dma_start(rows[s][:, :], sparse.rows_in[bass.ds(e * CAP, CAP), :]).then_inc(x_loaded[s], 16)
            sp.sem_inc(y_ready, R)
            sp.dma_start(b1_rows[:, :], b1).then_inc(b1_loaded, 16)
            for s in range(R):
                load_rows(s, s)
            with sp.Fori(1, E // R) as turn:
                for s in range(R):
                    e = turn * R + s
                    sp.wait_ge(y_ready, e + 1)
                    load_weights(sp, s, e)
                    load_rows(s, e)

        @block.gpsimd
        def _(pool):
            nc.gpsimd.memset(ones[:, :], 1.0).then_inc(consts, 1)
            with pool.Fori(0, E // 2) as pair:
                for k in range(2):
                    e = pair * 2 + k
                    pool.wait_ge(y_copied, e + 1)
                    pool.sem_inc(carried, 1)
                    pool.dma_start(sparse.rows_out[bass.ds(e * CAP, CAP), :], y_sb[k][:, :]).then_inc(y_stored[k], 16)
            for k in range(2):
                pool.wait_ge(y_stored[k], 16 * (E // 2))

        @block.tensor
        def _(pe):
            def turn_rows(turn, s):
                e = turn * R + s
                pe.wait_ge(x_loaded[s], (turn + 1) * 16)
                if due(e):
                    pe.wait_ge(x_copied, e)
                for c in range(DC):
                    last = nc.tensor.transpose(t_ps[:, c * P:(c + 1) * P], rows[s][:, c * P:(c + 1) * P],
                                               core.ident[:, :])
                last.then_inc(x_turned, 1)

            def up(turn, s):
                e, k = turn * R + s, s % 2
                pe.wait_ge(w_loaded[s], (turn + 1) * 48)
                pe.wait_ge(x_copied, e + 1)
                for n in range(HC):
                    if n % HB == 0:
                        pe.wait_ge(gelu_done, e * HC + n + HB)
                    for c in range(DC):
                        last = nc.tensor.matmul(h_ps[n // HB][:, (n % HB) * P:(n % HB + 1) * P], w1_sb[s][:, c, n * P:(n + 1) * P],
                                                rows_t[k][:, c, :], start=c == 0, stop=c == DC - 1)
                    if n % HB == HB - 1:
                        last.then_inc(h_ready, 1)

            def down(turn, s):
                e, k = turn * R + s, s % 2
                if due(e - 1):
                    pe.wait_ge(y_copied, e - 1)
                nc.tensor.matmul(y_ps[k][:, 0:D], ones[:, :], b2_sb[s][:, :], start=True, stop=False)
                for n in range(HC):
                    pe.wait_ge(gelu_done, HC + e * HC + n + 1)
                    last = nc.tensor.matmul(y_ps[k][:, 0:D], h_t[k][:, n, :], w2_sb[s][:, n, :],
                                            start=False, stop=n == HC - 1)
                last.then_inc(y_ready, 1)

            pe.wait_ge(consts, 1)
            pe.wait_ge(b1_loaded, 16)
            for n in range(HC):
                last = nc.tensor.transpose(h_ps[0][:, n * E:(n + 1) * E],
                                           b1_rows[:, n * P:(n + 1) * P], core.ident[0:E, 0:E])
            last.then_inc(b1_turned, 1)
            pe.wait_ge(b1_copied, 1)
            turn_rows(0, 0)
            for s in range(R):
                up(0, s)
                turn_rows((s + 1) // R, (s + 1) % R)
                down(0, s)
            with pe.Fori(1, E // R - 1) as turn:
                for s in range(R):
                    up(turn, s)
                    turn_rows(turn + (s + 1) // R, (s + 1) % R)
                    down(turn, s)
            for s in range(R):
                up(E // R - 1, s)
                if s + 1 < R:
                    turn_rows(E // R - 1, s + 1)
                down(E // R - 1, s)

        @block.scalar
        def _(act):
            act.sem_inc(gelu_done, HC)
            with act.Fori(0, E // 2) as pair:
                for k in range(2):
                    e = pair * 2 + k
                    act.wait_ge(b1_ready, e + 1)
                    act.wait_ge(y_ready, e + R - 1)
                    for n in range(HC):
                        if n % HB == 0:
                            act.wait_ge(h_ready, e * (HC // HB) + n // HB + 1)
                        nc.scalar.activation(h_t[k][:, n, :], h_ps[n // HB][:, (n % HB) * P:(n % HB + 1) * P], ACT.Gelu,
                                             bias=b1_e[k][:, n:n + 1]).then_inc(gelu_done, 1)

        @block.vector
        def _(dve):
            dve.wait_ge(b1_turned, 1)
            nc.vector.tensor_copy(b1_t[:, :, :], h_ps[0][:, :].rearrange("p (n e) -> p n e", e=E)).then_inc(b1_copied, 1)
            nc.vector.drain()
            def prepare(e, k):
                dve.wait_ge(gelu_done, HC + e * HC)
                nc.vector.tensor_copy(b1_e[k][:, :], b1_t[:, :, e]).then_inc(b1_ready, 1)
                dve.wait_ge(x_turned, e + 1)
                nc.vector.tensor_copy(rows_t[k][:, :, :],
                                      t_ps[:, 0:D].rearrange("p (c q) -> p c q", q=P)).then_inc(x_copied, 1)

            def finish(e, k, stored):
                dve.wait_ge(y_ready, R + e + 1)
                dve.wait_ge(y_stored[k], stored)
                nc.vector.tensor_copy(y_sb[k][:, :], y_ps[k][:, 0:D]).then_inc(y_copied, 1)

            prepare(0, 0)
            with dve.Fori(0, E // 2 - 1) as pair:
                for k in range(2):
                    prepare(pair * 2 + k + 1, 1 - k)
                    finish(pair * 2 + k, k, pair * 16)
            prepare(E - 1, 1)
            for k in range(2):
                finish(E - 2 + k, k, (E // 2 - 1) * 16)


def combine(core, sparse, name, best, valid, place):
    nc = core.nc
    NK = TPB * TOP
    ctx = ExitStack()
    with ctx:
        sb = lambda n, s, dt=FP32: ctx.enter_context(nc.sbuf_tensor(f"{name}_{n}", s, dt))
        sem = lambda n: core.semaphore(f"{name}_{n}")
        shifted = sb("shifted", [P, B, TOP, TPB])
        total = sb("total", [P, B, 1, TPB])
        index = [sb(f"index{k}", [P, NK], U32) for k in range(2)]
        gate = [sb(f"gate{k}", [P, NK]) for k in range(2)]
        back = [sb(f"back{k}", [P, NK, D]) for k in range(2)]
        shift_ready = sem("c_shift")
        exp_ready = sem("c_exp")
        index_ready = sem("c_index")
        carried = sem("c_carried")
        gathered = [sem(f"c_gathered{k}") for k in range(2)]
        used = sem("c_used")
        block = ctx.enter_context(nc.Block())

        @block.scalar
        def _(act):
            act.wait_ge(shift_ready, 1)
            nc.scalar.activation(shifted[:, :, :, :], shifted[:, :, :, :], ACT.Exp).then_inc(exp_ready, 1)

        @block.gpsimd
        def _(pool):
            with pool.Fori(0, B // 2) as pair:
                for k in range(2):
                    i = pair * 2 + k
                    pool.wait_ge(index_ready, i + 1)
                    pool.sem_inc(carried, 1)
                    for n in range(NK):
                        nc.gpsimd.indirect_dma_start(
                            out=back[k][:, n, :], out_offset=None, in_=sparse.rows_out,
                            in_offset=bass.IndirectOffsetOnAxis(ap=index[k][:, n:n + 1], axis=0),
                            bounds_check=sparse.rows_out.shape[0] - 1, oob_is_err=False).then_inc(gathered[k], 16)

        @block.vector
        def _(dve):
            def fetch(i, k):
                nc.vector.drain()
                nc.vector.tensor_copy(gate[k][:, :], shifted[:, i, :, :].rearrange("p r j -> p (r j)"))
                nc.vector.tensor_copy(index[k][:, :], place[:, i, :, :].rearrange("p r j -> p (r j)")).then_inc(index_ready, 1)

            def use(i, k, count):
                nc.vector.drain()
                dve.wait_ge(gathered[k], count)
                for r in range(TOP):
                    if r:
                        nc.vector.drain()
                    for j in range(TPB):
                        xt = core.tile(i + 1, j)
                        nc.vector.scalar_tensor_tensor(out=xt, in0=back[k][:, r * TPB + j, :],
                                                       scalar=gate[k][:, r * TPB + j:r * TPB + j + 1], in1=xt,
                                                       op0=ALU.mult, op1=ALU.add)

            nc.vector.tensor_tensor(shifted[:, :, :, :], best[:, :, :, :],
                                    best[:, :, 0:1, :].broadcast_to([P, B, TOP, TPB]), ALU.subtract).then_inc(shift_ready, 1)
            dve.wait_ge(exp_ready, 1)
            nc.vector.tensor_tensor(total[:, :, :, :], shifted[:, :, 0:1, :], shifted[:, :, 1:2, :], ALU.add)
            nc.vector.drain()
            nc.vector.tensor_tensor(total[:, :, :, :], total[:, :, :, :], shifted[:, :, 2:3, :], ALU.add)
            nc.vector.drain()
            nc.vector.reciprocal(total[:, :, :, :], total[:, :, :, :])
            nc.vector.drain()
            nc.vector.tensor_tensor(shifted[:, :, :, :], shifted[:, :, :, :],
                                    total[:, :, :, :].broadcast_to([P, B, TOP, TPB]), ALU.mult)
            nc.vector.drain()
            nc.vector.scalar_tensor_tensor(
                out=shifted[:, :, :, :].rearrange("p b r j -> p (b r j)"),
                in0=shifted[:, :, :, :].rearrange("p b r j -> p (b r j)"), scalar=0.5,
                in1=valid[:, :, :, :].rearrange("p b r j -> p (b r j)"), op0=ALU.mult, op1=ALU.mult)
            for k in range(2):
                fetch(k, k)
            with dve.Fori(0, B // 2 - 1) as pair:
                for k in range(2):
                    i = pair * 2 + k
                    use(i, k, (pair + 1) * (16 * NK))
                    fetch(i + 2, k)
            for k in range(2):
                use(B - 2 + k, k, (B // 2) * (16 * NK))



WIN = 32


def attn0_phase(core, name, skew_dram, w_disp, b_disp, w_val, b_val, rel_pos, w_state, b_state, w_strain,
                b_strain, w_state_i, w_state_j, w_pos, w_bond, b_bond, w_damage, b_damage,
                w_damage_out, b_damage_out, w_cproj, b_cproj):
    nc = core.nc
    BD = w_state.shape[0]
    NH = D // BD
    HH = P // BD
    HALF = NH // HH
    PAD = WIN
    DG = 4
    NQ = WIN // DG
    STEPS = HALF * NQ
    PG = P // HH
    GSTEPS = PG // DG
    GROUPS = STEPS // GSTEPS
    SPAN = 2 * WIN
    NBLK = S // WIN
    BPT = P // WIN
    HP = NH // 2
    ctx = ExitStack()
    with ctx:
        sb = lambda n, s, dt=FP32: ctx.enter_context(nc.sbuf_tensor(f"{name}_{n}", s, dt))
        ps = lambda n, s: ctx.enter_context(nc.psum_tensor(f"{name}_{n}", s, FP32))
        sem = lambda n: core.semaphore(f"{name}_{n}")
        norm = Norm(core, ctx, name, pad=PAD)
        w_disp_sb = sb("w_disp", [P, DC, D])
        w_val_sb = sb("w_val", [P, DC, HP, 2, BD])
        w_out_sb = sb("w_out", [P, DC, D])
        b_out_sb = sb("b_out", [1, D])
        ones = sb("ones", [1, P])
        b_disp_sb = sb("b_disp", [P, HALF])
        b_val_sb = sb("b_val", [P, HP, 2, BD])
        bond_b = sb("bond_b", [P, 1])
        damage_b = sb("damage_b", [P, 1])
        STATE, STRAIN, STATE_I, STATE_J, DAMAGE = range(5)
        COLS = 5 * BD
        SM = COLS + 5 + WIN
        small = sb("small", [BD, SM])
        rel_t = sb("rel_t", [BD, WIN])
        w_pos_sb = sb("w_pos", [BD, BD])
        select = sb("select", [BD, HH, BD])
        small_rep = sb("small_rep", [P, SM])
        diag = sb("diag", [P, HH, BD])
        mats = [sb(f"mat{n}", [P, HH, BD]) for n in range(5)]
        neg_strain = sb("neg_strain", [P, HH, BD])
        col_bond = sb("col_bond", [P, 2 * PG - 1, HH])
        col_damage = sb("col_damage", [P, 2 * PG - 1, HH])
        sig = sb("sig", [P, S])
        logits = sb("logits", [P, S])
        inv_count = sb("inv_count", [P, S])
        early = sb("early", [P, WIN])
        disp = [sb(f"disp{h}", [P, S]) for h in range(HALF)]
        sum_a = sb("sum_a", [P, PAD + S])
        sum_b = sb("sum_b", [P, PAD + S])
        state = [sb(f"state{h}", [P, S]) for h in range(HALF)]
        a_sb = [[sb(f"a{k}{h}", [P, PAD + S]) for h in range(HALF)] for k in range(2)]
        c_sb = [[sb(f"c{k}{h}", [P, PAD + S]) for h in range(HALF)] for k in range(2)]
        q_sb = [[sb(f"q{k}{h}", [P, S]) for h in range(HALF)] for k in range(2)]
        f_sb = [[sb(f"f{k}{h}", [P, S]) for h in range(HALF)] for k in range(2)]
        bond_buf = [sb(f"bond_buf{k}", [P, DG, S]) for k in range(2)]
        dmg_buf = [sb(f"dmg_buf{k}", [P, DG, S]) for k in range(2)]
        bond = sb("bond", [P, TPB, NH, WIN])
        expd = sb("expd", [P, TPB, NH, WIN])
        top = sb("top", [P, TPB * NH, 1])
        inv_sum = [sb(f"inv_sum{k}", [P, TPB, NH]) for k in range(2)]
        skewed = sb("skewed", [P, TPB, NH * SPAN])
        turned = sb("turned", [P, HP, P])
        vals = sb("vals", [P, NBLK, HP, 2, BD])
        ctx_sb = sb("ctx", [P, D])
        ctx_t = sb("ctx_t", [P, DC, P])
        bond_ps = [ps(f"bond_ps{n}", [P, S]) for n in range(2)]
        dmg_ps = [ps(f"dmg_ps{n}", [P, S]) for n in range(2)]
        t_ps = ps("t_ps", [P, 512])
        o_ps = ps("o_ps", [P, 512])
        misc = ps("misc", [P, 512])
        pj = norm.tp

        loaded = sem("loaded")
        rel_loaded = sem("rel_loaded")
        zeroed = sem("zeroed")
        consts = sem("consts")
        tables_a = sem("tables_a")
        tables_b = sem("tables_b")
        tables = sem("tables")
        bond_pre = sem("bond_pre")
        dmg_pre = sem("dmg_pre")
        gelu_done = sem("gelu_done")
        chunk_used = sem("chunk_used")
        sig_done = sem("sig_done")
        combined = sem("combined")
        logits_copied = sem("logits_copied")
        inv_ready = sem("inv_ready")
        weights_stored = sem("weights_stored")
        logits_turned = sem("logits_turned")
        soft_ready = sem("soft_ready")
        exp_done = sem("exp_done")
        skew_stored = sem("skew_stored")
        skew_loaded = sem("skew_loaded")
        w_turned = sem("w_turned")
        w_copied = sem("w_copied")
        out_ready = sem("out_ready")
        ctx_ready = sem("ctx_ready")
        ctx_turned = sem("ctx_turned")
        ctx_copied = sem("ctx_copied")
        proj_ready = sem("proj_ready")
        proj_added = sem("proj_added")
        pj_ready = sem("pj_ready")
        pj_copied = sem("pj_copied")
        state_ready = sem("state_ready")
        val_ready = sem("val_ready")
        val_copied = sem("val_copied")
        block = ctx.enter_context(nc.Block())

        PJ = [(what, h) for what in ("disp", "u", "c", "a", "q") for h in range(HALF)]
        PJ_STEP = 3
        NPJ = len(PJ)
        T_STEP = 6

        def tile_at(q, step):
            x, odd = divmod(q - step, 2)
            return x if 0 <= x < TPB and not odd else None

        def window(x, d):
            first = x[:, d + 1:d + 1 + S]
            return bass.AP(tensor=first.tensor, offset=first.offset, ap=[first.ap[0], [1, DG], [1, S]])

        @block.sync
        def _(sp):
            def load(dst, src, **kind):
                sp.dma_start(dst, src, **kind).then_inc(loaded, 16)
            load(w_disp_sb[:, :, :], w_disp.rearrange("(c p) n -> p c n", p=P))
            load(w_val_sb[:, :, :, :, :].rearrange("p c h r d -> p c (h r d)"), w_val.rearrange("(c p) n -> p c n", p=P))
            load(w_out_sb[:, :, :], w_cproj.rearrange("(c p) n -> p c n", p=P))
            load(b_out_sb[:, :], b_cproj.rearrange("(o n) -> o n", o=1))
            load(b_disp_sb[:, :], b_disp.rearrange("(h p) -> p h", p=P), allow_slow_non_contiguous=True)
            load(b_val_sb[:, :, :, :].rearrange("p h r d -> p (h r d)"), b_val.partition_broadcast(P))
            load(bond_b[:, :], b_bond.partition_broadcast(P))
            load(damage_b[:, :], b_damage_out.partition_broadcast(P))
            for n, w in enumerate((w_state, w_strain, w_state_i, w_state_j, w_damage)):
                load(small[:, n * BD:(n + 1) * BD], w)
            load(small[:, COLS:COLS + 1], w_bond)
            load(small[:, COLS + 1:COLS + 2], w_damage_out)
            for n, b in enumerate((b_state, b_strain, b_damage)):
                load(small[:, COLS + 2 + n:COLS + 3 + n], b.rearrange("(d o) -> d o", o=1))
            sp.dma_start(rel_t[:, :], rel_pos.rearrange("w d -> d w"),
                         allow_slow_non_contiguous=True).then_inc(rel_loaded, 16)
            sp.dma_start(w_pos_sb[:, :], w_pos).then_inc(rel_loaded, 16)

            def skew_weights(j):
                sp.wait_ge(exp_done, j + 1)
                for a in range(BPT):
                    row = TPB * NH * SPAN
                    rows = bass.AP(tensor=skew_dram.tensor, offset=a * WIN * row + 1,
                                   ap=[[row + 1, WIN], [SPAN, TPB * NH], [1, WIN]])
                    sp.dma_start(rows, expd[a * WIN:(a + 1) * WIN, :, :, :].rearrange(
                        "p j h w -> p (j h) w")).then_inc(skew_stored, 16)
                sp.wait_ge(w_turned, 1 + j * TPB)
                sp.wait_ge(skew_stored, (j + 1) * 16 * BPT)
                sp.sem_inc(weights_stored, 1)
                sp.dma_start(skewed[:, :, :].rearrange("p j s -> p (j s)"), skew_dram).then_inc(skew_loaded, 16)

            sp.sem_inc(weights_stored, 1)
            with sp.Fori(0, B + 1) as j:
                skew_weights(j)

        LOADED = 16 * 18

        @block.gpsimd
        def _(pool):
            for k in range(2):
                nc.gpsimd.memset(norm.xn_t[k][:, :, 0:PAD], 0.0)
                nc.gpsimd.memset(inv_sum[k][:, :, :], 0.0)
                for h in range(HALF):
                    nc.gpsimd.memset(a_sb[k][h][:, 0:PAD], 0.0)
                    nc.gpsimd.memset(c_sb[k][h][:, 0:PAD], 0.0)
            nc.gpsimd.memset(vals[:, :, :, :, :], 0.0)
            nc.gpsimd.memset(sum_a[:, :], 0.0)
            nc.gpsimd.memset(sum_b[:, :], 0.0)
            nc.gpsimd.memset(bond[:, :, :, :], 0.0)
            nc.gpsimd.memset(col_bond[:, :, :], 0.0)
            nc.gpsimd.memset(col_damage[:, :, :], 0.0)
            nc.gpsimd.memset(ones[:, :], 1.0)
            nc.gpsimd.memset(early[:, :], 0.0)
            nc.gpsimd.memset(diag[:, :, :], 1.0)
            nc.gpsimd.iota(inv_count[:, :], pattern=[[1, S]], base=1, channel_multiplier=0,
                           allow_small_or_imprecise_dtypes=True).then_inc(consts, 1)
            pool.wait_ge(consts, 1)
            nc.gpsimd.affine_select(out=early[:, :], in_=early[:, :], compare_op=ALU.is_ge, fill=MASKED,
                                    base=-(WIN - 1), pattern=[[1, WIN]], channel_multiplier=1)
            nc.gpsimd.affine_select(out=diag[:, :, :], in_=diag[:, :, :], compare_op=ALU.is_ge, fill=0.0,
                                    base=0, pattern=[[-BD, HH], [0, BD]], channel_multiplier=1).then_inc(consts, 1)
            pool.wait_ge(consts, 2)
            nc.gpsimd.affine_select(out=diag[:, :, :], in_=diag[:, :, :], compare_op=ALU.is_ge, fill=0.0,
                                    base=BD - 1, pattern=[[BD, HH], [0, BD]], channel_multiplier=-1).then_inc(consts, 1)
            with pool.Fori(0, B // 2) as pair:
                for k in range(2):
                    i = pair * 2 + k
                    pool.wait_ge(pj_copied, (i + 1) * NPJ)
                    for q in range(STEPS):
                        h, dg = divmod(q, NQ)
                        pool.wait_ge(chunk_used, i * 2 * STEPS + 2 * q + 2)
                        d = dg * DG
                        nc.gpsimd.tensor_tensor(dmg_buf[q % 2][:, :, :], window(c_sb[k][h], d),
                                                f_sb[k][h][:, :].unsqueeze(1).broadcast_to([P, DG, S]),
                                                ALU.add).then_inc(dmg_pre, 1)

        @block.tensor
        def _(pe):
            def chunk(i, k, q, kind):
                g, part = divmod(q, GSTEPS)
                buf, bank, col = ((bond_buf, bond_ps, col_bond), (dmg_buf, dmg_ps, col_damage))[kind]
                if part == 0:
                    pe.wait_ge((logits_copied, sig_done)[kind], i * GROUPS + g + 1)
                pe.wait_ge(gelu_done, i * 2 * STEPS + 2 * q + kind + 1)
                for dd in range(DG):
                    d = part * DG + dd
                    last = nc.tensor.matmul(bank[g % 2][:, :], col[:, PG - 1 - d:2 * PG - 1 - d, :].rearrange("p d h -> p (d h)"),
                                            buf[q % 2][:, dd, :], start=d == 0, stop=d == PG - 1)
                last.then_inc(chunk_used, 1)

            def turn_logits(n, g):
                pe.wait_ge(combined, n + 3)
                for j in range(TPB):
                    last = nc.tensor.transpose(bond_ps[g % 2][:, j * P:(j + 1) * P], logits[:, j * P:(j + 1) * P],
                                               core.ident[:, :])
                last.then_inc(logits_turned, 1)

            def product(i, k, n):
                what, h = PJ[n]
                if due(i * NPJ + n):
                    pe.wait_ge(pj_copied, i * NPJ + n)
                mm = lambda w, x, first, end: nc.tensor.matmul(pj[:, :], w, x, start=first, stop=end)
                flat = lambda m: m[:, :, :].rearrange("p h d -> p (h d)")
                if what == "disp":
                    norm.wait_xn_t(pe, i)
                    for c in range(DC):
                        last = mm(w_disp_sb[:, c, h * P:(h + 1) * P], norm.xn_t[k][:, c, PAD:], c == 0, c == DC - 1)
                elif what == "u":
                    last = mm(flat(mats[STATE]), disp[h][:, :], True, True)
                elif what == "a":
                    pe.wait_ge(state_ready, i * HALF + h + 1)
                    mm(flat(mats[STRAIN]), disp[h][:, :], True, False)
                    last = mm(flat(mats[STATE_J]), state[h][:, :], False, True)
                elif what == "q":
                    mm(flat(neg_strain), disp[h][:, :], True, False)
                    last = mm(flat(mats[STATE_I]), state[h][:, :], False, True)
                else:
                    last = mm(flat(mats[DAMAGE]), disp[h][:, :], True, True)
                last.then_inc(pj_ready, 1)

            def values(i, k, n):
                for a in range(4):
                    at = (4 * n + a) * WIN
                    for r in range(2):
                        for c in range(DC):
                            last = nc.tensor.matmul(t_ps[r * SPAN:(r + 1) * SPAN, a * P:(a + 1) * P],
                                                    norm.xn_t[k][:, c, at:at + SPAN], w_val_sb[:, c, :, r, :],
                                                    start=c == 0, stop=c == DC - 1)
                last.then_inc(val_ready, 1)

            def turn(j, x, vals_before):
                if x == 0:
                    pe.wait_ge(skew_loaded, (j + 1) * 16)
                pe.wait_ge(val_copied, 1 + vals_before * 2)
                pe.wait_ge(ctx_ready, 1 + j * TPB + x)
                for hp in range(HP):
                    bank = (t_ps, o_ps)[hp // 4]
                    last = nc.tensor.transpose(bank[:, hp % 4 * P:(hp % 4 + 1) * P],
                                               skewed[:, x, hp * P:(hp + 1) * P], core.ident[:, :])
                last.then_inc(w_turned, 1)

            def sums(j, x):
                pe.wait_ge(w_copied, j * TPB + x + 1)
                for hp in range(HP):
                    for a in range(BPT):
                        last = nc.tensor.matmul(o_ps[a * WIN:(a + 1) * WIN, hp * 2 * BD:(hp + 1) * 2 * BD],
                                                turned[:, hp, a * WIN:(a + 1) * WIN],
                                                vals[:, x * BPT + a, hp, :, :].rearrange("p r d -> p (r d)"),
                                                start=True, stop=True)
                last.then_inc(out_ready, 1)

            def turn_ctx(j, x):
                pe.wait_ge(ctx_ready, j * TPB + x + 2)
                pe.wait_ge(proj_added, 1 + j * TPB + x)
                for c in range(DC):
                    last = nc.tensor.transpose(misc[:, c * P:(c + 1) * P], ctx_sb[:, c * P:(c + 1) * P], core.ident[:, :])
                last.then_inc(ctx_turned, 1)

            def project(j, x):
                pe.wait_ge(ctx_copied, j * TPB + x + 1)
                for c in range(DC):
                    nc.tensor.matmul(misc[:, D:2 * D], ctx_t[:, c, :], w_out_sb[:, c, :], start=c == 0, stop=False)
                nc.tensor.matmul(misc[:, D:2 * D], ones[:, :], b_out_sb[:, :], start=False, stop=True).then_inc(proj_ready, 1)

            def finish_step(j, q, live=1):
                x = tile_at(q, T_STEP)
                if x is not None:
                    turn(j, x, j * 4 + live * x)
                x = tile_at(q, T_STEP + 1)
                if x is not None:
                    sums(j, x)
                x = tile_at(q, T_STEP + 2)
                if x is not None:
                    turn_ctx(j, x)
                x = tile_at(q, T_STEP + 3)
                if x is not None:
                    project(j, x)

            def prepare_step(i, k, q):
                if q == 1:
                    if due(i * NPJ):
                        pe.wait_ge(pj_copied, i * NPJ)
                if q in (1, 2):
                    norm.pe_transpose(i, chunks=(q - 1,))
                if 0 <= q - PJ_STEP < NPJ:
                    product(i, k, q - PJ_STEP)

            pe.wait_ge(tables_a, 1)
            nc.tensor.matmul(pj[0:BD, 0:WIN], w_pos_sb[:, :], rel_t[:, :], start=True, stop=True).then_inc(pj_ready, 1)
            pe.wait_ge(tables_b, 1)
            nc.tensor.matmul(misc[:, 0:SM], select[:, :, :].rearrange("k h d -> k (h d)"), small[:, :],
                             start=True, stop=True).then_inc(proj_ready, 1)
            pe.wait_ge(tables, 1)
            for q in range(STEPS):
                prepare_step(0, 0, q)
            with pe.Fori(0, B // 2) as pair:
                for k in range(2):
                    i = pair * 2 + k
                    for q in range(STEPS):
                        chunk(i, k, q, 0)
                        if q % GSTEPS == 2:
                            g = (q // GSTEPS - 1) % GROUPS
                            turn_logits(i * GROUPS + q // GSTEPS - 1, g)
                        finish_step(i, q)
                        n = tile_at(q, T_STEP + 1)
                        if n is not None:
                            values(i, k, n)
                        prepare_step(i + 1, 1 - k, q)
                        chunk(i, k, q, 1)
            turn_logits(B * GROUPS - 1, GROUPS - 1)
            for q in range(STEPS):
                finish_step(B, q, live=0)

        @block.scalar
        def _(act):
            def gelu(i, q, kind):
                act.wait_ge((bond_pre, dmg_pre)[kind], i * STEPS + q + 1)
                buf = (bond_buf, dmg_buf)[kind][q % 2]
                nc.scalar.activation(buf[:, :, :], buf[:, :, :], ACT.Gelu).then_inc(gelu_done, 1)

            def sigmoid(n, g):
                act.wait_ge(chunk_used, 4 + (n + 1) * 2 * GSTEPS)
                act.wait_ge(combined, n + 2)
                nc.scalar.activation(sig[:, :], dmg_ps[g % 2][:, :], ACT.Sigmoid,
                                     bias=damage_b[:, 0:1]).then_inc(sig_done, 1)

            def exps(j):
                act.wait_ge(inv_ready, j + 1)
                act.wait_ge(weights_stored, j + 1)
                act.wait_ge(soft_ready, j + 1)
                nc.scalar.activation(expd[:, :, :, :], bond[:, :, :, :], ACT.Exp).then_inc(exp_done, 1)

            norm.act_std(0)
            with act.Fori(0, B) as i:
                for q in range(STEPS):
                    gelu(i, q, 0)
                    if q == 0:
                        norm.act_std(i + 1)
                    if q % GSTEPS == 1:
                        sigmoid(i * GROUPS + q // GSTEPS - 1, (q // GSTEPS - 1) % GROUPS)
                    if q == 4:
                        exps(i)
                    gelu(i, q, 1)
            sigmoid(B * GROUPS - 1, GROUPS - 1)
            exps(B)

        @block.vector
        def _(dve):
            def combine(n, g):
                dve.wait_ge(sig_done, n + 3)
                nc.vector.scalar_tensor_tensor(out=logits[:, :], in0=sig[:, :], scalar=-10.0,
                                               in1=bond_ps[g % 2][:, :], op0=ALU.mult,
                                               op1=ALU.add).then_inc(combined, 1)

            def copy_logits(n, g):
                h, places = g // 2, slice(g % 2 * PG, (g % 2 + 1) * PG)
                turned_g = bond_ps[g % 2][:, :].rearrange("p (j d h) -> p j h d", j=TPB, d=PG)
                dst = bond[:, :, h * HH:(h + 1) * HH, places]
                dve.wait_ge(logits_turned, n + 2)
                nc.vector.scalar_tensor_tensor(out=dst[:, 0, :, :], in0=turned_g[:, 0, :, :], scalar=bond_b[:, 0:1],
                                               in1=early[:, places].unsqueeze(1).broadcast_to([P, HH, PG]),
                                               op0=ALU.add, op1=ALU.add)
                nc.vector.tensor_scalar(dst[:, 1:, :, :], turned_g[:, 1:, :, :], bond_b[:, 0:1], None,
                                        ALU.add).then_inc(logits_copied, 1)

            def less_top(j):
                rows = bond[:, :, :, :].rearrange("p j h w -> p (j h) w")
                nc.vector.drain()
                nc.vector.tensor_reduce(top[:, :, 0], rows, AX.X, ALU.max)
                nc.vector.drain()
                nc.vector.tensor_tensor(rows, rows, top[:, :, :].broadcast_to([P, TPB * NH, WIN]),
                                        ALU.subtract).then_inc(soft_ready, 1)

            def inverse_sums(j, k):
                nc.vector.drain()
                dve.wait_ge(exp_done, j + 1)
                nc.vector.tensor_reduce(inv_sum[k][:, :, :].rearrange("p j h -> p (j h)"),
                                        expd[:, :, :, :].rearrange("p j h w -> p (j h) w"), AX.X, ALU.add)
                nc.vector.drain()
                nc.vector.reciprocal(inv_sum[k][:, :, :], inv_sum[k][:, :, :]).then_inc(inv_ready, 1)

            def add_projected(j, x):
                dve.wait_ge(proj_ready, 1 + j * TPB + x + 1)
                xt = core.tile(j, x)
                nc.vector.tensor_tensor(xt, misc[:, D:2 * D], xt, ALU.add).then_inc(proj_added, 1)

            def finish_step(j, k, q):
                if q == 2:
                    combine(j * GROUPS - 1, GROUPS - 1)
                if q == 3:
                    copy_logits(j * GROUPS - 1, GROUPS - 1)
                    less_top(j)
                if q == 6:
                    inverse_sums(j, k)
                x = tile_at(q, T_STEP + 1)
                if x is not None:
                    dve.wait_ge(w_turned, j * TPB + x + 2)
                    for half, bank in enumerate((t_ps, o_ps)):
                        last = nc.vector.tensor_copy(turned[:, half * 4:half * 4 + 4, :],
                                                     bank[:, :].rearrange("p (n t) -> p n t", t=P))
                    last.then_inc(w_copied, 1)
                x = tile_at(q, T_STEP + 2)
                if x is not None:
                    dve.wait_ge(out_ready, j * TPB + x + 1)
                    dve.wait_ge(ctx_turned, 1 + j * TPB + x)
                    nc.vector.tensor_tensor(ctx_sb[:, :].rearrange("p (h d) -> p h d", d=BD),
                                            o_ps[:, 0:D].rearrange("p (h d) -> p h d", d=BD),
                                            inv_sum[k][:, x, :].unsqueeze(2).broadcast_to([P, NH, BD]),
                                            ALU.mult).then_inc(ctx_ready, 1)
                x = tile_at(q, T_STEP + 3)
                if x is not None:
                    dve.wait_ge(ctx_turned, j * TPB + x + 2)
                    nc.vector.tensor_copy(ctx_t[:, :, :], misc[:, 0:D].rearrange("p (c q) -> p c q", q=P)).then_inc(ctx_copied, 1)
                x = tile_at(q, T_STEP + 4)
                if x is not None:
                    add_projected(j, x)
                if q == STEPS - 1:
                    add_projected(j, TPB - 1)

            def copy_product(i, k, n):
                what, h = PJ[n]
                bias = lambda m: small_rep[:, COLS + 2 + m:COLS + 3 + m]
                dve.wait_ge(pj_ready, 1 + i * NPJ + n + 1)
                if what == "disp":
                    last = nc.vector.tensor_scalar(disp[h][:, :], pj[:, :], b_disp_sb[:, h:h + 1], None, ALU.add)
                elif what == "u":
                    nc.vector.tensor_copy(sum_a[:, PAD:], pj[:, :])
                    last = nc.vector.tensor_scalar(state[h][:, :], pj[:, :], bias(0), None, ALU.subtract)
                elif what == "a":
                    last = nc.vector.tensor_copy(a_sb[k][h][:, PAD:], pj[:, :])
                elif what == "q":
                    last = nc.vector.tensor_scalar(q_sb[k][h][:, :], pj[:, :], bias(1), None, ALU.add)
                else:
                    nc.vector.tensor_copy(c_sb[k][h][:, PAD:], pj[:, :])
                    last = nc.vector.tensor_scalar(f_sb[k][h][:, :], pj[:, :], -1.0, bias(2), ALU.mult, ALU.add)
                last.then_inc(pj_copied, 1)
                if what == "u":
                    src, dst, step = sum_a, sum_b, 1
                    while step < WIN:
                        nc.vector.drain()
                        nc.vector.tensor_tensor(dst[:, step:], src[:, step:], src[:, 0:PAD + S - step], ALU.add)
                        src, dst, step = dst, src, 2 * step
                    nc.vector.drain()
                    nc.vector.tensor_tensor(dst[:, PAD:], src[:, PAD:], inv_count[:, :], ALU.mult)
                    nc.vector.drain()
                    nc.vector.tensor_tensor(state[h][:, :], dst[:, PAD:], state[h][:, :], ALU.subtract).then_inc(state_ready, 1)
                    nc.vector.drain()

            def prepare_step(i, k, q):
                if q == 0:
                    norm.dve_stats(i)
                if q == 1:
                    norm.dve_normalise(i)
                if q in (2, 3):
                    norm.dve_copy_t(i, k, guard=False, chunks=(q - 2,))
                if 0 <= q - PJ_STEP - 1 < NPJ:
                    copy_product(i, k, q - PJ_STEP - 1)

            def copy_values(i, n):
                dve.wait_ge(val_ready, i * 4 + n + 1)
                for r in range(2):
                    rows = slice(r * SPAN, (r + 1) * SPAN)
                    nc.vector.tensor_tensor(
                        vals[rows, 4 * n:4 * n + 4, :, r, :],
                        t_ps[rows, :].rearrange("p (a h d) -> p a h d", a=4, d=BD),
                        b_val_sb[rows, :, r, :].unsqueeze(1).broadcast_to([SPAN, 4, HP, BD]),
                        ALU.add).then_inc(val_copied, 1)

            def bond_chunk(i, k, q):
                h, dg = divmod(q, NQ)
                dve.wait_ge(chunk_used, i * 2 * STEPS + 2 * q + 1)
                for dd in range(DG):
                    d = dg * DG + dd
                    last = nc.vector.scalar_tensor_tensor(
                        out=bond_buf[q % 2][:, dd, :], in0=a_sb[k][h][:, d + 1:d + 1 + S],
                        scalar=small_rep[:, COLS + 5 + d:COLS + 6 + d], in1=q_sb[k][h][:, :],
                        op0=ALU.add, op1=ALU.add)
                last.then_inc(bond_pre, 1)

            dve.sem_inc(chunk_used, 4)
            for sem_from_1 in (sig_done, combined, logits_copied, inv_ready, w_turned, ctx_ready, ctx_turned,
                               proj_added, val_copied):
                dve.sem_inc(sem_from_1, 1)
            for banks in (bond_ps, dmg_ps):
                for n in range(2):
                    nc.vector.memset(banks[n][:, :], 0.0)
            nc.vector.tensor_copy(select[:, :, :], core.ident[0:BD, 0:BD].unsqueeze(1).broadcast_to([BD, HH, BD]))
            dve.wait_ge(consts, 3)
            nc.vector.tensor_scalar(inv_count[:, :], inv_count[:, :], float(WIN), None, ALU.min)
            nc.vector.drain()
            nc.vector.reciprocal(inv_count[:, :], inv_count[:, :])
            dve.wait_ge(loaded, LOADED)
            dve.wait_ge(rel_loaded, 32)
            nc.vector.drain().then_inc(tables_a, 1)
            dve.wait_ge(pj_ready, 1)
            nc.vector.tensor_copy(small[:, COLS + 5:], pj[0:BD, 0:WIN]).then_inc(tables_b, 1)
            dve.wait_ge(proj_ready, 1)
            nc.vector.tensor_copy(small_rep[:, :], misc[:, 0:SM])
            nc.vector.drain()
            for n in range(5):
                nc.vector.tensor_tensor(mats[n][:, :, :], diag[:, :, :],
                                        small_rep[:, n * BD:(n + 1) * BD].unsqueeze(1).broadcast_to([P, HH, BD]), ALU.mult)
            nc.vector.tensor_scalar(col_bond[:, PG - 1, :], diag[:, :, 0], small_rep[:, COLS:COLS + 1], None, ALU.mult)
            nc.vector.tensor_scalar(col_damage[:, PG - 1, :], diag[:, :, 0], small_rep[:, COLS + 1:COLS + 2], None, ALU.mult)
            nc.vector.drain()
            nc.vector.tensor_scalar(neg_strain[:, :, :], mats[STRAIN][:, :, :], -1.0, None, ALU.mult).then_inc(tables, 1)
            for q in range(STEPS):
                prepare_step(0, 0, q)
            with dve.Fori(0, B // 2) as pair:
                for k in range(2):
                    i = pair * 2 + k
                    for q in range(STEPS):
                        if q == 0:
                            nc.vector.drain()
                        bond_chunk(i, k, q)
                        g = q // GSTEPS - 1
                        if g >= 0 and q % GSTEPS == 2:
                            combine(i * GROUPS + g, g)
                        if g >= 0 and q % GSTEPS == 3:
                            copy_logits(i * GROUPS + g, g)
                        prepare_step(i + 1, 1 - k, q)
                        n = tile_at(q, T_STEP + 2)
                        if n is not None:
                            copy_values(i, n)
                        finish_step(i, 1 - k, q)
            for q in range(STEPS):
                finish_step(B, 1, q)


def macaron(nc, t, out, phases="f0 a0 f0 f1 a1 f1"):
    with ExitStack() as ctx:
        core = Core(nc, ctx)
        load_phase(core, t["L0_attn_x"])
        sparse = Sparse(core, ctx, t["L0_ffn_w1"].shape[0])
        if "f0" in phases:
            clear_rows(core, sparse.rows_in, "sparse")
        skew = nc.dram_tensor("skew", (P, TPB * (D // 16) * 2 * WIN), FP32, kind="Internal").ap()
        if "a0" in phases:
            clear_rows(core, skew.rearrange("p (r d) -> (p r) d", d=D), "skew")
        for n, ph in enumerate(phases.split()):
            core.free_semaphores()
            if ph == "f0":
                ffn0_phase(core, sparse, f"f0_{n}", *[t["L0_ffn_" + s] for s in
                           ("gate_w", "gate_b", "w1", "b1", "w2", "b2")])
            if ph == "f1":
                ffn1_phase(core, f"f1_{n}", *[t["L1_ffn_" + s] for s in
                           ("gate_W", "W1", "b1", "W2", "b2", "Ws1", "bs1", "Ws2", "bs2", "route_scale")])
            if ph == "a0":
                attn0_phase(core, f"a0_{n}", skew, *[t["L0_attn_" + s] for s in
                            ("w_disp", "b_disp", "w_val", "b_val", "rel_pos_emb", "w_state", "b_state", "w_strain",
                             "b_strain", "w_state_i", "w_state_j", "w_pos", "w_bond_out", "b_bond_out", "w_damage",
                             "b_damage", "w_damage_out", "b_damage_out", "w_cproj", "b_cproj")])
            if ph == "a1":
                attn1_phase(core, f"a1_{n}", *[t["L1_attn_" + s] for s in
                            ("Wq", "Wk", "Wv", "Wo", "bo", "rel_emb")])
        core.free_semaphores()
        store_phase(core, out)
        core.free_semaphores()


_L0_ATTN = ("x", "w_disp", "b_disp", "w_val", "b_val", "rel_pos_emb", "w_state", "b_state", "w_strain", "b_strain",
            "w_state_i", "w_state_j", "w_pos", "w_bond_out", "b_bond_out", "w_damage", "b_damage", "w_damage_out",
            "b_damage_out", "w_cproj", "b_cproj")
_L0_FFN = ("gate_w", "gate_b", "w1", "b1", "w2", "b2")
_L1_ATTN = ("Wq", "Wk", "Wv", "Wo", "bo", "rel_emb")
_L1_FFN = ("gate_W", "W1", "b1", "W2", "b2", "Ws1", "bs1", "Ws2", "bs2", "route_scale")
_INS = [part + n for part, names in (("L0_attn_", _L0_ATTN), ("L0_ffn_", _L0_FFN), ("L1_attn_", _L1_ATTN),
                                     ("L1_ffn_", _L1_FFN)) for n in names]


def kernel(**inputs):
    import numpy as _np
    import concourse.bacc as _bacc
    from concourse import mybir as _mybir
    from concourse.bass_utils import run_bass_kernel_spmd as _run

    nc = _bacc.Bacc("TRN2", target_bir_lowering=False, num_devices=1)
    arrays, tensors = {}, {}
    for name in _INS:
        a = _np.ascontiguousarray(inputs[name])
        a = a.reshape(a.shape or (1,))
        arrays[f"in_{name}_dram"] = a
        tensors[name] = nc.dram_tensor(f"in_{name}_dram", a.shape, _mybir.dt.from_np(a.dtype),
                                       kind="ExternalInput").ap()
    x = inputs["L0_attn_x"]
    out = nc.dram_tensor("out_0_dram", tuple(x.shape), _mybir.dt.float32, kind="ExternalOutput").ap()
    macaron(nc, tensors, out)
    r = _run(nc, [arrays], core_ids=[0])
    return r.results[0]["out_0_dram"]
```

```python
from contextlib import ExitStack

import numpy as np

import concourse.bass as bass
from concourse import mybir

FP32 = mybir.dt.float32
BF16 = mybir.dt.bfloat16
U32 = mybir.dt.uint32
ALU = mybir.AluOpType
ACT = mybir.ActivationFunctionType
AX = mybir.AxisListType

P = 128
B, S, D = 8, 512, 256
TPB = S // P
DC = D // P
EPS = 1e-5


def due(count):
    return not isinstance(count, int) or count > 0


class Core:

    def __init__(self, nc, ctx):
        self.nc = nc
        self.sems = []
        self.cleared = nc.alloc_semaphore("scratch_cleared")
        self.clears = 0
        self.x = ctx.enter_context(nc.sbuf_tensor("x_resid", [P, (B + 2) * TPB, D], FP32))
        self.ident = ctx.enter_context(nc.sbuf_tensor("ident", [P, P], FP32))

    def semaphore(self, name):
        self.sems.append(self.nc.alloc_semaphore(name))
        return self.sems[-1]

    def free_semaphores(self):
        self.nc.clear_and_free_semaphores(self.sems)
        self.nc.all_engine_barrier()
        self.sems = []

    def x_batch(self, i):
        return self.x[:, bass.ds((i + 1) * TPB, TPB), :]

    def tile(self, n, j):
        return self.x[:, n * TPB + j, :]


def load_phase(core, x_dram, scratch):
    nc = core.nc
    with ExitStack() as ctx:
        x_in = core.semaphore("x_in")
        zeroed = core.semaphore("zeroed")
        spare_zeroed = core.semaphore("spare_zeroed")
        block = ctx.enter_context(nc.Block())

        @block.sync
        def _(sp):
            sp.dma_start(core.x[:, TPB:(B + 1) * TPB, :],
                         x_dram.rearrange("b (j p) d -> p (b j) d", p=P)).then_inc(x_in, 16)
            sp.wait_ge(spare_zeroed, 1)
            per = TPB
            for rows in scratch:
                view = rows.rearrange("(n p r) d -> n p r d", p=P, r=per)
                for m in range(rows.shape[0] // (P * per)):
                    sp.dma_start(view[m], core.x[:, (B + 1) * TPB:, :]).then_inc(core.cleared, 16)
                    core.clears += 1
            sp.wait_ge(x_in, 16)

        @block.gpsimd
        def _(pool):
            nc.gpsimd.memset(core.x[:, (B + 1) * TPB:, :], 0.0).then_inc(spare_zeroed, 1)
            nc.gpsimd.memset(core.x[:, 0:TPB, :], 0.0)
            nc.gpsimd.memset(core.ident[:, :], 0.0).then_inc(zeroed, 1)
            pool.wait_ge(zeroed, 1)
            nc.gpsimd.affine_select(out=core.ident[:, :], in_=core.ident[:, :], compare_op=ALU.not_equal,
                                    fill=1.0, base=0, pattern=[[-1, P]], channel_multiplier=1)


def store_phase(core, out_dram):
    nc = core.nc
    with ExitStack() as ctx:
        stored = core.semaphore("stored")
        block = ctx.enter_context(nc.Block())

        @block.sync
        def _(sp):
            sp.dma_start(out_dram.rearrange("b (j p) d -> p (b j) d", p=P),
                         core.x[:, TPB:(B + 1) * TPB, :]).then_inc(stored, 16)
            sp.wait_ge(stored, 16)


class Norm:

    def __init__(self, core, ctx, name, xn_buffers=1, pad=0):
        nc = core.nc
        self.core, self.nc = core, nc
        sb = lambda n, s: ctx.enter_context(nc.sbuf_tensor(f"{name}_{n}", s, FP32))
        sem = lambda n: core.semaphore(f"{name}_{n}")
        self.stats = sb("stats", [P, TPB, 6])
        self.mean_var = sb("mean_var", [P, TPB, 2])
        self.var_eps = sb("var_eps", [P, TPB])
        self.std = sb("std", [P, TPB])
        self.rstd = sb("rstd", [P, TPB])
        self.xns = [sb(f"xn{k}", [P, TPB, D]) for k in range(xn_buffers)]
        self.pad = pad
        self.xn_t = [sb(f"xn_t{k}", [P, DC, pad + S]) for k in range(2)]
        self.tp = ctx.enter_context(nc.psum_tensor(f"{name}_tp", [P, S], FP32))
        self.var_ready = sem("var_ready")
        self.std_ready = sem("std_ready")
        self.xn_ready = sem("xn_ready")
        self.t_ready = sem("t_ready")
        self.t_copied = sem("t_copied")
        self.free = sem("xn_t_free")

    def dve_stats(self, i):
        nc = self.nc
        for j in range(TPB):
            nc.vector.bn_stats(self.stats[:, j, :], self.core.tile(i + 1, j))
        nc.vector.drain()
        for j in range(TPB):
            nc.vector.bn_aggr(self.mean_var[:, j, :], self.stats[:, j, :])
        nc.vector.drain()
        nc.vector.tensor_scalar(self.var_eps[:, :], self.mean_var[:, :, 1], EPS, None,
                                ALU.add).then_inc(self.var_ready, 1)

    def act_std(self, i):
        self.nc.scalar.wait_ge(self.var_ready, i + 1)
        self.nc.scalar.activation(self.std[:, :], self.var_eps[:, :], ACT.Sqrt).then_inc(self.std_ready, 1)

    def dve_normalise(self, i, k=0):
        nc = self.nc
        nc.vector.wait_ge(self.std_ready, i + 1)
        nc.vector.reciprocal(self.rstd[:, :], self.std[:, :])
        nc.vector.drain()
        for j in range(TPB):
            last = nc.vector.tensor_scalar(self.xns[k][:, j, :], self.core.tile(i + 1, j),
                                           self.mean_var[:, j, 0:1], self.rstd[:, j:j + 1],
                                           ALU.subtract, ALU.mult)
        last.then_inc(self.xn_ready, 1)

    def pe_transpose(self, i, k=0, chunks=range(DC)):
        nc = self.nc
        nc.tensor.wait_ge(self.xn_ready, i + 1)
        for c in chunks:
            if due(i * DC + c):
                nc.tensor.wait_ge(self.t_copied, i * DC + c)
            for j in range(TPB):
                last = nc.tensor.transpose(self.tp[:, j * P:(j + 1) * P], self.xns[k][:, j, c * P:(c + 1) * P],
                                           self.core.ident[:, :])
            last.then_inc(self.t_ready, 1)

    def dve_copy_t(self, i, k, guard=True, chunks=range(DC)):
        nc = self.nc
        if guard:
            if due(i):
                nc.vector.wait_ge(self.free, i)
        for c in chunks:
            nc.vector.wait_ge(self.t_ready, i * DC + c + 1)
            nc.vector.tensor_copy(self.xn_t[k][:, c, self.pad:], self.tp[:, :]).then_inc(self.t_copied, 1)

    def wait_xn_t(self, eng, i):
        eng.wait_ge(self.t_copied, (i + 1) * DC)



def ffn1_phase(core, name, gate_w, w1, b1, w2, b2, ws1, bs1, ws2, bs2, route_scale):
    nc = core.nc
    E, H = w1.shape[0], w1.shape[2]
    NE = E + 1
    UNITS = 2 * (NE + 1)
    YB = 4
    ctx = ExitStack()
    with ctx:
        sb = lambda n, s, dt=FP32: ctx.enter_context(nc.sbuf_tensor(f"{name}_{n}", s, dt))
        ps = lambda n, s: ctx.enter_context(nc.psum_tensor(f"{name}_{n}", s, FP32))
        sem = lambda n: core.semaphore(f"{name}_{n}")
        norm = Norm(core, ctx, name)
        gate_w_sb = sb("gate_w", [P, DC, E])
        w1_sb = sb("w1", [P, NE, DC, H])
        w2_sb = sb("w2", [P, NE, D])
        b1_sb = sb("b1", [P, NE])
        b2_sb = sb("b2", [NE, D])
        route_sb = sb("route", [P, 1])
        iota_e = sb("iota_e", [P, TPB, E])
        sig = sb("sig", [P, TPB, E])
        score = sb("score", [P, TPB, E])
        top_v = sb("top_v", [P, TPB, 8])
        top_i = sb("top_i", [P, TPB, 8], U32)
        top_f = sb("top_f", [P, TPB, 2])
        inv = sb("inv", [P, TPB, 1])
        part = [sb(f"part{r}", [P, TPB, E]) for r in range(2)]
        weight = sb("weight", [P, TPB, 2])
        gate = [sb(f"gate{k}", [P, TPB, NE]) for k in range(2)]
        gate_t = [sb(f"gate_t{k}", [NE, S]) for k in range(2)]
        h_t = [sb(f"h_t{k}", [P, S]) for k in range(2)]
        acc = sb("acc", [P, TPB, D])
        gate_ps = ps("gate_ps", [P, 512])
        h_ps = [ps(f"h_ps{k}", [P, S]) for k in range(2)]
        y_ps = [ps(f"y_ps{k}", [P, 2, D]) for k in range(YB)]

        gate_loaded = sem("gate_loaded")
        loaded = sem("loaded")
        const_ready = sem("const_ready")
        logits_ready = sem("logits_ready")
        sig_ready = sem("sig_ready")
        gate_ready = sem("gate_ready")
        gate_t_ready = sem("gate_t_ready")
        gate_t_copied = sem("gate_t_copied")
        h_ready = sem("h_ready")
        act_ready = sem("act_ready")
        y_ready = sem("y_ready")
        y_free = sem("y_free")
        block = ctx.enter_context(nc.Block())

        @block.sync
        def _(sp):
            def load(dst, src, **kind):
                sp.dma_start(dst, src, **kind).then_inc(loaded, 16)
            sp.dma_start(gate_w_sb[:, :, :], gate_w.rearrange("(c p) e -> p c e", p=P)).then_inc(gate_loaded, 16)
            sp.dma_start(route_sb[:, :], route_scale.partition_broadcast(P)).then_inc(gate_loaded, 16)
            for e in range(E):
                load(w1_sb[:, e, :, :], w1[e].rearrange("(c p) h -> p c h", p=P))
            load(w1_sb[:, E, :, :], ws1.rearrange("(c p) h -> p c h", p=P))
            load(w2_sb[:, 0:E, :], w2.rearrange("e h d -> h e d"))
            load(w2_sb[:, E, :], ws2)
            load(b1_sb[:, 0:E], b1.rearrange("e h -> h e"), allow_slow_non_contiguous=True)
            load(b1_sb[:, E:NE], bs1.rearrange("(h o) -> h o", o=1))
            load(b2_sb[0:E, :], b2)
            load(b2_sb[E:NE, :], bs2.rearrange("(o d) -> o d", o=1))
        LOADED = 16 * (E + 7)

        @block.gpsimd
        def _(pool):
            nc.gpsimd.iota(iota_e[:, :, :], pattern=[[0, TPB], [1, E]], base=0, channel_multiplier=0,
                           allow_small_or_imprecise_dtypes=True)
            for k in range(2):
                last = nc.gpsimd.memset(gate[k][:, :, E:NE], 1.0)
            last.then_inc(const_ready, 1)

        @block.tensor
        def _(pe):
            def logits(i, k):
                norm.wait_xn_t(pe, i)
                for j in range(TPB):
                    for c in range(DC):
                        last = nc.tensor.matmul(gate_ps[:, j * E:(j + 1) * E],
                                                norm.xn_t[k][:, c, j * P:(j + 1) * P],
                                                gate_w_sb[:, c, :], start=c == 0, stop=c == DC - 1)
                last.then_inc(logits_ready, 1)

            def turn_gates(i, k):
                pe.wait_ge(gate_ready, i + 1)
                for j in range(TPB):
                    last = nc.tensor.transpose(gate_ps[0:NE, j * P:(j + 1) * P], gate[k][:, j, :],
                                               core.ident[:, :])
                last.then_inc(gate_t_ready, 1)

            def up(i, k, e):
                n = i * NE + e
                pe.wait_ge(act_ready, n + 1)
                if e == 0:
                    norm.wait_xn_t(pe, i)
                for c in range(DC):
                    last = nc.tensor.matmul(h_ps[(k * NE + e) % 2][:, :], w1_sb[:, e, c, :],
                                            norm.xn_t[k][:, c, :], start=c == 0, stop=c == DC - 1)
                last.then_inc(h_ready, 1)

            def down(i, k, e):
                pe.wait_ge(act_ready, 2 + i * NE + e + 1)
                h = h_t[(k * NE + e) % 2]
                for half in range(2):
                    m = 2 * (e + 1) + half
                    pe.wait_ge(y_free, i * UNITS + m + 1)
                    for j in range(2):
                        t = 2 * half + j
                        last = nc.tensor.matmul(y_ps[m % YB][:, j, :], h[:, t * P:(t + 1) * P],
                                                w2_sb[:, e, :], start=True, stop=True)
                        if e == NE - 1 and t == 0:
                            last.then_inc(norm.free, 1)
                    last.then_inc(y_ready, 1)

            def biases(i, k):
                pe.wait_ge(gate_t_copied, i + 1)
                for half in range(2):
                    pe.wait_ge(y_free, i * UNITS + half + 1)
                    for j in range(2):
                        t = 2 * half + j
                        last = nc.tensor.matmul(y_ps[half][:, j, :], gate_t[k][:, t * P:(t + 1) * P],
                                                b2_sb[:, :], start=True, stop=True)
                    last.then_inc(y_ready, 1)

            norm.pe_transpose(0)
            pe.wait_ge(gate_loaded, 32)
            logits(0, 0)
            turn_gates(0, 0)
            pe.wait_ge(loaded, LOADED)
            with pe.Fori(0, B // 2) as pair:
                for k in range(2):
                    i = pair * 2 + k
                    up(i, k, 0)
                    biases(i, k)
                    for e in range(NE):
                        if e + 1 < NE:
                            up(i, k, e + 1)
                        down(i, k, e)
                        if e in (2, 3):
                            norm.pe_transpose(i + 1, chunks=(e - 2,))
                        if e == 4:
                            logits(i + 1, 1 - k)
                        if e == 6:
                            turn_gates(i + 1, 1 - k)

        @block.scalar
        def _(act):
            def sigmoid(i):
                act.wait_ge(logits_ready, i + 1)
                nc.scalar.activation(sig[:, :, :], gate_ps[:, 0:TPB * E].rearrange("p (j e) -> p j e", e=E),
                                     ACT.Sigmoid).then_inc(sig_ready, 1)

            def gelu(i, k, e):
                n = i * NE + e
                act.wait_ge(h_ready, n + 1)
                nc.scalar.activation(h_t[(k * NE + e) % 2][:, :], h_ps[(k * NE + e) % 2][:, :], ACT.Gelu,
                                     bias=b1_sb[:, e:e + 1]).then_inc(act_ready, 1)

            act.sem_inc(act_ready, 2)
            norm.act_std(0)
            sigmoid(0)
            act.wait_ge(loaded, LOADED)
            with act.Fori(0, B // 2) as pair:
                for k in range(2):
                    i = pair * 2 + k
                    for e in range(NE):
                        gelu(i, k, e)
                        if e == 1:
                            norm.act_std(i + 1)
                        if e == 5:
                            sigmoid(i + 1)

        @block.vector
        def _(dve):
            def gates(i, k):
                dve.wait_ge(sig_ready, i + 1)
                nc.vector.tensor_scalar(score[:, :, :], sig[:, :, :], route_sb[:, 0:1], None, ALU.mult)
                nc.vector.drain()
                for j in range(TPB):
                    nc.vector.max(top_v[:, j, :], score[:, j, :])
                nc.vector.drain()
                for j in range(TPB):
                    nc.vector.max_index(top_i[:, j, :], top_v[:, j, :], score[:, j, :])
                nc.vector.tensor_tensor(inv[:, :, :], top_v[:, :, 0:1], top_v[:, :, 1:2], ALU.add)
                nc.vector.drain()
                nc.vector.reciprocal(inv[:, :, :], inv[:, :, :])
                nc.vector.tensor_copy(top_f[:, :, :], top_i[:, :, 0:2])
                nc.vector.drain()
                nc.vector.tensor_tensor(weight[:, :, :], top_v[:, :, 0:2],
                                        inv[:, :, :].broadcast_to([P, TPB, 2]), ALU.mult)
                for r in range(2):
                    nc.vector.tensor_tensor(part[r][:, :, :], iota_e[:, :, :],
                                            top_f[:, :, r:r + 1].broadcast_to([P, TPB, E]), ALU.is_equal)
                nc.vector.drain()
                for r in range(2):
                    nc.vector.tensor_tensor(part[r][:, :, :], part[r][:, :, :],
                                            weight[:, :, r:r + 1].broadcast_to([P, TPB, E]), ALU.mult)
                nc.vector.drain()
                nc.vector.tensor_tensor(gate[k][:, :, 0:E], part[0][:, :, :], part[1][:, :, :],
                                        ALU.add).then_inc(gate_ready, 1)

            def copy_gates(i, k):
                dve.wait_ge(gate_t_ready, i + 1)
                nc.vector.tensor_copy(gate_t[k][:, :], gate_ps[0:NE, :]).then_inc(gate_t_copied, 1)

            def add(i, k, n):
                nc.vector.drain()
                for half in range(2):
                    m = 2 * n + half
                    dve.wait_ge(y_ready, i * UNITS + m + 1)
                    y = y_ps[m % YB]
                    if n == 0:
                        last = nc.vector.tensor_copy(acc[:, 2 * half:2 * half + 2, :], y[:, :, :])
                    else:
                        for j in range(2):
                            t = 2 * half + j
                            last = nc.vector.scalar_tensor_tensor(
                                out=acc[:, t, :], in0=y[:, j, :], scalar=gate[k][:, t, n - 1:n],
                                in1=acc[:, t, :], op0=ALU.mult, op1=ALU.add)
                    last.then_inc(y_free, 1)

            dve.sem_inc(y_free, YB)
            dve.sem_inc(norm.free, 1)
            norm.dve_stats(0)
            norm.dve_normalise(0)
            norm.dve_copy_t(0, 0)
            dve.wait_ge(gate_loaded, 32)
            dve.wait_ge(const_ready, 1)
            gates(0, 0)
            copy_gates(0, 0)
            with dve.Fori(0, B // 2) as pair:
                for k in range(2):
                    i = pair * 2 + k
                    for n in range(NE + 1):
                        add(i, k, n)
                        if n == 1:
                            norm.dve_stats(i + 1)
                        if n == 2:
                            norm.dve_normalise(i + 1)
                        if n in (3, 4):
                            norm.dve_copy_t(i + 1, 1 - k, chunks=(n - 3,))
                        if n == 5:
                            gates(i + 1, 1 - k)
                        if n == 7:
                            copy_gates(i + 1, 1 - k)
                    nc.vector.drain()
                    nc.vector.scalar_tensor_tensor(out=core.x_batch(i), in0=acc[:, :, :], scalar=0.5,
                                                   in1=core.x_batch(i), op0=ALU.mult, op1=ALU.add)



MASKED = -1e30


def attn1_phase(core, name, parts_dram, wq, wk, wv, wo, bo, rel_emb):
    nc = core.nc
    NH = 16
    HD = D // NH
    CLIP = rel_emb.shape[0] - 1
    HG = 4
    QT = NH // HG
    NPJ = 2 * DC
    PAIRS = [(a, b) for a in range(3) for b in range(3) if a + b < 4]
    SCALE = HD ** -0.5
    UNITS = TPB * NH
    PR = 16
    LAG = 4
    TR = 5
    AHEAD = 4
    VC = 32
    TB = 2
    BY_ACT = [m % 4 in (0, 2, 3) for m in range(UNITS)]
    BEFORE = [(m + 1 - sum(BY_ACT[:m + 1]), sum(BY_ACT[:m + 1])) for m in range(UNITS)]
    N_DVE, N_ACT = BEFORE[-1]
    ctx = ExitStack()
    with ctx:
        sb = lambda n, s, dt=FP32: ctx.enter_context(nc.sbuf_tensor(f"{name}_{n}", s, dt))
        ps = lambda n, s: ctx.enter_context(nc.psum_tensor(f"{name}_{n}", s, FP32))
        sem = lambda n: core.semaphore(f"{name}_{n}")
        norm = Norm(core, ctx, name)
        wqk_sb = [sb(f"w{n}", [P, DC, D]) for n in "qk"]
        wv_sb = sb("wv", [P, DC, D])
        wo_sb = sb("wo", [P, DC, D])
        bo_sb = sb("bo", [1, D])
        ones = sb("ones", [1, P])
        rel_sb = sb("rel", [P, CLIP + 1])
        factor = sb("factor", [P, S])
        mask_f = sb("mask_f", [P, P])
        mask_b = sb("mask_b", [P, P], BF16)
        ident_b = sb("ident_b", [P, P], BF16)
        parts = sb("parts", [P, NPJ, 3, S], BF16)
        rest = [sb(f"rest{k}", [P, S]) for k in range(2)]
        q_s = [sb(f"q_s{k}", [P, NH, S], BF16) for k in range(2)]
        k_s = [sb(f"k_s{k}", [P, NH, S], BF16) for k in range(2)]
        v_sb = [sb(f"v{k}", [P, TPB, NH, VC]) for k in range(2)]
        prob = sb("prob", [P, PR, S])
        dist, hit = prob[:, 0, :], prob[:, 1, :]
        top = sb("top", [P, PR // HG, HG])
        neg_top = sb("neg_top", [P, PR // HG, HG])
        prob_t = sb("prob_t", [P, TR, S])
        inv = sb("inv", [P, NH, 1])
        o_sb = sb("o", [P, S])
        ctx_sb = sb("ctx", [P, D])
        ctx_t = sb("ctx_t", [P, DC, P])
        s_ps = [ps(f"s_ps{k}", [P, S]) for k in range(HG)]
        t_ps = [ps(f"t_ps{k}", [P, S]) for k in range(TB)]
        o_ps = ps("o_ps", [P, S])
        misc = norm.tp

        loaded = sem("loaded")
        pj_ready = sem("pj_ready")
        pj_taken = sem("pj_taken")
        split_begun = sem("split_begun")
        middle_ready = sem("middle_ready")
        parts_ready = sem("parts_ready")
        parts_stored = sem("parts_stored")
        parts_loaded = sem("parts_loaded")
        consts = sem("consts")
        mask_ready = sem("mask_ready")
        v_ready = sem("v_ready")
        v_dve = sem("v_dve")
        v_act = sem("v_act")
        qk_ready = sem("qk_ready")
        s_free = sem("s_free")
        groups_begun = sem("groups_begun")
        top_ready = sem("top_ready")
        exp_ready = sem("exp_ready")
        turned = sem("turned")
        t_dve = sem("t_dve")
        t_act = sem("t_act")
        pv_done = sem("pv_done")
        o_copied = sem("o_copied")
        o_turned = sem("o_turned")
        ctx_ready = sem("ctx_ready")
        ctx_turned = sem("ctx_turned")
        ctx_copied = sem("ctx_copied")
        out_ready = sem("out_ready")
        out_added = sem("out_added")
        block = ctx.enter_context(nc.Block())

        PJ_M = [2 * NH + 2 * n for n in range(NPJ)]
        V_M = UNITS - 7

        @block.sync
        def _(sp):
            def load(dst, src):
                sp.dma_start(dst, src).then_inc(loaded, 16)
            load(wv_sb[:, :, :], wv.rearrange("(c p) n -> p c n", p=P))
            load(wo_sb[:, :, :], wo.rearrange("(c p) n -> p c n", p=P))
            load(bo_sb[:, :], bo.rearrange("(o n) -> o n", o=1))
            load(rel_sb[:, :], rel_emb.partition_broadcast(P))
            for dst, src in zip(wqk_sb, (wq, wk)):
                load(dst[:, :, :], src.rearrange("(c p) n -> p c n", p=P))

            def spread(i, k):
                for n in range(NPJ):
                    c = n % DC
                    sp.wait_ge(parts_ready, i * NPJ + n + 1)
                    sp.dma_start(parts_dram[n // DC, :, c * P:(c + 1) * P, :].rearrange("a p s -> p a s"),
                                 parts[:, n, :, :]).then_inc(parts_stored, 16)
                sp.wait_ge(parts_stored, (i + 1) * NPJ * 16)
                for which, dst in enumerate((q_s[k], k_s[k])):
                    for block_row, pair_of_parts in enumerate(PAIRS):
                        sp.dma_start(dst[block_row * HD:(block_row + 1) * HD, :, :],
                                     parts_dram[which, pair_of_parts[which], :, :].rearrange(
                                         "(h r) s -> r h s", r=HD)).then_inc(parts_loaded, 16)

            spread(0, 0)
            with sp.Fori(0, B // 2) as pair:
                for k in range(2):
                    spread(pair * 2 + k + 1, 1 - k)
        LOADED = 16 * 6
        PARTS = 16 * 2 * len(PAIRS)

        @block.gpsimd
        def _(pool):
            nc.gpsimd.memset(ones[:, :], 1.0)
            for v in v_sb:
                nc.gpsimd.memset(v[:, :, :, HD:HD + 1], 1.0)
                nc.gpsimd.memset(v[:, :, :, HD + 1:VC], 0.0)
            nc.gpsimd.iota(dist, pattern=[[-1, S]], base=S - P, channel_multiplier=1,
                           allow_small_or_imprecise_dtypes=True)
            nc.gpsimd.memset(mask_f[:, :], 0.0).then_inc(consts, 1)
            pool.wait_ge(consts, 1)
            nc.gpsimd.affine_select(out=mask_f[:, :], in_=mask_f[:, :], compare_op=ALU.is_ge,
                                    fill=MASKED, base=0, pattern=[[-1, P]],
                                    channel_multiplier=1).then_inc(consts, 1)

            def split(i):
                for n in range(NPJ):
                    pool.wait_ge(pj_taken, i * NPJ + n + 1)
                    pool.sem_inc(split_begun, 1)
                    nc.gpsimd.tensor_copy(parts[:, n, 1, :], rest[n % 2][:, :]).then_inc(middle_ready, 1)
                    pool.wait_ge(middle_ready, i * NPJ + n + 1)
                    nc.gpsimd.tensor_tensor(parts[:, n, 2, :], rest[n % 2][:, :], parts[:, n, 1, :],
                                            ALU.subtract).then_inc(parts_ready, 1)

            with pool.Fori(0, B + 1) as i:
                split(i)

        @block.tensor
        def _(pe):
            def project(i, k, n):
                norm.wait_xn_t(pe, i)
                if n:
                    pe.wait_ge(pj_taken, i * NPJ + n)
                for c in range(DC):
                    last = nc.tensor.matmul(misc[:, :], wqk_sb[n // DC][:, c, n % DC * P:(n % DC + 1) * P],
                                            norm.xn_t[k][:, c, :], start=c == 0, stop=c == DC - 1)
                last.then_inc(pj_ready, 1)

            def project_v(i, k):
                pe.wait_ge(s_free, i * UNITS + HG)
                for half in range(2):
                    for j in range(2):
                        t = 2 * half + j
                        for c in range(DC):
                            last = nc.tensor.matmul(s_ps[half][:, j * D:(j + 1) * D],
                                                    norm.xn_t[k][:, c, t * P:(t + 1) * P], wv_sb[:, c, :],
                                                    start=c == 0, stop=c == DC - 1)
                    last.then_inc(v_ready, 1)

            def first_scores(i, k):
                pe.wait_ge(v_dve, i + 1)
                pe.wait_ge(v_act, i + 1)
                pe.wait_ge(parts_loaded, (i + 1) * PARTS)
                four_scores(i, k, 0)

            def scores(i, k, m):
                t, h = divmod(m, NH)
                width = (t + 1) * P
                pe.wait_ge(s_free, i * UNITS + m + 1)
                nc.tensor.matmul(s_ps[m % HG][:, 0:width], q_s[k][:, h, t * P:(t + 1) * P],
                                 k_s[k][:, h, 0:width], start=True, stop=False)
                nc.tensor.matmul(s_ps[m % HG][:, t * P:width], ident_b[:, :], mask_b[:, :],
                                 start=False, stop=True).then_inc(qk_ready, 1)

            def four_scores(i, k, m):
                for g in range(HG):
                    scores(i, k, m + g)

            def turn(i, m):
                t = m // NH
                pe.wait_ge(exp_ready, i * UNITS + m + 1)
                if m >= TB:
                    wait_copied(i, m - TB)
                for kb in range(t + 1):
                    last = nc.tensor.transpose(t_ps[m % TB][:, kb * P:(kb + 1) * P],
                                               prob[:, m % PR, kb * P:(kb + 1) * P], core.ident[:, :])
                last.then_inc(turned, 1)

            def wait_copied(i, m):
                dve_n, act_n = BEFORE[m]
                if BY_ACT[m]:
                    pe.wait_ge(t_act, i * N_ACT + act_n)
                else:
                    pe.wait_ge(t_dve, i * N_DVE + dve_n)

            def values(i, k, m):
                t, h = divmod(m, NH)
                group, g = divmod(h, HG)
                wait_copied(i, m)
                if h == 0:
                    pe.wait_ge(o_copied, i * TPB + t + 1)
                for kb in range(t + 1):
                    last = nc.tensor.matmul(o_ps[g * VC:(g + 1) * VC, group * P:(group + 1) * P],
                                            v_sb[k][:, kb, h, :], prob_t[:, m % TR, kb * P:(kb + 1) * P],
                                            start=kb == 0, stop=kb == t)
                last.then_inc(pv_done, 1)

            def turn_o(n):
                pe.wait_ge(o_copied, n + 1)
                pe.wait_ge(out_added, n + 1)
                for group in range(QT):
                    last = nc.tensor.transpose(misc[:, group * P:(group + 1) * P], o_sb[:, group * P:(group + 1) * P],
                                               core.ident[:, :])
                last.then_inc(o_turned, 1)

            def turn_ctx(n):
                pe.wait_ge(ctx_ready, n + 1)
                for c in range(DC):
                    last = nc.tensor.transpose(misc[:, c * P:(c + 1) * P], ctx_sb[:, c * P:(c + 1) * P],
                                               core.ident[:, :])
                last.then_inc(ctx_turned, 1)

            def output(n):
                pe.wait_ge(ctx_copied, n + 1)
                for c in range(DC):
                    nc.tensor.matmul(misc[:, D:2 * D], ctx_t[:, c, :], wo_sb[:, c, :],
                                     start=c == 0, stop=False)
                nc.tensor.matmul(misc[:, D:2 * D], ones[:, :], bo_sb[:, :], start=False,
                                 stop=True).then_inc(out_ready, 1)

            norm.pe_transpose(0)
            pe.wait_ge(loaded, LOADED)
            for n in range(NPJ):
                project(0, 0, n)
            project_v(0, 0)
            pe.wait_ge(mask_ready, 1)
            first_scores(0, 0)
            four_scores(0, 0, HG)
            with pe.Fori(0, B // 2) as pair:
                for k in range(2):
                    i = pair * 2 + k
                    for m in range(UNITS):
                        t, h = divmod(m, NH)
                        if m % HG == 2:
                            if m + 6 < UNITS:
                                four_scores(i, k, m + 6)
                            elif m + 6 > UNITS:
                                four_scores(i + 1, 1 - k, m + 6 - UNITS)
                        if m == V_M:
                            project_v(i + 1, 1 - k)
                        if m == V_M + 2:
                            first_scores(i + 1, 1 - k)
                        turn(i, m)
                        if m >= LAG:
                            values(i, k, m - LAG)
                        if h == 7:
                            if t == 1:
                                norm.wait_xn_t(pe, i + 1)
                            if t == 2:
                                pe.wait_ge(pj_taken, (i + 2) * NPJ)
                            turn_o(i * TPB + t)
                        if h == 11:
                            turn_ctx(i * TPB + t)
                        if h == 13:
                            output(i * TPB + t)
                        if m == NH:
                            pe.wait_ge(out_added, i * TPB + 2)
                            norm.pe_transpose(i + 1, chunks=(0,))
                        if m == NH + 3:
                            norm.pe_transpose(i + 1, chunks=(1,))
                        if m == PJ_M[0]:
                            pe.wait_ge(out_added, i * TPB + 3)
                        if m in PJ_M:
                            project(i + 1, 1 - k, PJ_M.index(m))
                    for m in range(UNITS - LAG, UNITS):
                        values(i, k, m)
            turn_o(B * TPB)
            turn_ctx(B * TPB)
            output(B * TPB)

        @block.scalar
        def _(act):
            def empty(i, m):
                t = m // NH
                act.wait_ge(turned, PR + i * UNITS + m + 1)
                act.wait_ge(pv_done, i * UNITS + m + 1)
                nc.scalar.copy(prob_t[:, m % TR, 0:(t + 1) * P],
                               t_ps[m % TB][:, 0:(t + 1) * P]).then_inc(t_act, 1)

            def exps(i, m):
                t, h = divmod(m, NH)
                if h % HG == 0:
                    act.wait_ge(top_ready, i * (UNITS // HG) + m // HG + 1)
                nc.scalar.activation(prob[:, m % PR, 0:(t + 1) * P], prob[:, m % PR, 0:(t + 1) * P],
                                     ACT.Exp, bias=neg_top[:, (m // HG) % (PR // HG), h % HG:h % HG + 1]).then_inc(exp_ready, 1)

            act.sem_inc(turned, PR)
            act.sem_inc(pv_done, TR)
            norm.act_std(0)

            def copy_v(i, k):
                act.wait_ge(v_ready, i * 2 + 2)
                nc.scalar.copy(v_sb[k][:, 2:4, :, 0:HD],
                               s_ps[1][:, :].rearrange("p (j h d) -> p j h d", j=2, d=HD)).then_inc(v_act, 1)

            copy_v(0, 0)
            for m in range(AHEAD):
                exps(0, m)
            with act.Fori(0, B // 2) as pair:
                for k in range(2):
                    i = pair * 2 + k
                    for m in range(UNITS):
                        if m + AHEAD < UNITS:
                            exps(i, m + AHEAD)
                        else:
                            exps(i + 1, m + AHEAD - UNITS)
                        if m == 5:
                            norm.act_std(i + 1)
                        if m == V_M:
                            copy_v(i + 1, 1 - k)
                        if BY_ACT[m]:
                            empty(i, m)

        @block.vector
        def _(dve):
            def tables():
                nc.vector.tensor_copy(mask_b[:, :], mask_f[:, :])
                nc.vector.tensor_copy(ident_b[:, :], core.ident[:, :]).then_inc(mask_ready, 1)
                nc.vector.tensor_scalar(dist, dist, float(CLIP), -1.0, ALU.min, ALU.max)
                nc.vector.memset(factor[:, :], 0.0)
                nc.vector.drain()
                for n in range(-1, CLIP + 1):
                    value = 1.0 if n < 0 else rel_sb[:, n:n + 1]
                    nc.vector.tensor_scalar(hit, dist, float(n), value, ALU.is_equal, ALU.mult)
                    nc.vector.drain()
                    nc.vector.tensor_tensor(factor[:, :], factor[:, :], hit, ALU.add)
                    nc.vector.drain()
                nc.vector.tensor_scalar(factor[:, :], factor[:, :], SCALE, None, ALU.mult)
                nc.vector.drain()

            def group(i, m):
                t = m // NH
                width = (t + 1) * P
                side = (m // HG) % (PR // HG)
                dve.wait_ge(qk_ready, i * UNITS + m + HG)
                dve.wait_ge(turned, i * UNITS + m + HG)
                dve.sem_inc(groups_begun, 1)
                for g in range(HG):
                    nc.vector.tensor_tensor_reduce(
                        out=prob[:, (m + g) % PR, 0:width], in0=s_ps[g][:, 0:width],
                        in1=factor[:, S - width:S], scale=1.0, scalar=-3.0e38, op0=ALU.mult, op1=ALU.max,
                        accum_out=top[:, side, g:g + 1]).then_inc(s_free, 1)
                nc.vector.drain()
                nc.vector.tensor_scalar(neg_top[:, side, :], top[:, side, :], -1.0, None,
                                        ALU.mult).then_inc(top_ready, 1)

            def empty(i, m):
                t = m // NH
                dve.wait_ge(turned, PR + i * UNITS + m + 1)
                dve.wait_ge(pv_done, i * UNITS + m + 1)
                nc.vector.tensor_copy(prob_t[:, m % TR, 0:(t + 1) * P],
                                      t_ps[m % TB][:, 0:(t + 1) * P]).then_inc(t_dve, 1)

            def copy_o(n):
                dve.wait_ge(pv_done, TR + n * NH)
                nc.vector.tensor_copy(o_sb[:, :], o_ps[:, :]).then_inc(o_copied, 1)

            def divide(n):
                o = misc[:, :].rearrange("p (h d) -> p h d", d=VC)
                dve.wait_ge(o_turned, n + 1)
                nc.vector.reciprocal(inv[:, :, :], o[:, :, HD:HD + 1])
                nc.vector.drain()
                nc.vector.tensor_tensor(ctx_sb[:, :].rearrange("p (h d) -> p h d", d=HD), o[:, :, 0:HD],
                                        inv[:, :, :].broadcast_to([P, NH, HD]), ALU.mult).then_inc(ctx_ready, 1)

            def copy_ctx(n):
                dve.wait_ge(ctx_turned, n + 1)
                nc.vector.tensor_copy(ctx_t[:, :, :], misc[:, 0:D].rearrange("p (c q) -> p c q", q=P)).then_inc(ctx_copied, 1)

            def add_out(n, xt):
                dve.wait_ge(out_ready, n + 1)
                nc.vector.tensor_tensor(xt, misc[:, D:2 * D], xt, ALU.add).then_inc(out_added, 1)

            def take_product(i, n):
                dve.wait_ge(pj_ready, i * NPJ + n + 1)
                if n >= 2:
                    dve.wait_ge(parts_ready, i * NPJ + n - 1)
                nc.vector.tensor_copy(parts[:, n, 0, :], misc[:, :])
                nc.vector.drain()
                nc.vector.tensor_tensor(rest[n % 2][:, :], misc[:, :], parts[:, n, 0, :],
                                        ALU.subtract).then_inc(pj_taken, 1)

            def copy_v(i, k):
                dve.wait_ge(v_ready, i * 2 + 1)
                nc.vector.tensor_copy(v_sb[k][:, 0:2, :, 0:HD],
                                      s_ps[0][:, :].rearrange("p (j h d) -> p j h d", j=2, d=HD)).then_inc(v_dve, 1)

            dve.sem_inc(s_free, HG)
            dve.sem_inc(out_added, 1)
            nc.vector.memset(o_ps[:, :], 1.0)
            norm.dve_stats(0)
            norm.dve_normalise(0)
            norm.dve_copy_t(0, 0, guard=False)
            for n in range(NPJ):
                take_product(0, n)
            copy_v(0, 0)
            dve.wait_ge(loaded, LOADED)
            dve.wait_ge(consts, 2)
            tables()
            group(0, 0)
            group(0, HG)
            with dve.Fori(0, B // 2) as pair:
                for k in range(2):
                    i = pair * 2 + k
                    for m in range(UNITS):
                        t, h = divmod(m, NH)
                        if h == 4:
                            copy_o(i * TPB + t)
                        if h == 12:
                            copy_ctx(i * TPB + t)
                        if m % HG == 2 and m + 6 < UNITS:
                            group(i, m + 6)
                        if m % HG == 2 and m + 6 > UNITS:
                            group(i + 1, m + 6 - UNITS)
                        if m == V_M:
                            copy_v(i + 1, 1 - k)
                        if m - 1 in PJ_M:
                            take_product(i + 1, PJ_M.index(m - 1))
                        if m == V_M + 3:
                            group(i + 1, 0)
                        if not BY_ACT[m]:
                            empty(i, m)
                        if h == 9:
                            divide(i * TPB + t)
                        if h == 15:
                            add_out(i * TPB + t, core.tile(i, TPB - 1) if t == 0 else core.tile(i + 1, t - 1))
                        if m == 5:
                            norm.dve_stats(i + 1)
                        if m == 13:
                            norm.dve_normalise(i + 1)
                        if m == NH + 1:
                            norm.dve_copy_t(i + 1, 1 - k, guard=False, chunks=(0,))
                        if m == NH + 4:
                            norm.dve_copy_t(i + 1, 1 - k, guard=False, chunks=(1,))
            copy_o(B * TPB)
            divide(B * TPB)
            copy_ctx(B * TPB)
            add_out(B * TPB, core.tile(B, TPB - 1))



TOP = 3
CAP = 128


class Sparse:

    def __init__(self, core, ctx, experts):
        nc = core.nc
        self.rows_in = nc.dram_tensor("rows_in", (experts * CAP, D), FP32, kind="Internal").ap()
        self.rows_out = nc.dram_tensor("rows_out", (experts * CAP, D), FP32, kind="Internal").ap()


def ffn0_phase(core, sparse, name, gate_w, gate_b, w1, b1, w2, b2):
    nc = core.nc
    E, H = w1.shape[0], w1.shape[2]
    HC = H // P
    R = 4
    NT = B * TPB
    NK = TPB * TOP
    ctx = ExitStack()
    with ctx:
        sb = lambda n, s, dt=FP32: ctx.enter_context(nc.sbuf_tensor(f"{name}_{n}", s, dt))
        sem = lambda n: core.semaphore(f"{name}_{n}")
        w1_sb = [sb(f"w1_{s}", [P, DC, H]) for s in range(R)]
        w2_sb = [sb(f"w2_{s}", [P, HC, D]) for s in range(R)]
        b2_sb = [sb(f"b2_{s}", [1, D]) for s in range(R)]
        best = sb("best", [P, B, TOP, TPB])
        valid = sb("valid", [P, B, TOP, TPB])
        place = sb("place", [P, B, TOP, TPB], U32)
        w_loaded = [sem(f"w_loaded{s}") for s in range(R)]

        def load_weights(sp, s, e):
            sp.dma_start(w1_sb[s][:, :, :], w1[e, :, :].rearrange("(c p) h -> p c h", p=P)).then_inc(w_loaded[s], 16)
            sp.dma_start(w2_sb[s][:, :, :], w2[e, :, :].rearrange("(c p) d -> p c d", p=P)).then_inc(w_loaded[s], 16)
            sp.dma_start(b2_sb[s][:, :], b2[bass.ds(e, 1), :]).then_inc(w_loaded[s], 16)

        route(core, sparse, name, gate_w, gate_b, E, best, valid, place, load_weights, R)
        experts(core, sparse, name, b1, E, H, R, w1_sb, w2_sb, b2_sb, w_loaded, load_weights)
        combine(core, sparse, name, best, valid, place)


def route(core, sparse, name, gate_w, gate_b, E, best, valid, place, load_weights, R):
    nc = core.nc
    NK = TPB * TOP
    NB = 4
    ctx = ExitStack()
    with ctx:
        sb = lambda n, s, dt=FP32: ctx.enter_context(nc.sbuf_tensor(f"{name}_{n}", s, dt))
        ps = lambda n, s: ctx.enter_context(nc.psum_tensor(f"{name}_{n}", s, FP32))
        sem = lambda n: core.semaphore(f"{name}_{n}")
        norm = Norm(core, ctx, name, xn_buffers=NB)
        gate_w_sb = sb("gate_w", [P, DC, E])
        gate_b_sb = sb("gate_b", [P, E])
        iota_e = sb("iota_e", [P, E])
        before_f = sb("before_f", [P, P])
        before = sb("before", [P, P], BF16)
        ones = sb("ones", [P, P], BF16)
        logits = sb("logits", [P, TPB, E])
        top_v = sb("top_v", [P, TPB, 8])
        top_i = sb("top_i", [P, TPB, 8], U32)
        expert = sb("expert", [P, TOP, TPB])
        pick = sb("pick", [P, TOP, TPB, E])
        some = sb("some", [P, TPB, E])
        mask = sb("mask", [P, TPB, E], BF16)
        carry = sb("carry", [P, TPB + 1, E], BF16)
        product = sb("product", [P, TOP, TPB, E])
        pos = sb("pos", [P, TOP, TPB])
        over = sb("over", [P, TOP, TPB])
        near = sb("near", [P, TOP, TPB])
        target = [sb(f"target{k}", [P, TOP, TPB], U32) for k in range(NB)]
        logit_ps = ps("logit_ps", [P, 512])
        pos_ps = ps("pos_ps", [P, 512])

        loaded = sem("r_loaded")
        consts = sem("r_consts")
        logits_ready = sem("r_logits")
        mask_ready = sem("r_mask")
        pos_ready = sem("r_pos")
        pos_read = sem("r_pos_read")
        target_ready = sem("r_target")
        carried = sem("r_carried")
        scattered = [sem(f"r_scattered{k}") for k in range(NB)]
        block = ctx.enter_context(nc.Block())
        LOADED = 16 * 2

        @block.sync
        def _(sp):
            sp.dma_start(gate_w_sb[:, :, :], gate_w.rearrange("(c p) e -> p c e", p=P)).then_inc(loaded, 16)
            sp.dma_start(gate_b_sb[:, :], gate_b.partition_broadcast(P)).then_inc(loaded, 16)
            for s in range(R):
                load_weights(sp, s, s)

        @block.gpsimd
        def _(pool):
            nc.gpsimd.iota(iota_e[:, :], pattern=[[1, E]], base=0, channel_multiplier=0,
                           allow_small_or_imprecise_dtypes=True)
            nc.gpsimd.memset(carry[:, :, :], 0.0)
            nc.gpsimd.memset(ones[:, :], 1.0)
            nc.gpsimd.memset(before_f[:, :], 1.0).then_inc(consts, 1)
            pool.wait_ge(consts, 1)
            nc.gpsimd.affine_select(out=before_f[:, :], in_=before_f[:, :], compare_op=ALU.is_gt, fill=0.0,
                                    base=0, pattern=[[1, P]], channel_multiplier=-1).then_inc(consts, 1)
            pool.wait_ge(core.cleared, 16 * core.clears)
            with pool.Fori(0, B // NB) as turn:
                for k in range(NB):
                    i = turn * NB + k
                    pool.wait_ge(target_ready, i + 1)
                    pool.sem_inc(carried, 1)
                    for r in range(TOP):
                        for j in range(TPB):
                            nc.gpsimd.indirect_dma_start(
                                out=sparse.rows_in, out_offset=bass.IndirectOffsetOnAxis(ap=target[k][:, r, j:j + 1], axis=0),
                                in_=norm.xns[k][:, j, :], in_offset=None, bounds_check=E * CAP - 1,
                                oob_is_err=False).then_inc(scattered[k], 16)
            for k in range(NB):
                pool.wait_ge(scattered[k], 16 * NK * (B // NB))

        @block.tensor
        def _(pe):
            norm.pe_transpose(0, 0)
            pe.wait_ge(loaded, LOADED)
            with pe.Fori(0, B // NB) as turn:
                for k in range(NB):
                    i = turn * NB + k
                    norm.wait_xn_t(pe, i)
                    pe.wait_ge(mask_ready, i + 1)
                    for j in range(TPB):
                        for c in range(DC):
                            last = nc.tensor.matmul(logit_ps[:, j * E:(j + 1) * E],
                                                    norm.xn_t[k % 2][:, c, j * P:(j + 1) * P],
                                                    gate_w_sb[:, c, :], start=c == 0, stop=c == DC - 1)
                    last.then_inc(logits_ready, 1)
                    norm.pe_transpose(i + 1, (k + 1) % NB)
                    pe.wait_ge(mask_ready, i + 2)
                    pe.wait_ge(pos_read, i + 1)
                    nc.tensor.matmul(pos_ps[:, 0:TPB * E], before[:, :], mask[:, :, :].rearrange("p j e -> p (j e)"),
                                     start=True, stop=False).then_inc(norm.free, 1)
                    nc.tensor.matmul(pos_ps[:, 0:TPB * E], ones[:, :], carry[:, 0:TPB, :].rearrange("p j e -> p (j e)"),
                                     start=False, stop=True).then_inc(pos_ready, 1)

        @block.scalar
        def _(act):
            norm.act_std(0)
            with act.Fori(0, B) as i:
                norm.act_std(i + 1)

        @block.vector
        def _(dve):
            for sem_from_1 in (mask_ready, pos_read, norm.free):
                dve.sem_inc(sem_from_1, 1)
            norm.dve_stats(0)
            norm.dve_normalise(0, 0)
            norm.dve_copy_t(0, 0)
            dve.wait_ge(loaded, LOADED)
            dve.wait_ge(consts, 2)
            nc.vector.tensor_copy(before[:, :], before_f[:, :])
            def step(turn, k):
                i = turn * NB + k
                following = (k + 1) % NB
                nc.vector.drain()
                norm.dve_stats(i + 1)
                dve.wait_ge(logits_ready, i + 1)
                nc.vector.tensor_tensor(logits[:, :, :], logit_ps[:, 0:TPB * E].rearrange("p (j e) -> p j e", e=E),
                                        gate_b_sb[:, :].unsqueeze(1).broadcast_to([P, TPB, E]), ALU.add)
                nc.vector.drain()
                for j in range(TPB):
                    nc.vector.max(top_v[:, j, :], logits[:, j, :])
                nc.vector.drain()
                for j in range(TPB):
                    nc.vector.max_index(top_i[:, j, :], top_v[:, j, :], logits[:, j, :])
                nc.vector.tensor_copy(best[:, i, :, :], top_v[:, :, 0:TOP].rearrange("p j r -> p r j"))
                nc.vector.drain()
                nc.vector.tensor_copy(expert[:, :, :], top_i[:, :, 0:TOP].rearrange("p j r -> p r j"))
                scatters = turn * (16 * NK) + (0 if following else 16 * NK)
                if due(scatters):
                    dve.wait_ge(scattered[following], scatters)
                norm.dve_normalise(i + 1, following)
                nc.vector.drain()
                nc.vector.tensor_tensor(pick[:, :, :, :],
                                        iota_e[:, :].unsqueeze(1).unsqueeze(1).broadcast_to([P, TOP, TPB, E]),
                                        expert[:, :, :].unsqueeze(3).broadcast_to([P, TOP, TPB, E]), ALU.is_equal)
                nc.vector.tensor_copy(carry[:, 0, :], carry[:, TPB, :])
                nc.vector.drain()
                nc.vector.tensor_tensor(some[:, :, :], pick[:, 0, :, :], pick[:, 1, :, :], ALU.add)
                nc.vector.drain()
                nc.vector.tensor_tensor(mask[:, :, :], some[:, :, :], pick[:, 2, :, :], ALU.add)
                for j in range(TPB):
                    nc.vector.drain()
                    last = nc.vector.tensor_tensor(carry[:, j + 1, :], carry[:, j, :], mask[:, j, :], ALU.add)
                last.then_inc(mask_ready, 1)
                norm.dve_copy_t(i + 1, following % 2)
                dve.wait_ge(pos_ready, i + 1)
                nc.vector.tensor_tensor(
                    product[:, :, :, :], pick[:, :, :, :],
                    pos_ps[:, 0:TPB * E].rearrange("p (j e) -> p j e", e=E).unsqueeze(1).broadcast_to([P, TOP, TPB, E]),
                    ALU.mult).then_inc(pos_read, 1)
                nc.vector.drain()
                nc.vector.tensor_reduce(pos[:, :, :], product[:, :, :, :], AX.X, ALU.add)
                nc.vector.drain()
                nc.vector.tensor_scalar(valid[:, i, :, :], pos[:, :, :], float(CAP), None, ALU.is_lt)
                nc.vector.tensor_scalar(over[:, :, :], pos[:, :, :], float(CAP), float(2 * E * CAP), ALU.is_ge, ALU.mult)
                nc.vector.tensor_scalar(near[:, :, :], pos[:, :, :], float(CAP - 1), None, ALU.min)
                nc.vector.tensor_scalar(expert[:, :, :], expert[:, :, :], float(CAP), None, ALU.mult)
                nc.vector.drain()
                nc.vector.tensor_tensor(place[:, i, :, :], expert[:, :, :], near[:, :, :], ALU.add)
                nc.vector.tensor_tensor(over[:, :, :], over[:, :, :], pos[:, :, :], ALU.add)
                nc.vector.drain()
                nc.vector.tensor_tensor(target[k][:, :, :], over[:, :, :], expert[:, :, :], ALU.add).then_inc(target_ready, 1)

            for k in range(NB):
                step(0, k)
            with dve.Fori(1, B // NB) as turn:
                for k in range(NB):
                    step(turn, k)


def experts(core, sparse, name, b1, E, H, R, w1_sb, w2_sb, b2_sb, w_loaded, load_weights):
    nc = core.nc
    HC = H // P
    HB = 2
    ctx = ExitStack()
    with ctx:
        sb = lambda n, s, dt=FP32: ctx.enter_context(nc.sbuf_tensor(f"{name}_{n}", s, dt))
        ps = lambda n, s: ctx.enter_context(nc.psum_tensor(f"{name}_{n}", s, FP32))
        sem = lambda n: core.semaphore(f"{name}_{n}")
        ones = sb("e_ones", [1, P])
        b1_rows = sb("b1_rows", [E, H])
        b1_t = sb("b1_t", [P, HC, E])
        b1_e = [sb(f"b1_e{k}", [P, HC]) for k in range(2)]
        rows = [sb(f"rows{s}", [P, D]) for s in range(R)]
        rows_t = [sb(f"rows_t{k}", [P, DC, P]) for k in range(2)]
        h_t = [sb(f"h_t{k}", [P, HC, P]) for k in range(2)]
        y_sb = [sb(f"y{k}", [P, D]) for k in range(2)]
        t_ps = ps("t_ps", [P, 512])
        h_ps = [ps(f"h_ps{n}", [P, 512]) for n in range(HC // HB)]
        y_ps = [ps(f"y_ps{k}", [P, 512]) for k in range(2)]

        b1_loaded = sem("b1_loaded")
        consts = sem("e_consts")
        b1_turned = sem("b1_turned")
        b1_copied = sem("b1_copied")
        b1_ready = sem("b1_ready")
        x_loaded = [sem(f"x_loaded{s}") for s in range(R)]
        x_turned = sem("x_turned")
        x_copied = sem("x_copied")
        h_ready = sem("h_ready")
        gelu_done = sem("gelu_done")
        y_ready = sem("e_y_ready")
        y_copied = sem("y_copied")
        carried = sem("e_carried")
        y_stored = [sem(f"y_stored{k}") for k in range(2)]
        block = ctx.enter_context(nc.Block())

        @block.sync
        def _(sp):
            def load_rows(s, e):
                sp.dma_start(rows[s][:, :], sparse.rows_in[bass.ds(e * CAP, CAP), :]).then_inc(x_loaded[s], 16)
            sp.sem_inc(y_ready, R)
            sp.dma_start(b1_rows[:, :], b1).then_inc(b1_loaded, 16)
            for s in range(R):
                load_rows(s, s)
            with sp.Fori(1, E // R) as turn:
                for s in range(R):
                    e = turn * R + s
                    sp.wait_ge(y_ready, e + 1)
                    load_weights(sp, s, e)
                    load_rows(s, e)

        @block.gpsimd
        def _(pool):
            nc.gpsimd.memset(ones[:, :], 1.0).then_inc(consts, 1)
            with pool.Fori(0, E // 2) as pair:
                for k in range(2):
                    e = pair * 2 + k
                    pool.wait_ge(y_copied, e + 1)
                    pool.sem_inc(carried, 1)
                    pool.dma_start(sparse.rows_out[bass.ds(e * CAP, CAP), :], y_sb[k][:, :]).then_inc(y_stored[k], 16)
            for k in range(2):
                pool.wait_ge(y_stored[k], 16 * (E // 2))

        @block.tensor
        def _(pe):
            def turn_rows(turn, s):
                e = turn * R + s
                pe.wait_ge(x_loaded[s], (turn + 1) * 16)
                if due(e):
                    pe.wait_ge(x_copied, e)
                for c in range(DC):
                    last = nc.tensor.transpose(t_ps[:, c * P:(c + 1) * P], rows[s][:, c * P:(c + 1) * P],
                                               core.ident[:, :])
                last.then_inc(x_turned, 1)

            def up(turn, s):
                e, k = turn * R + s, s % 2
                pe.wait_ge(w_loaded[s], (turn + 1) * 48)
                pe.wait_ge(x_copied, e + 1)
                for n in range(HC):
                    if n % HB == 0:
                        pe.wait_ge(gelu_done, e * HC + n + HB)
                    for c in range(DC):
                        last = nc.tensor.matmul(h_ps[n // HB][:, (n % HB) * P:(n % HB + 1) * P], w1_sb[s][:, c, n * P:(n + 1) * P],
                                                rows_t[k][:, c, :], start=c == 0, stop=c == DC - 1)
                    if n % HB == HB - 1:
                        last.then_inc(h_ready, 1)

            def down(turn, s):
                e, k = turn * R + s, s % 2
                if due(e - 1):
                    pe.wait_ge(y_copied, e - 1)
                nc.tensor.matmul(y_ps[k][:, 0:D], ones[:, :], b2_sb[s][:, :], start=True, stop=False)
                for n in range(HC):
                    pe.wait_ge(gelu_done, HC + e * HC + n + 1)
                    last = nc.tensor.matmul(y_ps[k][:, 0:D], h_t[k][:, n, :], w2_sb[s][:, n, :],
                                            start=False, stop=n == HC - 1)
                last.then_inc(y_ready, 1)

            pe.wait_ge(consts, 1)
            pe.wait_ge(b1_loaded, 16)
            for n in range(HC):
                last = nc.tensor.transpose(h_ps[0][:, n * E:(n + 1) * E],
                                           b1_rows[:, n * P:(n + 1) * P], core.ident[0:E, 0:E])
            last.then_inc(b1_turned, 1)
            pe.wait_ge(b1_copied, 1)
            def step(turn, s, last):
                if not (last and s + 1 >= R):
                    up(turn + (s + 1) // R, (s + 1) % R)
                if not (last and s + 2 >= R):
                    turn_rows(turn + (s + 2) // R, (s + 2) % R)
                down(turn, s)

            turn_rows(0, 0)
            up(0, 0)
            turn_rows(0, 1)
            for s in range(R):
                step(0, s, False)
            with pe.Fori(1, E // R - 1) as turn:
                for s in range(R):
                    step(turn, s, False)
            for s in range(R):
                step(E // R - 1, s, True)

        @block.scalar
        def _(act):
            act.sem_inc(gelu_done, HC)
            with act.Fori(0, E // 2) as pair:
                for k in range(2):
                    e = pair * 2 + k
                    act.wait_ge(b1_ready, e + 1)
                    act.wait_ge(y_ready, e + R - 1)
                    for n in range(HC):
                        if n % HB == 0:
                            act.wait_ge(h_ready, e * (HC // HB) + n // HB + 1)
                        nc.scalar.activation(h_t[k][:, n, :], h_ps[n // HB][:, (n % HB) * P:(n % HB + 1) * P], ACT.Gelu,
                                             bias=b1_e[k][:, n:n + 1]).then_inc(gelu_done, 1)

        @block.vector
        def _(dve):
            dve.wait_ge(b1_turned, 1)
            nc.vector.tensor_copy(b1_t[:, :, :], h_ps[0][:, :].rearrange("p (n e) -> p n e", e=E)).then_inc(b1_copied, 1)
            nc.vector.drain()
            def prepare(e, k):
                if due(e):
                    dve.wait_ge(gelu_done, e * HC)
                nc.vector.tensor_copy(b1_e[k][:, :], b1_t[:, :, e]).then_inc(b1_ready, 1)
                dve.wait_ge(x_turned, e + 1)
                nc.vector.tensor_copy(rows_t[k][:, :, :],
                                      t_ps[:, 0:D].rearrange("p (c q) -> p c q", q=P)).then_inc(x_copied, 1)

            def finish(e, k, stored):
                dve.wait_ge(y_ready, R + e + 1)
                if due(stored):
                    dve.wait_ge(y_stored[k], stored)
                nc.vector.tensor_copy(y_sb[k][:, :], y_ps[k][:, 0:D]).then_inc(y_copied, 1)

            prepare(0, 0)
            prepare(1, 1)
            for k in range(2):
                prepare(k + 2, k)
                finish(k, k, 0)
            with dve.Fori(1, E // 2 - 1) as pair:
                for k in range(2):
                    prepare(pair * 2 + k + 2, k)
                    finish(pair * 2 + k, k, pair * 16)
            for k in range(2):
                finish(E - 2 + k, k, (E // 2 - 1) * 16)


def combine(core, sparse, name, best, valid, place):
    nc = core.nc
    NK = TPB * TOP
    ctx = ExitStack()
    with ctx:
        sb = lambda n, s, dt=FP32: ctx.enter_context(nc.sbuf_tensor(f"{name}_{n}", s, dt))
        sem = lambda n: core.semaphore(f"{name}_{n}")
        shifted = sb("shifted", [P, B, TOP, TPB])
        total = sb("total", [P, B, 1, TPB])
        index = [sb(f"index{k}", [P, NK], U32) for k in range(2)]
        gate = [sb(f"gate{k}", [P, NK]) for k in range(2)]
        back = [sb(f"back{k}", [P, NK, D]) for k in range(2)]
        shift_ready = sem("c_shift")
        exp_ready = sem("c_exp")
        index_ready = sem("c_index")
        carried = sem("c_carried")
        gathered = [sem(f"c_gathered{k}") for k in range(2)]
        used = sem("c_used")
        block = ctx.enter_context(nc.Block())

        @block.scalar
        def _(act):
            act.wait_ge(shift_ready, 1)
            nc.scalar.activation(shifted[:, :, :, :], shifted[:, :, :, :], ACT.Exp).then_inc(exp_ready, 1)

        @block.gpsimd
        def _(pool):
            with pool.Fori(0, B // 2) as pair:
                for k in range(2):
                    i = pair * 2 + k
                    pool.wait_ge(index_ready, i + 1)
                    pool.sem_inc(carried, 1)
                    for n in range(NK):
                        nc.gpsimd.indirect_dma_start(
                            out=back[k][:, n, :], out_offset=None, in_=sparse.rows_out,
                            in_offset=bass.IndirectOffsetOnAxis(ap=index[k][:, n:n + 1], axis=0),
                            bounds_check=sparse.rows_out.shape[0] - 1, oob_is_err=False).then_inc(gathered[k], 16)

        @block.vector
        def _(dve):
            def fetch(i, k):
                nc.vector.drain()
                nc.vector.tensor_copy(gate[k][:, :], shifted[:, i, :, :].rearrange("p r j -> p (r j)"))
                nc.vector.tensor_copy(index[k][:, :], place[:, i, :, :].rearrange("p r j -> p (r j)")).then_inc(index_ready, 1)

            def use(i, k, count):
                nc.vector.drain()
                dve.wait_ge(gathered[k], count)
                for r in range(TOP):
                    if r:
                        nc.vector.drain()
                    for j in range(TPB):
                        xt = core.tile(i + 1, j)
                        nc.vector.scalar_tensor_tensor(out=xt, in0=back[k][:, r * TPB + j, :],
                                                       scalar=gate[k][:, r * TPB + j:r * TPB + j + 1], in1=xt,
                                                       op0=ALU.mult, op1=ALU.add)

            nc.vector.tensor_tensor(shifted[:, :, :, :], best[:, :, :, :],
                                    best[:, :, 0:1, :].broadcast_to([P, B, TOP, TPB]), ALU.subtract).then_inc(shift_ready, 1)
            dve.wait_ge(exp_ready, 1)
            nc.vector.tensor_tensor(total[:, :, :, :], shifted[:, :, 0:1, :], shifted[:, :, 1:2, :], ALU.add)
            nc.vector.drain()
            nc.vector.tensor_tensor(total[:, :, :, :], total[:, :, :, :], shifted[:, :, 2:3, :], ALU.add)
            nc.vector.drain()
            nc.vector.reciprocal(total[:, :, :, :], total[:, :, :, :])
            nc.vector.drain()
            nc.vector.tensor_tensor(shifted[:, :, :, :], shifted[:, :, :, :],
                                    total[:, :, :, :].broadcast_to([P, B, TOP, TPB]), ALU.mult)
            nc.vector.drain()
            nc.vector.scalar_tensor_tensor(
                out=shifted[:, :, :, :].rearrange("p b r j -> p (b r j)"),
                in0=shifted[:, :, :, :].rearrange("p b r j -> p (b r j)"), scalar=0.5,
                in1=valid[:, :, :, :].rearrange("p b r j -> p (b r j)"), op0=ALU.mult, op1=ALU.mult)
            for k in range(2):
                fetch(k, k)
            with dve.Fori(0, B // 2 - 1) as pair:
                for k in range(2):
                    i = pair * 2 + k
                    use(i, k, (pair + 1) * (16 * NK))
                    fetch(i + 2, k)
            for k in range(2):
                use(B - 2 + k, k, (B // 2) * (16 * NK))



WIN = 32


def attn0_phase(core, name, skew_dram, w_disp, b_disp, w_val, b_val, rel_pos, w_state, b_state, w_strain,
                b_strain, w_state_i, w_state_j, w_pos, w_bond, b_bond, w_damage, b_damage,
                w_damage_out, b_damage_out, w_cproj, b_cproj):
    nc = core.nc
    BD = w_state.shape[0]
    NH = D // BD
    HH = P // BD
    HALF = NH // HH
    PAD = WIN
    DG = 4
    NQ = WIN // DG
    STEPS = HALF * NQ
    PG = P // HH
    GSTEPS = PG // DG
    GROUPS = STEPS // GSTEPS
    SPAN = 2 * WIN
    NBLK = S // WIN
    BPT = P // WIN
    HP = NH // 2
    ctx = ExitStack()
    with ctx:
        sb = lambda n, s, dt=FP32: ctx.enter_context(nc.sbuf_tensor(f"{name}_{n}", s, dt))
        ps = lambda n, s: ctx.enter_context(nc.psum_tensor(f"{name}_{n}", s, FP32))
        sem = lambda n: core.semaphore(f"{name}_{n}")
        norm = Norm(core, ctx, name, pad=PAD)
        w_disp_sb = sb("w_disp", [P, DC, D])
        w_val_sb = sb("w_val", [P, DC, HP, 2, BD])
        w_out_sb = sb("w_out", [P, DC, D])
        b_out_sb = sb("b_out", [1, D])
        ones = sb("ones", [1, P])
        b_disp_sb = sb("b_disp", [P, HALF])
        b_val_sb = sb("b_val", [P, HP, 2, BD])
        bond_b = sb("bond_b", [P, 1])
        damage_b = sb("damage_b", [P, 1])
        STATE, STRAIN, STATE_I, STATE_J, DAMAGE = range(5)
        COLS = 5 * BD
        SM = COLS + 5 + WIN
        small = sb("small", [BD, SM])
        rel_t = sb("rel_t", [BD, WIN])
        w_pos_sb = sb("w_pos", [BD, BD])
        select = sb("select", [BD, HH, BD])
        small_rep = sb("small_rep", [P, SM])
        diag = sb("diag", [P, HH, BD])
        mats = [sb(f"mat{n}", [P, HH, BD]) for n in range(5)]
        neg_strain = sb("neg_strain", [P, HH, BD])
        col_bond = sb("col_bond", [P, 2 * PG - 1, HH])
        col_damage = sb("col_damage", [P, 2 * PG - 1, HH])
        sig = sb("sig", [P, S])
        logits = sb("logits", [P, S])
        inv_count = sb("inv_count", [P, S])
        early = sb("early", [P, WIN])
        disp = [sb(f"disp{h}", [P, S]) for h in range(HALF)]
        sum_a = sb("sum_a", [P, PAD + S])
        sum_b = sb("sum_b", [P, PAD + S])
        state = [sb(f"state{h}", [P, S]) for h in range(HALF)]
        a_sb = [[sb(f"a{k}{h}", [P, PAD + S]) for h in range(HALF)] for k in range(2)]
        c_sb = [[sb(f"c{k}{h}", [P, PAD + S]) for h in range(HALF)] for k in range(2)]
        q_sb = [[sb(f"q{k}{h}", [P, S]) for h in range(HALF)] for k in range(2)]
        f_sb = [[sb(f"f{k}{h}", [P, S]) for h in range(HALF)] for k in range(2)]
        bond_buf = [sb(f"bond_buf{k}", [P, DG, S]) for k in range(2)]
        dmg_buf = [sb(f"dmg_buf{k}", [P, DG, S]) for k in range(2)]
        bond = sb("bond", [P, TPB, NH, WIN])
        expd = sb("expd", [P, TPB, NH, WIN])
        top = sb("top", [P, TPB * NH, 1])
        inv_sum = [sb(f"inv_sum{k}", [P, TPB, NH]) for k in range(2)]
        skewed = sb("skewed", [P, TPB, NH * SPAN])
        turned = sb("turned", [P, HP, P])
        vals = sb("vals", [P, NBLK, HP, 2, BD])
        ctx_sb = sb("ctx", [P, D])
        ctx_t = sb("ctx_t", [P, DC, P])
        bond_ps = [ps(f"bond_ps{n}", [P, S]) for n in range(2)]
        dmg_ps = [ps(f"dmg_ps{n}", [P, S]) for n in range(2)]
        t_ps = ps("t_ps", [P, 512])
        o_ps = ps("o_ps", [P, 512])
        misc = ps("misc", [P, 512])
        pj = norm.tp

        loaded = sem("loaded")
        rel_loaded = sem("rel_loaded")
        zeroed = sem("zeroed")
        consts = sem("consts")
        tables_a = sem("tables_a")
        tables_b = sem("tables_b")
        tables = sem("tables")
        bond_pre = sem("bond_pre")
        dmg_pre = sem("dmg_pre")
        gelu_done = sem("gelu_done")
        chunk_used = sem("chunk_used")
        sig_done = sem("sig_done")
        combined = sem("combined")
        logits_copied = sem("logits_copied")
        inv_ready = sem("inv_ready")
        weights_stored = sem("weights_stored")
        logits_turned = sem("logits_turned")
        soft_ready = sem("soft_ready")
        exp_done = sem("exp_done")
        skew_stored = sem("skew_stored")
        skew_loaded = sem("skew_loaded")
        w_turned = sem("w_turned")
        w_copied = sem("w_copied")
        out_ready = sem("out_ready")
        ctx_ready = sem("ctx_ready")
        ctx_turned = sem("ctx_turned")
        ctx_copied = sem("ctx_copied")
        proj_ready = sem("proj_ready")
        proj_added = sem("proj_added")
        pj_ready = sem("pj_ready")
        pj_copied = sem("pj_copied")
        state_ready = sem("state_ready")
        val_ready = sem("val_ready")
        val_copied = sem("val_copied")
        block = ctx.enter_context(nc.Block())

        PJ = [(what, h) for what in ("disp", "u", "c", "a", "q") for h in range(HALF)]
        PJ_STEP = 3
        NPJ = len(PJ)
        T_STEP = 6

        def tile_at(q, step):
            x, odd = divmod(q - step, 2)
            return x if 0 <= x < TPB and not odd else None

        def window(x, d):
            first = x[:, d + 1:d + 1 + S]
            return bass.AP(tensor=first.tensor, offset=first.offset, ap=[first.ap[0], [1, DG], [1, S]])

        @block.sync
        def _(sp):
            def load(dst, src, **kind):
                sp.dma_start(dst, src, **kind).then_inc(loaded, 16)
            load(w_disp_sb[:, :, :], w_disp.rearrange("(c p) n -> p c n", p=P))
            load(w_val_sb[:, :, :, :, :].rearrange("p c h r d -> p c (h r d)"), w_val.rearrange("(c p) n -> p c n", p=P))
            load(w_out_sb[:, :, :], w_cproj.rearrange("(c p) n -> p c n", p=P))
            load(b_out_sb[:, :], b_cproj.rearrange("(o n) -> o n", o=1))
            load(b_disp_sb[:, :], b_disp.rearrange("(h p) -> p h", p=P), allow_slow_non_contiguous=True)
            load(b_val_sb[:, :, :, :].rearrange("p h r d -> p (h r d)"), b_val.partition_broadcast(P))
            load(bond_b[:, :], b_bond.partition_broadcast(P))
            load(damage_b[:, :], b_damage_out.partition_broadcast(P))
            for n, w in enumerate((w_state, w_strain, w_state_i, w_state_j, w_damage)):
                load(small[:, n * BD:(n + 1) * BD], w)
            load(small[:, COLS:COLS + 1], w_bond)
            load(small[:, COLS + 1:COLS + 2], w_damage_out)
            for n, b in enumerate((b_state, b_strain, b_damage)):
                load(small[:, COLS + 2 + n:COLS + 3 + n], b.rearrange("(d o) -> d o", o=1))
            sp.dma_start(rel_t[:, :], rel_pos.rearrange("w d -> d w"),
                         allow_slow_non_contiguous=True).then_inc(rel_loaded, 16)
            sp.dma_start(w_pos_sb[:, :], w_pos).then_inc(rel_loaded, 16)

            def skew_weights(j):
                sp.wait_ge(exp_done, j + 1)
                for a in range(BPT):
                    row = TPB * NH * SPAN
                    rows = bass.AP(tensor=skew_dram.tensor, offset=a * WIN * row + 1,
                                   ap=[[row + 1, WIN], [SPAN, TPB * NH], [1, WIN]])
                    sp.dma_start(rows, expd[a * WIN:(a + 1) * WIN, :, :, :].rearrange(
                        "p j h w -> p (j h) w")).then_inc(skew_stored, 16)
                sp.wait_ge(w_turned, 1 + j * TPB)
                sp.wait_ge(skew_stored, (j + 1) * 16 * BPT)
                sp.sem_inc(weights_stored, 1)
                sp.dma_start(skewed[:, :, :].rearrange("p j s -> p (j s)"), skew_dram).then_inc(skew_loaded, 16)

            sp.sem_inc(weights_stored, 1)
            sp.wait_ge(core.cleared, 16 * core.clears)
            with sp.Fori(0, B + 1) as j:
                skew_weights(j)

        LOADED = 16 * 18

        @block.gpsimd
        def _(pool):
            for k in range(2):
                nc.gpsimd.memset(norm.xn_t[k][:, :, 0:PAD], 0.0)
                nc.gpsimd.memset(inv_sum[k][:, :, :], 0.0)
                for h in range(HALF):
                    nc.gpsimd.memset(a_sb[k][h][:, 0:PAD], 0.0)
                    nc.gpsimd.memset(c_sb[k][h][:, 0:PAD], 0.0)
            nc.gpsimd.memset(vals[:, :, :, :, :], 0.0)
            nc.gpsimd.memset(sum_a[:, :], 0.0)
            nc.gpsimd.memset(sum_b[:, :], 0.0)
            nc.gpsimd.memset(bond[:, :, :, :], 0.0)
            nc.gpsimd.memset(col_bond[:, :, :], 0.0)
            nc.gpsimd.memset(col_damage[:, :, :], 0.0)
            nc.gpsimd.memset(ones[:, :], 1.0)
            nc.gpsimd.memset(early[:, :], 0.0)
            nc.gpsimd.memset(diag[:, :, :], 1.0)
            nc.gpsimd.iota(inv_count[:, :], pattern=[[1, S]], base=1, channel_multiplier=0,
                           allow_small_or_imprecise_dtypes=True).then_inc(consts, 1)
            pool.wait_ge(consts, 1)
            nc.gpsimd.affine_select(out=early[:, :], in_=early[:, :], compare_op=ALU.is_ge, fill=MASKED,
                                    base=-(WIN - 1), pattern=[[1, WIN]], channel_multiplier=1)
            nc.gpsimd.affine_select(out=diag[:, :, :], in_=diag[:, :, :], compare_op=ALU.is_ge, fill=0.0,
                                    base=0, pattern=[[-BD, HH], [0, BD]], channel_multiplier=1).then_inc(consts, 1)
            pool.wait_ge(consts, 2)
            nc.gpsimd.affine_select(out=diag[:, :, :], in_=diag[:, :, :], compare_op=ALU.is_ge, fill=0.0,
                                    base=BD - 1, pattern=[[BD, HH], [0, BD]], channel_multiplier=-1).then_inc(consts, 1)
            with pool.Fori(0, B // 2) as pair:
                for k in range(2):
                    i = pair * 2 + k
                    pool.wait_ge(pj_copied, (i + 1) * NPJ)
                    for q in range(STEPS):
                        h, dg = divmod(q, NQ)
                        pool.wait_ge(chunk_used, i * 2 * STEPS + 2 * q + 2)
                        d = dg * DG
                        nc.gpsimd.tensor_tensor(dmg_buf[q % 2][:, :, :], window(c_sb[k][h], d),
                                                f_sb[k][h][:, :].unsqueeze(1).broadcast_to([P, DG, S]),
                                                ALU.add).then_inc(dmg_pre, 1)

        @block.tensor
        def _(pe):
            def chunk(i, k, q, kind):
                g, part = divmod(q, GSTEPS)
                buf, bank, col = ((bond_buf, bond_ps, col_bond), (dmg_buf, dmg_ps, col_damage))[kind]
                if part == 0:
                    pe.wait_ge((logits_copied, sig_done)[kind], i * GROUPS + g + 1)
                pe.wait_ge(gelu_done, i * 2 * STEPS + 2 * q + kind + 1)
                for dd in range(DG):
                    d = part * DG + dd
                    last = nc.tensor.matmul(bank[g % 2][:, :], col[:, PG - 1 - d:2 * PG - 1 - d, :].rearrange("p d h -> p (d h)"),
                                            buf[q % 2][:, dd, :], start=d == 0, stop=d == PG - 1)
                last.then_inc(chunk_used, 1)

            def turn_logits(n, g):
                pe.wait_ge(combined, n + 3)
                for j in range(TPB):
                    last = nc.tensor.transpose(bond_ps[g % 2][:, j * P:(j + 1) * P], logits[:, j * P:(j + 1) * P],
                                               core.ident[:, :])
                last.then_inc(logits_turned, 1)

            def product(i, k, n):
                what, h = PJ[n]
                if due(i * NPJ + n):
                    pe.wait_ge(pj_copied, i * NPJ + n)
                mm = lambda w, x, first, end: nc.tensor.matmul(pj[:, :], w, x, start=first, stop=end)
                flat = lambda m: m[:, :, :].rearrange("p h d -> p (h d)")
                if what == "disp":
                    norm.wait_xn_t(pe, i)
                    for c in range(DC):
                        last = mm(w_disp_sb[:, c, h * P:(h + 1) * P], norm.xn_t[k][:, c, PAD:], c == 0, c == DC - 1)
                elif what == "u":
                    last = mm(flat(mats[STATE]), disp[h][:, :], True, True)
                elif what == "a":
                    pe.wait_ge(state_ready, i * HALF + h + 1)
                    mm(flat(mats[STRAIN]), disp[h][:, :], True, False)
                    last = mm(flat(mats[STATE_J]), state[h][:, :], False, True)
                elif what == "q":
                    mm(flat(neg_strain), disp[h][:, :], True, False)
                    last = mm(flat(mats[STATE_I]), state[h][:, :], False, True)
                else:
                    last = mm(flat(mats[DAMAGE]), disp[h][:, :], True, True)
                last.then_inc(pj_ready, 1)

            def values(i, k, n):
                for a in range(4):
                    at = (4 * n + a) * WIN
                    for r in range(2):
                        for c in range(DC):
                            last = nc.tensor.matmul(t_ps[r * SPAN:(r + 1) * SPAN, a * P:(a + 1) * P],
                                                    norm.xn_t[k][:, c, at:at + SPAN], w_val_sb[:, c, :, r, :],
                                                    start=c == 0, stop=c == DC - 1)
                last.then_inc(val_ready, 1)

            def turn(j, x, vals_before):
                if x == 0:
                    pe.wait_ge(skew_loaded, (j + 1) * 16)
                pe.wait_ge(val_copied, 1 + vals_before * 2)
                pe.wait_ge(ctx_ready, 1 + j * TPB + x)
                for hp in range(HP):
                    bank = (t_ps, o_ps)[hp // 4]
                    last = nc.tensor.transpose(bank[:, hp % 4 * P:(hp % 4 + 1) * P],
                                               skewed[:, x, hp * P:(hp + 1) * P], core.ident[:, :])
                last.then_inc(w_turned, 1)

            def sums(j, x):
                pe.wait_ge(w_copied, j * TPB + x + 1)
                for hp in range(HP):
                    for a in range(BPT):
                        last = nc.tensor.matmul(o_ps[a * WIN:(a + 1) * WIN, hp * 2 * BD:(hp + 1) * 2 * BD],
                                                turned[:, hp, a * WIN:(a + 1) * WIN],
                                                vals[:, x * BPT + a, hp, :, :].rearrange("p r d -> p (r d)"),
                                                start=True, stop=True)
                last.then_inc(out_ready, 1)

            def turn_ctx(j, x):
                pe.wait_ge(ctx_ready, j * TPB + x + 2)
                pe.wait_ge(proj_added, 1 + j * TPB + x)
                for c in range(DC):
                    last = nc.tensor.transpose(misc[:, c * P:(c + 1) * P], ctx_sb[:, c * P:(c + 1) * P], core.ident[:, :])
                last.then_inc(ctx_turned, 1)

            def project(j, x):
                pe.wait_ge(ctx_copied, j * TPB + x + 1)
                for c in range(DC):
                    nc.tensor.matmul(misc[:, D:2 * D], ctx_t[:, c, :], w_out_sb[:, c, :], start=c == 0, stop=False)
                nc.tensor.matmul(misc[:, D:2 * D], ones[:, :], b_out_sb[:, :], start=False, stop=True).then_inc(proj_ready, 1)

            def finish_step(j, q, live=1):
                x = tile_at(q, T_STEP)
                if x is not None:
                    turn(j, x, j * 4 + live * x)
                x = tile_at(q, T_STEP + 1)
                if x is not None:
                    sums(j, x)
                x = tile_at(q, T_STEP + 2)
                if x is not None:
                    turn_ctx(j, x)
                x = tile_at(q, T_STEP + 3)
                if x is not None:
                    project(j, x)

            def prepare_step(i, k, q):
                if q == 1:
                    if due(i * NPJ):
                        pe.wait_ge(pj_copied, i * NPJ)
                if q in (1, 2):
                    norm.pe_transpose(i, chunks=(q - 1,))
                if 0 <= q - PJ_STEP < NPJ:
                    product(i, k, q - PJ_STEP)

            for q in range(PJ_STEP):
                prepare_step(0, 0, q)
            pe.wait_ge(tables_a, 1)
            nc.tensor.matmul(pj[0:BD, 0:WIN], w_pos_sb[:, :], rel_t[:, :], start=True, stop=True).then_inc(pj_ready, 1)
            pe.wait_ge(tables_b, 1)
            nc.tensor.matmul(misc[:, 0:SM], select[:, :, :].rearrange("k h d -> k (h d)"), small[:, :],
                             start=True, stop=True).then_inc(proj_ready, 1)
            pe.wait_ge(tables, 1)
            for q in range(PJ_STEP, STEPS):
                prepare_step(0, 0, q)
            with pe.Fori(0, B // 2) as pair:
                for k in range(2):
                    i = pair * 2 + k
                    for q in range(STEPS):
                        chunk(i, k, q, 0)
                        if q % GSTEPS == 2:
                            g = (q // GSTEPS - 1) % GROUPS
                            turn_logits(i * GROUPS + q // GSTEPS - 1, g)
                        finish_step(i, q)
                        n = tile_at(q, T_STEP + 1)
                        if n is not None:
                            values(i, k, n)
                        prepare_step(i + 1, 1 - k, q)
                        chunk(i, k, q, 1)
            turn_logits(B * GROUPS - 1, GROUPS - 1)
            for q in range(STEPS):
                finish_step(B, q, live=0)

        @block.scalar
        def _(act):
            def gelu(i, q, kind):
                act.wait_ge((bond_pre, dmg_pre)[kind], i * STEPS + q + 1)
                buf = (bond_buf, dmg_buf)[kind][q % 2]
                nc.scalar.activation(buf[:, :, :], buf[:, :, :], ACT.Gelu).then_inc(gelu_done, 1)

            def sigmoid(n, g):
                act.wait_ge(chunk_used, 4 + (n + 1) * 2 * GSTEPS)
                act.wait_ge(combined, n + 2)
                nc.scalar.activation(sig[:, :], dmg_ps[g % 2][:, :], ACT.Sigmoid,
                                     bias=damage_b[:, 0:1]).then_inc(sig_done, 1)

            def exps(j):
                act.wait_ge(inv_ready, j + 1)
                act.wait_ge(weights_stored, j + 1)
                act.wait_ge(soft_ready, j + 1)
                nc.scalar.activation(expd[:, :, :, :], bond[:, :, :, :], ACT.Exp).then_inc(exp_done, 1)

            norm.act_std(0)
            with act.Fori(0, B) as i:
                for q in range(STEPS):
                    gelu(i, q, 0)
                    if q == 0:
                        norm.act_std(i + 1)
                    if q % GSTEPS == 1:
                        sigmoid(i * GROUPS + q // GSTEPS - 1, (q // GSTEPS - 1) % GROUPS)
                    if q == 4:
                        exps(i)
                    gelu(i, q, 1)
            sigmoid(B * GROUPS - 1, GROUPS - 1)
            exps(B)

        @block.vector
        def _(dve):
            def combine(n, g):
                dve.wait_ge(sig_done, n + 3)
                nc.vector.scalar_tensor_tensor(out=logits[:, :], in0=sig[:, :], scalar=-10.0,
                                               in1=bond_ps[g % 2][:, :], op0=ALU.mult,
                                               op1=ALU.add).then_inc(combined, 1)

            def copy_logits(n, g):
                h, places = g // 2, slice(g % 2 * PG, (g % 2 + 1) * PG)
                turned_g = bond_ps[g % 2][:, :].rearrange("p (j d h) -> p j h d", j=TPB, d=PG)
                dst = bond[:, :, h * HH:(h + 1) * HH, places]
                dve.wait_ge(logits_turned, n + 2)
                nc.vector.scalar_tensor_tensor(out=dst[:, 0, :, :], in0=turned_g[:, 0, :, :], scalar=bond_b[:, 0:1],
                                               in1=early[:, places].unsqueeze(1).broadcast_to([P, HH, PG]),
                                               op0=ALU.add, op1=ALU.add)
                nc.vector.tensor_scalar(dst[:, 1:, :, :], turned_g[:, 1:, :, :], bond_b[:, 0:1], None,
                                        ALU.add).then_inc(logits_copied, 1)

            def less_top(j):
                rows = bond[:, :, :, :].rearrange("p j h w -> p (j h) w")
                nc.vector.drain()
                nc.vector.tensor_reduce(top[:, :, 0], rows, AX.X, ALU.max)
                nc.vector.drain()
                nc.vector.tensor_tensor(rows, rows, top[:, :, :].broadcast_to([P, TPB * NH, WIN]),
                                        ALU.subtract).then_inc(soft_ready, 1)

            def inverse_sums(j, k):
                nc.vector.drain()
                dve.wait_ge(exp_done, j + 1)
                nc.vector.tensor_reduce(inv_sum[k][:, :, :].rearrange("p j h -> p (j h)"),
                                        expd[:, :, :, :].rearrange("p j h w -> p (j h) w"), AX.X, ALU.add)
                nc.vector.drain()
                nc.vector.reciprocal(inv_sum[k][:, :, :], inv_sum[k][:, :, :]).then_inc(inv_ready, 1)

            def add_projected(j, x):
                dve.wait_ge(proj_ready, 1 + j * TPB + x + 1)
                xt = core.tile(j, x)
                nc.vector.tensor_tensor(xt, misc[:, D:2 * D], xt, ALU.add).then_inc(proj_added, 1)

            def finish_step(j, k, q):
                if q == 2:
                    combine(j * GROUPS - 1, GROUPS - 1)
                if q == 3:
                    copy_logits(j * GROUPS - 1, GROUPS - 1)
                    less_top(j)
                if q == 6:
                    inverse_sums(j, k)
                x = tile_at(q, T_STEP + 1)
                if x is not None:
                    dve.wait_ge(w_turned, j * TPB + x + 2)
                    for half, bank in enumerate((t_ps, o_ps)):
                        last = nc.vector.tensor_copy(turned[:, half * 4:half * 4 + 4, :],
                                                     bank[:, :].rearrange("p (n t) -> p n t", t=P))
                    last.then_inc(w_copied, 1)
                x = tile_at(q, T_STEP + 2)
                if x is not None:
                    dve.wait_ge(out_ready, j * TPB + x + 1)
                    dve.wait_ge(ctx_turned, 1 + j * TPB + x)
                    nc.vector.tensor_tensor(ctx_sb[:, :].rearrange("p (h d) -> p h d", d=BD),
                                            o_ps[:, 0:D].rearrange("p (h d) -> p h d", d=BD),
                                            inv_sum[k][:, x, :].unsqueeze(2).broadcast_to([P, NH, BD]),
                                            ALU.mult).then_inc(ctx_ready, 1)
                x = tile_at(q, T_STEP + 3)
                if x is not None:
                    dve.wait_ge(ctx_turned, j * TPB + x + 2)
                    nc.vector.tensor_copy(ctx_t[:, :, :], misc[:, 0:D].rearrange("p (c q) -> p c q", q=P)).then_inc(ctx_copied, 1)
                x = tile_at(q, T_STEP + 4)
                if x is not None:
                    add_projected(j, x)
                if q == STEPS - 1:
                    add_projected(j, TPB - 1)

            def copy_product(i, k, n):
                what, h = PJ[n]
                bias = lambda m: small_rep[:, COLS + 2 + m:COLS + 3 + m]
                dve.wait_ge(pj_ready, 1 + i * NPJ + n + 1)
                if what == "disp":
                    last = nc.vector.tensor_scalar(disp[h][:, :], pj[:, :], b_disp_sb[:, h:h + 1], None, ALU.add)
                elif what == "u":
                    nc.vector.tensor_copy(sum_a[:, PAD:], pj[:, :])
                    last = nc.vector.tensor_scalar(state[h][:, :], pj[:, :], bias(0), None, ALU.subtract)
                elif what == "a":
                    last = nc.vector.tensor_copy(a_sb[k][h][:, PAD:], pj[:, :])
                elif what == "q":
                    last = nc.vector.tensor_scalar(q_sb[k][h][:, :], pj[:, :], bias(1), None, ALU.add)
                else:
                    nc.vector.tensor_copy(c_sb[k][h][:, PAD:], pj[:, :])
                    last = nc.vector.tensor_scalar(f_sb[k][h][:, :], pj[:, :], -1.0, bias(2), ALU.mult, ALU.add)
                last.then_inc(pj_copied, 1)
                if what == "u":
                    src, dst, step = sum_a, sum_b, 1
                    while step < WIN:
                        nc.vector.drain()
                        nc.vector.tensor_tensor(dst[:, step:], src[:, step:], src[:, 0:PAD + S - step], ALU.add)
                        src, dst, step = dst, src, 2 * step
                    nc.vector.drain()
                    nc.vector.tensor_tensor(dst[:, PAD:], src[:, PAD:], inv_count[:, :], ALU.mult)
                    nc.vector.drain()
                    nc.vector.tensor_tensor(state[h][:, :], dst[:, PAD:], state[h][:, :], ALU.subtract).then_inc(state_ready, 1)
                    nc.vector.drain()

            def prepare_step(i, k, q):
                if q == 0:
                    norm.dve_stats(i)
                if q == 1:
                    norm.dve_normalise(i)
                if q in (2, 3):
                    norm.dve_copy_t(i, k, guard=False, chunks=(q - 2,))
                if 0 <= q - PJ_STEP - 1 < NPJ:
                    copy_product(i, k, q - PJ_STEP - 1)

            def copy_values(i, n):
                dve.wait_ge(val_ready, i * 4 + n + 1)
                for r in range(2):
                    rows = slice(r * SPAN, (r + 1) * SPAN)
                    nc.vector.tensor_tensor(
                        vals[rows, 4 * n:4 * n + 4, :, r, :],
                        t_ps[rows, :].rearrange("p (a h d) -> p a h d", a=4, d=BD),
                        b_val_sb[rows, :, r, :].unsqueeze(1).broadcast_to([SPAN, 4, HP, BD]),
                        ALU.add).then_inc(val_copied, 1)

            def bond_chunk(i, k, q):
                h, dg = divmod(q, NQ)
                dve.wait_ge(chunk_used, i * 2 * STEPS + 2 * q + 1)
                for dd in range(DG):
                    d = dg * DG + dd
                    last = nc.vector.scalar_tensor_tensor(
                        out=bond_buf[q % 2][:, dd, :], in0=a_sb[k][h][:, d + 1:d + 1 + S],
                        scalar=small_rep[:, COLS + 5 + d:COLS + 6 + d], in1=q_sb[k][h][:, :],
                        op0=ALU.add, op1=ALU.add)
                last.then_inc(bond_pre, 1)

            dve.sem_inc(chunk_used, 4)
            for sem_from_1 in (sig_done, combined, logits_copied, inv_ready, w_turned, ctx_ready, ctx_turned,
                               proj_added, val_copied):
                dve.sem_inc(sem_from_1, 1)
            for banks in (bond_ps, dmg_ps):
                for n in range(2):
                    nc.vector.memset(banks[n][:, :], 0.0)
            nc.vector.tensor_copy(select[:, :, :], core.ident[0:BD, 0:BD].unsqueeze(1).broadcast_to([BD, HH, BD]))
            for q in range(PJ_STEP + 1):
                prepare_step(0, 0, q)
            dve.wait_ge(consts, 3)
            nc.vector.tensor_scalar(inv_count[:, :], inv_count[:, :], float(WIN), None, ALU.min)
            nc.vector.drain()
            nc.vector.reciprocal(inv_count[:, :], inv_count[:, :])
            dve.wait_ge(loaded, LOADED)
            dve.wait_ge(rel_loaded, 32)
            nc.vector.drain().then_inc(tables_a, 1)
            dve.wait_ge(pj_ready, 1)
            nc.vector.tensor_copy(small[:, COLS + 5:], pj[0:BD, 0:WIN]).then_inc(tables_b, 1)
            dve.wait_ge(proj_ready, 1)
            nc.vector.tensor_copy(small_rep[:, :], misc[:, 0:SM])
            nc.vector.drain()
            for n in range(5):
                nc.vector.tensor_tensor(mats[n][:, :, :], diag[:, :, :],
                                        small_rep[:, n * BD:(n + 1) * BD].unsqueeze(1).broadcast_to([P, HH, BD]), ALU.mult)
            nc.vector.tensor_scalar(col_bond[:, PG - 1, :], diag[:, :, 0], small_rep[:, COLS:COLS + 1], None, ALU.mult)
            nc.vector.tensor_scalar(col_damage[:, PG - 1, :], diag[:, :, 0], small_rep[:, COLS + 1:COLS + 2], None, ALU.mult)
            nc.vector.drain()
            nc.vector.tensor_scalar(neg_strain[:, :, :], mats[STRAIN][:, :, :], -1.0, None, ALU.mult).then_inc(tables, 1)
            for q in range(PJ_STEP + 1, STEPS):
                prepare_step(0, 0, q)
            with dve.Fori(0, B // 2) as pair:
                for k in range(2):
                    i = pair * 2 + k
                    for q in range(STEPS):
                        if q == 0:
                            nc.vector.drain()
                        bond_chunk(i, k, q)
                        g = q // GSTEPS - 1
                        if g >= 0 and q % GSTEPS == 2:
                            combine(i * GROUPS + g, g)
                        if g >= 0 and q % GSTEPS == 3:
                            copy_logits(i * GROUPS + g, g)
                        prepare_step(i + 1, 1 - k, q)
                        n = tile_at(q, T_STEP + 2)
                        if n is not None:
                            copy_values(i, n)
                        finish_step(i, 1 - k, q)
            for q in range(STEPS):
                finish_step(B, 1, q)


def macaron(nc, t, out, phases="f0 a0 f0 f1 a1 f1"):
    with ExitStack() as ctx:
        core = Core(nc, ctx)
        sparse = Sparse(core, ctx, t["L0_ffn_w1"].shape[0])
        skew = nc.dram_tensor("skew", (P, TPB * (D // 16) * 2 * WIN), FP32, kind="Internal").ap()
        parts = nc.dram_tensor("parts", (2, 3, D, S), BF16, kind="Internal").ap()
        load_phase(core, t["L0_attn_x"], (sparse.rows_in, skew.rearrange("p (r d) -> (p r) d", d=D)))
        for n, ph in enumerate(phases.split()):
            core.free_semaphores()
            if ph == "f0":
                ffn0_phase(core, sparse, f"f0_{n}", *[t["L0_ffn_" + s] for s in
                           ("gate_w", "gate_b", "w1", "b1", "w2", "b2")])
            if ph == "f1":
                ffn1_phase(core, f"f1_{n}", *[t["L1_ffn_" + s] for s in
                           ("gate_W", "W1", "b1", "W2", "b2", "Ws1", "bs1", "Ws2", "bs2", "route_scale")])
            if ph == "a0":
                attn0_phase(core, f"a0_{n}", skew, *[t["L0_attn_" + s] for s in
                            ("w_disp", "b_disp", "w_val", "b_val", "rel_pos_emb", "w_state", "b_state", "w_strain",
                             "b_strain", "w_state_i", "w_state_j", "w_pos", "w_bond_out", "b_bond_out", "w_damage",
                             "b_damage", "w_damage_out", "b_damage_out", "w_cproj", "b_cproj")])
            if ph == "a1":
                attn1_phase(core, f"a1_{n}", parts, *[t["L1_attn_" + s] for s in
                            ("Wq", "Wk", "Wv", "Wo", "bo", "rel_emb")])
        core.free_semaphores()
        store_phase(core, out)
        core.free_semaphores()


_L0_ATTN = ("x", "w_disp", "b_disp", "w_val", "b_val", "rel_pos_emb", "w_state", "b_state", "w_strain", "b_strain",
            "w_state_i", "w_state_j", "w_pos", "w_bond_out", "b_bond_out", "w_damage", "b_damage", "w_damage_out",
            "b_damage_out", "w_cproj", "b_cproj")
_L0_FFN = ("gate_w", "gate_b", "w1", "b1", "w2", "b2")
_L1_ATTN = ("Wq", "Wk", "Wv", "Wo", "bo", "rel_emb")
_L1_FFN = ("gate_W", "W1", "b1", "W2", "b2", "Ws1", "bs1", "Ws2", "bs2", "route_scale")
_INS = [part + n for part, names in (("L0_attn_", _L0_ATTN), ("L0_ffn_", _L0_FFN), ("L1_attn_", _L1_ATTN),
                                     ("L1_ffn_", _L1_FFN)) for n in names]


def kernel(**inputs):
    import numpy as _np
    import concourse.bacc as _bacc
    from concourse import mybir as _mybir
    from concourse.bass_utils import run_bass_kernel_spmd as _run

    nc = _bacc.Bacc("TRN2", target_bir_lowering=False, num_devices=1)
    arrays, tensors = {}, {}
    for name in _INS:
        a = _np.ascontiguousarray(inputs[name])
        a = a.reshape(a.shape or (1,))
        arrays[f"in_{name}_dram"] = a
        tensors[name] = nc.dram_tensor(f"in_{name}_dram", a.shape, _mybir.dt.from_np(a.dtype),
                                       kind="ExternalInput").ap()
    x = inputs["L0_attn_x"]
    out = nc.dram_tensor("out_0_dram", tuple(x.shape), _mybir.dt.float32, kind="ExternalOutput").ap()
    macaron(nc, tensors, out)
    r = _run(nc, [arrays], core_ids=[0])
    return r.results[0]["out_0_dram"]
```
